# Optimizing a Trainium2 kernel written in Bass

```python
import numpy as np
import jax
import jax.numpy as jnp

def _softmax(x, axis=-1):
    return jax.nn.softmax(x, axis=axis)

def _gelu(x):
    return jax.nn.gelu(x, approximate=True)

def _silu(x):
    return jax.nn.silu(x)

def _sigmoid(x):
    return jax.nn.sigmoid(x)

def _layernorm(x, axis=-1, eps=1e-05):
    m = jnp.mean(x, axis=axis, keepdims=True)
    v = jnp.var(x, axis=axis, keepdims=True)
    return (x - m) / jnp.sqrt(v + eps)

def _scatter_add(tgt, idx, src, axis=0):
    return tgt.at[idx].add(src)

def _segment_sum(src, seg, n):
    return jax.ops.segment_sum(src, seg, n)
kernel_name = 'mk_seq_preln_d2_jaxref_r8_33eab3'

def setup_inputs(seed: int=0):
    np.random.seed(seed)
    _w = jnp.asarray

    def _L0_attn_setup():
        import jax, jax.numpy as jnp
        import numpy as np
        D_MODEL = 256
        N_HEADS = 16
        D_HEAD = D_MODEL // N_HEADS
        B, S = (2, 256)
        EPS = 1e-05

        def _mhsa(X, ln_g, ln_b, Wq, bq, Wk, bk, Wv, bv, Wo, bo):
            n_ctx = X.shape[-2]
            mu = jnp.mean(X, axis=-1, keepdims=True)
            var = jnp.mean(jnp.square(X - mu), axis=-1, keepdims=True)
            Xn = (X - mu) * jax.lax.rsqrt(var + EPS) * ln_g + ln_b

            def split_heads(t):
                return t.reshape(t.shape[:-1] + (N_HEADS, D_HEAD)).swapaxes(-2, -3)
            Q = split_heads(Xn @ Wq + bq)
            K = split_heads(Xn @ Wk + bk)
            V = split_heads(Xn @ Wv + bv)
            scores = jnp.einsum('bhqd,bhkd->bhqk', Q, K) / jnp.sqrt(jnp.float32(D_HEAD))
            causal = jnp.tril(jnp.ones((n_ctx, n_ctx), dtype=bool))
            scores = jnp.where(causal, scores, jnp.float32(-jnp.inf))
            A = jax.nn.softmax(scores, axis=-1)
            AV = jnp.einsum('bhqk,bhkd->bhqd', A, V)
            AV = AV.swapaxes(-2, -3).reshape(X.shape[:-1] + (D_MODEL,))
            return AV @ Wo + bo
        key = jax.random.key(seed)
        ks = jax.random.split(key, 10)
        sd = 1.0 / np.sqrt(D_MODEL)
        inp = {'X': jax.random.normal(ks[0], (B, S, D_MODEL), dtype=jnp.float32), 'ln_g': jnp.ones((D_MODEL,), jnp.float32), 'ln_b': jnp.zeros((D_MODEL,), jnp.float32), 'Wq': jax.random.uniform(ks[1], (D_MODEL, D_MODEL), jnp.float32, -sd, sd), 'bq': jax.random.uniform(ks[2], (D_MODEL,), jnp.float32, -sd, sd), 'Wk': jax.random.uniform(ks[3], (D_MODEL, D_MODEL), jnp.float32, -sd, sd), 'bk': jax.random.uniform(ks[4], (D_MODEL,), jnp.float32, -sd, sd), 'Wv': jax.random.uniform(ks[5], (D_MODEL, D_MODEL), jnp.float32, -sd, sd), 'bv': jax.random.uniform(ks[6], (D_MODEL,), jnp.float32, -sd, sd), 'Wo': jax.random.uniform(ks[7], (D_MODEL, D_MODEL), jnp.float32, -sd, sd), 'bo': jax.random.uniform(ks[8], (D_MODEL,), jnp.float32, -sd, sd)}
        return inp
    _L0_attn_in = _L0_attn_setup()

    def _L0_ffn_setup():
        import jax, jax.numpy as jnp
        import numpy as np
        BLOCK_SIZE = 32
        HIDDEN_SIZE = 256
        MLP_DIM = 2048
        NVFP4_LUT = jnp.array([0.0, 0.5, 1.0, 1.5, 2.0, 3.0, 4.0, 6.0, 0.0, -0.5, -1.0, -1.5, -2.0, -3.0, -4.0, -6.0], dtype=jnp.float32)

        def dequant_nvfp4(W_packed, scales, block=BLOCK_SIZE):
            N = W_packed.shape[0]
            low = W_packed & 15
            high = W_packed >> 4 & 15
            idx = jnp.stack([low, high], axis=-1).reshape(N, -1)
            vals = NVFP4_LUT[idx]
            K = vals.shape[1]
            vals = vals.reshape(N, K // block, block) * scales[:, :, None]
            return vals.reshape(N, K)
        key = jax.random.key(seed)
        ks = jax.random.split(key, 7)
        x = jax.random.normal(ks[0], (4, 32, HIDDEN_SIZE), dtype=jnp.float32)
        gate_W_packed = jax.random.randint(ks[1], (MLP_DIM, HIDDEN_SIZE // 2), 0, 32, dtype=jnp.int32)
        gate_scales = jax.random.uniform(ks[2], (MLP_DIM, HIDDEN_SIZE // BLOCK_SIZE), dtype=jnp.float32) * 0.1 + 0.001
        up_W_packed = jax.random.randint(ks[3], (MLP_DIM, HIDDEN_SIZE // 2), 0, 32, dtype=jnp.int32)
        up_scales = jax.random.uniform(ks[4], (MLP_DIM, HIDDEN_SIZE // BLOCK_SIZE), dtype=jnp.float32) * 0.1 + 0.001
        down_W_packed = jax.random.randint(ks[5], (HIDDEN_SIZE, MLP_DIM // 2), 0, 32, dtype=jnp.int32)
        down_scales = jax.random.uniform(ks[6], (HIDDEN_SIZE, MLP_DIM // BLOCK_SIZE), dtype=jnp.float32) * 0.1 + 0.001
        return {'x': x, 'gate_W_packed': gate_W_packed, 'gate_scales': gate_scales, 'up_W_packed': up_W_packed, 'up_scales': up_scales, 'down_W_packed': down_W_packed, 'down_scales': down_scales}
    _L0_ffn_in = _L0_ffn_setup()

    def _L1_attn_setup():
        import jax, jax.numpy as jnp
        import numpy as np
        IN_FEATURES = 256
        HEAD_NUM = 64
        D = IN_FEATURES // HEAD_NUM
        SCALE = float(np.sqrt(D))
        key = jax.random.key(seed)
        ks = jax.random.split(key, 9)
        F = IN_FEATURES
        x = jax.random.normal(ks[0], (4, 128, F), dtype=jnp.float32)
        w = lambda k: jax.random.normal(k, (F, F), dtype=jnp.float32) * 0.02
        b = lambda k: jax.random.normal(k, (F,), dtype=jnp.float32) * 0.01
        return {'x': x, 'Wq': w(ks[1]), 'bq': b(ks[2]), 'Wk': w(ks[3]), 'bk': b(ks[4]), 'Wv': w(ks[5]), 'bv': b(ks[6]), 'Wo': w(ks[7]), 'bo': b(ks[8])}
    _L1_attn_in = _L1_attn_setup()

    def _L1_ffn_setup():
        import jax, jax.numpy as jnp
        import numpy as np
        HIDDEN = 256
        FFN = 176
        N_EXPERTS = 64
        TOP_K = 6
        N_SHARED = 2
        SHARED_FFN = FFN * N_SHARED
        ROUTED_SCALING = 1.0
        EPS = 1e-20

        def _moe_forward(x, gate_w, w_gate_up, w_down, ws_gate_up, ws_down):
            T = x.shape[0]
            logits = jnp.einsum('th,eh->te', x.astype(jnp.float32), gate_w.astype(jnp.float32))
            scores = jax.nn.softmax(logits, axis=-1)
            topk_w, topk_ids = jax.lax.top_k(scores, TOP_K)
            topk_w = topk_w / (jnp.sum(topk_w, axis=-1, keepdims=True) + EPS)
            topk_w = topk_w * ROUTED_SCALING
            comb = jnp.zeros((T, N_EXPERTS), dtype=x.dtype)
            comb = comb.at[jnp.arange(T)[:, None], topk_ids].add(topk_w.astype(x.dtype))
            gu = jnp.einsum('th,efh->tef', x, w_gate_up)
            g, u = (gu[..., :FFN], gu[..., FFN:])
            act = jax.nn.silu(g) * u
            act = act * comb[:, :, None]
            routed = jnp.einsum('tef,ehf->th', act, w_down)
            sgu = jnp.einsum('th,fh->tf', x, ws_gate_up)
            sg, su = (sgu[..., :SHARED_FFN], sgu[..., SHARED_FFN:])
            shared = jnp.einsum('tf,hf->th', jax.nn.silu(sg) * su, ws_down)
            return routed + shared
        key = jax.random.key(seed)
        k0, k1, k2, k3, k4, k5 = jax.random.split(key, 6)
        hidden_states = jax.random.normal(k0, (1, 32, HIDDEN), dtype=jnp.float32)
        gate_w = jax.random.normal(k1, (N_EXPERTS, HIDDEN), dtype=jnp.float32) * 0.05
        w_gate_up = jax.random.normal(k2, (N_EXPERTS, 2 * FFN, HIDDEN), dtype=jnp.float32) * 0.02
        w_down = jax.random.normal(k3, (N_EXPERTS, HIDDEN, FFN), dtype=jnp.float32) * 0.02
        ws_gate_up = jax.random.normal(k4, (2 * SHARED_FFN, HIDDEN), dtype=jnp.float32) * 0.02
        ws_down = jax.random.normal(k5, (HIDDEN, SHARED_FFN), dtype=jnp.float32) * 0.02
        return {'hidden_states': hidden_states, 'gate_w': gate_w, 'w_gate_up': w_gate_up, 'w_down': w_down, 'ws_gate_up': ws_gate_up, 'ws_down': ws_down}
    _L1_ffn_in = _L1_ffn_setup()
    _d = {'L0_attn_X': _L0_attn_in['X'], 'L0_attn_ln_g': _L0_attn_in['ln_g'], 'L0_attn_ln_b': _L0_attn_in['ln_b'], 'L0_attn_Wq': _L0_attn_in['Wq'], 'L0_attn_bq': _L0_attn_in['bq'], 'L0_attn_Wk': _L0_attn_in['Wk'], 'L0_attn_bk': _L0_attn_in['bk'], 'L0_attn_Wv': _L0_attn_in['Wv'], 'L0_attn_bv': _L0_attn_in['bv'], 'L0_attn_Wo': _L0_attn_in['Wo'], 'L0_attn_bo': _L0_attn_in['bo'], 'L0_ffn_gate_W_packed': _L0_ffn_in['gate_W_packed'], 'L0_ffn_gate_scales': _L0_ffn_in['gate_scales'], 'L0_ffn_up_W_packed': _L0_ffn_in['up_W_packed'], 'L0_ffn_up_scales': _L0_ffn_in['up_scales'], 'L0_ffn_down_W_packed': _L0_ffn_in['down_W_packed'], 'L0_ffn_down_scales': _L0_ffn_in['down_scales'], 'L1_attn_Wq': _L1_attn_in['Wq'], 'L1_attn_bq': _L1_attn_in['bq'], 'L1_attn_Wk': _L1_attn_in['Wk'], 'L1_attn_bk': _L1_attn_in['bk'], 'L1_attn_Wv': _L1_attn_in['Wv'], 'L1_attn_bv': _L1_attn_in['bv'], 'L1_attn_Wo': _L1_attn_in['Wo'], 'L1_attn_bo': _L1_attn_in['bo'], 'L1_ffn_gate_w': _L1_ffn_in['gate_w'], 'L1_ffn_w_gate_up': _L1_ffn_in['w_gate_up'], 'L1_ffn_w_down': _L1_ffn_in['w_down'], 'L1_ffn_ws_gate_up': _L1_ffn_in['ws_gate_up'], 'L1_ffn_ws_down': _L1_ffn_in['ws_down']}
    _x0 = _d['L0_attn_X']
    _d['L0_attn_X'] = jax.random.normal(jax.random.fold_in(jax.random.key(seed), 1), (4, 512, 256), dtype=_x0.dtype)
    del _x0
    return _d

def reference(L0_attn_X, L0_attn_ln_g, L0_attn_ln_b, L0_attn_Wq, L0_attn_bq, L0_attn_Wk, L0_attn_bk, L0_attn_Wv, L0_attn_bv, L0_attn_Wo, L0_attn_bo, L0_ffn_gate_W_packed, L0_ffn_gate_scales, L0_ffn_up_W_packed, L0_ffn_up_scales, L0_ffn_down_W_packed, L0_ffn_down_scales, L1_attn_Wq, L1_attn_bq, L1_attn_Wk, L1_attn_bk, L1_attn_Wv, L1_attn_bv, L1_attn_Wo, L1_attn_bo, L1_ffn_gate_w, L1_ffn_w_gate_up, L1_ffn_w_down, L1_ffn_ws_gate_up, L1_ffn_ws_down):

    def _L0_attn_ref(X, ln_g, ln_b, Wq, bq, Wk, bk, Wv, bv, Wo, bo):
        import jax, jax.numpy as jnp
        import numpy as np
        D_MODEL = 256
        N_HEADS = 16
        D_HEAD = D_MODEL // N_HEADS
        B, S = (2, 256)
        EPS = 1e-05

        def _mhsa(X, ln_g, ln_b, Wq, bq, Wk, bk, Wv, bv, Wo, bo):
            n_ctx = X.shape[-2]
            mu = jnp.mean(X, axis=-1, keepdims=True)
            var = jnp.mean(jnp.square(X - mu), axis=-1, keepdims=True)
            Xn = (X - mu) * jax.lax.rsqrt(var + EPS) * ln_g + ln_b

            def split_heads(t):
                return t.reshape(t.shape[:-1] + (N_HEADS, D_HEAD)).swapaxes(-2, -3)
            Q = split_heads(Xn @ Wq + bq)
            K = split_heads(Xn @ Wk + bk)
            V = split_heads(Xn @ Wv + bv)
            scores = jnp.einsum('bhqd,bhkd->bhqk', Q, K) / jnp.sqrt(jnp.float32(D_HEAD))
            causal = jnp.tril(jnp.ones((n_ctx, n_ctx), dtype=bool))
            scores = jnp.where(causal, scores, jnp.float32(-jnp.inf))
            A = jax.nn.softmax(scores, axis=-1)
            AV = jnp.einsum('bhqk,bhkd->bhqd', A, V)
            AV = AV.swapaxes(-2, -3).reshape(X.shape[:-1] + (D_MODEL,))
            return AV @ Wo + bo
        return _mhsa(X, ln_g, ln_b, Wq, bq, Wk, bk, Wv, bv, Wo, bo)

    def _L0_ffn_ref(x, gate_W_packed, gate_scales, up_W_packed, up_scales, down_W_packed, down_scales):
        import jax, jax.numpy as jnp
        import numpy as np
        BLOCK_SIZE = 32
        HIDDEN_SIZE = 256
        MLP_DIM = 2048
        NVFP4_LUT = jnp.array([0.0, 0.5, 1.0, 1.5, 2.0, 3.0, 4.0, 6.0, 0.0, -0.5, -1.0, -1.5, -2.0, -3.0, -4.0, -6.0], dtype=jnp.float32)

        def dequant_nvfp4(W_packed, scales, block=BLOCK_SIZE):
            N = W_packed.shape[0]
            low = W_packed & 15
            high = W_packed >> 4 & 15
            idx = jnp.stack([low, high], axis=-1).reshape(N, -1)
            vals = NVFP4_LUT[idx]
            K = vals.shape[1]
            vals = vals.reshape(N, K // block, block) * scales[:, :, None]
            return vals.reshape(N, K)
        B, S, H = x.shape
        xt = x.reshape(B * S, H)
        Wg = dequant_nvfp4(gate_W_packed, gate_scales)
        Wu = dequant_nvfp4(up_W_packed, up_scales)
        Wd = dequant_nvfp4(down_W_packed, down_scales)
        gate = jnp.einsum('th,nh->tn', xt, Wg)
        up = jnp.einsum('th,nh->tn', xt, Wu)
        gelu = jnp.tanh(0.7978845608028654 * (gate + 0.044715 * gate ** 3)) * gate * 0.5 + gate * 0.5
        inter = gelu * up
        out = jnp.einsum('tn,hn->th', inter, Wd)
        return out.reshape(B, S, H)

    def _L1_attn_ref(x, Wq, bq, Wk, bk, Wv, bv, Wo, bo):
        import jax, jax.numpy as jnp
        import numpy as np
        IN_FEATURES = 256
        HEAD_NUM = 64
        D = IN_FEATURES // HEAD_NUM
        SCALE = float(np.sqrt(D))
        B, S, F = x.shape
        d = D
        h = F // d
        q = x @ Wq + bq
        k = x @ Wk + bk
        v = x @ Wv + bv

        def to_heads(t):
            return t.reshape(B, S, d, h).transpose(0, 2, 1, 3)
        q, k, v = (to_heads(q), to_heads(k), to_heads(v))
        scores = jnp.einsum('bdsh,bdth->bdst', q, k) / SCALE
        weights = jax.nn.softmax(scores, axis=-1)
        feats = jnp.einsum('bdst,bdth->bdsh', weights, v)
        feats = feats.transpose(0, 2, 1, 3).reshape(B, S, F)
        return feats @ Wo + bo

    def _L1_ffn_ref(hidden_states, gate_w, w_gate_up, w_down, ws_gate_up, ws_down):
        import jax, jax.numpy as jnp
        import numpy as np
        HIDDEN = 256
        FFN = 176
        N_EXPERTS = 64
        TOP_K = 6
        N_SHARED = 2
        SHARED_FFN = FFN * N_SHARED
        ROUTED_SCALING = 1.0
        EPS = 1e-20

        def _moe_forward(x, gate_w, w_gate_up, w_down, ws_gate_up, ws_down):
            T = x.shape[0]
            logits = jnp.einsum('th,eh->te', x.astype(jnp.float32), gate_w.astype(jnp.float32))
            scores = jax.nn.softmax(logits, axis=-1)
            topk_w, topk_ids = jax.lax.top_k(scores, TOP_K)
            topk_w = topk_w / (jnp.sum(topk_w, axis=-1, keepdims=True) + EPS)
            topk_w = topk_w * ROUTED_SCALING
            comb = jnp.zeros((T, N_EXPERTS), dtype=x.dtype)
            comb = comb.at[jnp.arange(T)[:, None], topk_ids].add(topk_w.astype(x.dtype))
            gu = jnp.einsum('th,efh->tef', x, w_gate_up)
            g, u = (gu[..., :FFN], gu[..., FFN:])
            act = jax.nn.silu(g) * u
            act = act * comb[:, :, None]
            routed = jnp.einsum('tef,ehf->th', act, w_down)
            sgu = jnp.einsum('th,fh->tf', x, ws_gate_up)
            sg, su = (sgu[..., :SHARED_FFN], sgu[..., SHARED_FFN:])
            shared = jnp.einsum('tf,hf->th', jax.nn.silu(sg) * su, ws_down)
            return routed + shared
        B, S, H = hidden_states.shape
        x = hidden_states.reshape(-1, H)
        out = _moe_forward(x, gate_w, w_gate_up, w_down, ws_gate_up, ws_down)
        return out.reshape(B, S, H)
    x = L0_attn_X
    x = x + _L0_attn_ref(_layernorm(x, axis=-1), L0_attn_ln_g, L0_attn_ln_b, L0_attn_Wq, L0_attn_bq, L0_attn_Wk, L0_attn_bk, L0_attn_Wv, L0_attn_bv, L0_attn_Wo, L0_attn_bo)
    x = x + _L0_ffn_ref(_layernorm(x, axis=-1), L0_ffn_gate_W_packed, L0_ffn_gate_scales, L0_ffn_up_W_packed, L0_ffn_up_scales, L0_ffn_down_W_packed, L0_ffn_down_scales)
    x = x + _L1_attn_ref(_layernorm(x, axis=-1), L1_attn_Wq, L1_attn_bq, L1_attn_Wk, L1_attn_bk, L1_attn_Wv, L1_attn_bv, L1_attn_Wo, L1_attn_bo)
    x = x + _L1_ffn_ref(_layernorm(x, axis=-1), L1_ffn_gate_w, L1_ffn_w_gate_up, L1_ffn_w_down, L1_ffn_ws_gate_up, L1_ffn_ws_down)
    return x

_drawn_inputs = setup_inputs


def setup_inputs(seed=0):
    import zlib

    import numpy as np

    out = dict(_drawn_inputs(seed))
    spreads = {'L0_attn_ln_g': (1.0, 0.6), 'L0_attn_ln_b': (0.0, 0.1)}
    factors = {'L0_attn_bq': 8.0,
     'L0_attn_bk': 64.0,
     'L1_attn_Wq': 8.0,
     'L1_attn_bq': 8.0,
     'L1_attn_Wk': 8.0,
     'L1_attn_bk': 64.0,
     'L1_attn_Wv': 8.0,
     'L1_attn_bv': 22.056,
     'L1_attn_Wo': 8.0,
     'L1_attn_bo': 61.878,
     'L1_ffn_gate_w': 8.0,
     'L1_ffn_w_gate_up': 8.0,
     'L1_ffn_w_down': 8.0,
     'L1_ffn_ws_gate_up': 8.0,
     'L1_ffn_ws_down': 8.0}
    for name, (base, spread) in spreads.items():
        noise = np.random.default_rng([zlib.crc32(name.encode()), seed]).standard_normal(out[name].shape)
        drawn = base * np.exp(spread * noise) if base else spread * noise
        out[name] = jnp.asarray(drawn.astype(out[name].dtype))
    for name, factor in factors.items():
        out[name] = (out[name] * factor).astype(out[name].dtype)
    return out
```

```python
from contextlib import ExitStack

import numpy as np

import concourse.bass as bass
from concourse import mybir

F32 = mybir.dt.float32
F32R = mybir.dt.float32r
BF16 = mybir.dt.bfloat16
I32 = mybir.dt.int32
U32 = mybir.dt.uint32
ALU = mybir.AluOpType
ACT = mybir.ActivationFunctionType
AX_X = mybir.AxisListType.X

P = 128
D = 256
T = 2048
S = 512
B = T // S
CT = 4
CHUNK = CT * P
NCH = T // CHUNK
KD = D // P
NTT = T // P
LN_EPS = 1e-5
NEG = -1e30


class Scope:

    def __init__(self, nc, ctx, tag):
        self.nc, self.ctx, self.tag = nc, ctx, tag

    def sbuf(self, name, shape, dt=F32):
        return self.ctx.enter_context(self.nc.sbuf_tensor(f"{self.tag}_{name}", shape, dt))

    def psum(self, name, shape, dt=F32):
        return self.ctx.enter_context(self.nc.psum_tensor(f"{self.tag}_{name}", shape, dt))

    def sem(self, name):
        return self.ctx.enter_context(self.nc.semaphore(f"{self.tag}_{name}"))


def make_constants(nc, x_dram, x_sb, ident, ident_bf, mask_q, mask_k):
    with ExitStack() as ctx:
        s = Scope(nc, ctx, "const")
        x_loaded, filled, shaped = s.sem("x_loaded"), s.sem("filled"), s.sem("shaped")
        block = ctx.enter_context(nc.Block())

        @block.sync
        def _(sp):
            for c in range(NCH):
                sp.dma_start(x_sb[:, c * CT:(c + 1) * CT, :],
                             x_dram[c].rearrange("(i p) d -> p i d", p=P)).then_inc(x_loaded, 16)
            sp.wait_ge(x_loaded, 16 * NCH)

        @block.gpsimd
        def _(pool):
            for t in (ident, ident_bf, mask_q, mask_k):
                pool.memset(t[:, :], 0.0).then_inc(filled, 1)
            pool.wait_ge(filled, 4)
            for t in (ident, ident_bf):
                pool.affine_select(out=t[:, :], in_=t[:, :], compare_op=ALU.not_equal, fill=1.0, base=0,
                                   pattern=[[-1, P]], channel_multiplier=1).then_inc(shaped, 1)
            pool.affine_select(out=mask_q[:, :], in_=mask_q[:, :], compare_op=ALU.is_ge, fill=NEG, base=0,
                               pattern=[[-1, P]], channel_multiplier=1).then_inc(shaped, 1)
            pool.affine_select(out=mask_k[:, :], in_=mask_k[:, :], compare_op=ALU.is_ge, fill=NEG, base=0,
                               pattern=[[1, P]], channel_multiplier=-1).then_inc(shaped, 1)
            pool.wait_ge(shaped, 4)


class NormStats:

    def __init__(self, s, tag=""):
        self.stats = s.sbuf(f"stats{tag}", [P, NTT, 6])
        self.mv = s.sbuf(f"mv{tag}", [P, NTT, 2])
        self.var = s.sbuf(f"var{tag}", [P, NTT])
        self.inv = s.sbuf(f"inv{tag}", [P, NTT])
        self.root = s.sbuf(f"root{tag}", [P, NTT])
        self.tmp = s.sbuf(f"tmp{tag}", [P, NTT])
        self.rstd = s.sbuf(f"rstd{tag}", [P, NTT])
        self.inv_done = s.sem(f"inv_done{tag}")
        self.root_done = s.sem(f"root_done{tag}")

    def on_vector(self, dve, src):
        for i in range(NTT):
            dve.bn_stats(self.stats[:, i, :], src[:, i, :])
        dve.drain()
        for i in range(NTT):
            dve.bn_aggr(self.mv[:, i, :], self.stats[:, i, :])
        dve.drain()
        dve.tensor_scalar(self.var[:, :], self.mv[:, :, 1], LN_EPS, None, ALU.add)
        dve.drain()
        dve.reciprocal(self.inv[:, :], self.var[:, :]).then_inc(self.inv_done, 1)
        dve.wait_ge(self.root_done, 1)
        dve.tensor_tensor(self.tmp[:, :], self.root[:, :], self.root[:, :], ALU.mult)
        dve.drain()
        dve.tensor_tensor(self.inv[:, :], self.tmp[:, :], self.var[:, :], ALU.mult)
        dve.drain()
        dve.tensor_scalar(self.tmp[:, :], self.inv[:, :], -0.5, 1.5, ALU.mult, ALU.add)
        dve.drain()
        dve.tensor_tensor(self.rstd[:, :], self.tmp[:, :], self.root[:, :], ALU.mult)
        dve.drain()

    def on_scalar(self, act):
        act.wait_ge(self.inv_done, 1)
        act.activation(self.root[:, :], self.inv[:, :], ACT.Sqrt).then_inc(self.root_done, 1)


def project_qkv(nc, tag, x_sb, ident, w, affine, q_dram, k_dram, v_dram, heads, pitch):
    hd = D // heads
    with ExitStack() as ctx:
        s = Scope(nc, ctx, tag)
        ns = NormStats(s)
        ns2 = NormStats(s, "2") if affine else None
        wt = [s.sbuf(f"w{n}", [P, KD, D]) for n in "qkv"]
        bqk = s.sbuf("bqk", [P, 2, KD])
        bv = s.sbuf("bv", [P, D])
        xo = s.sbuf("xo", [P, NTT, D]) if affine else x_sb
        xn = s.sbuf("xn", [P, CT, D])
        x1 = s.sbuf("x1", [P, CT, D]) if affine else None
        x2 = s.sbuf("x2", [P, CT, D]) if affine else None
        gb = s.sbuf("gb", [P, 2, D]) if affine else None
        xt = s.sbuf("xt", [P, KD, CHUNK])
        hi = s.sbuf("hi", [P, 2, KD, CHUNK], F32R)
        lo = s.sbuf("lo", [P, 2, KD, CHUNK], F32R)
        vs = s.sbuf("vs", [P, CT, heads * pitch])
        v4 = vs[:, :, :].rearrange("p i (h c) -> p i h c", c=pitch)
        ps_t = s.psum("ps_t", [P, KD, CHUNK])
        ps_qk = s.psum("ps_qk", [P, 2, CHUNK])
        ps_v = s.psum("ps_v", [P, 2, 512])

        weights_loaded = s.sem("weights_loaded")
        v_columns_set = s.sem("v_columns_set")
        normed = s.sem("normed")
        transposed = s.sem("transposed")
        xt_ready = s.sem("xt_ready")
        qk_done = s.sem("qk_done")
        hi_done = s.sem("hi_done")
        lo_done = s.sem("lo_done")
        v_done = s.sem("v_done")
        v_written = s.sem("v_written")
        qk_stored = s.sem("qk_stored")
        v_stored = s.sem("v_stored")
        block = ctx.enter_context(nc.Block())
        NQ = 2 * KD
        NW = 8 if affine else 6

        @block.sync
        def _(sp):
            for t, a in zip(wt, (w["Wq"], w["Wk"], w["Wv"])):
                sp.dma_start(t[:, :, :], a.rearrange("(k p) n -> p k n", p=P)).then_inc(weights_loaded, 16)
            sp.dma_start(bqk[:, 0, :], w["bq"]).then_inc(weights_loaded, 16)
            sp.dma_start(bqk[:, 1, :], w["bk"]).then_inc(weights_loaded, 16)
            sp.dma_start(bv[:, :], w["bv"].partition_broadcast(P)).then_inc(weights_loaded, 16)
            if affine:
                for j in range(2):
                    sp.dma_start(gb[:, j, :], affine[j].partition_broadcast(P)).then_inc(weights_loaded, 16)
            with sp.Fori(0, NCH) as c:
                sp.wait_ge(lo_done, c * NQ + NQ)
                for j, dst in enumerate((q_dram, k_dram)):
                    for part, t in enumerate((hi, lo)):
                        sp.dma_start(dst[part].rearrange("(k p) t -> p k t", p=P)[:, :, bass.ds(c * CHUNK, CHUNK)],
                                     t[:, j, :, :].bitcast(F32)).then_inc(qk_stored, 16)
                sp.wait_ge(v_written, c * CT + CT)
                sp.dma_start(v_dram.rearrange("(i p) f -> p i f", p=P)[:, bass.ds(c * CT, CT), :],
                             vs[:, :, :]).then_inc(v_stored, 16)
            sp.wait_ge(qk_stored, 16 * 4 * NCH)
            sp.wait_ge(v_stored, 16 * NCH)

        @block.gpsimd
        def _(pool):
            pool.memset(vs[:, :, :], 0.0).then_inc(v_columns_set, 1)
            pool.wait_ge(v_columns_set, 1)
            for i in range(CT):
                pool.memset(v4[:, i, :, hd:hd + 1], 1.0).then_inc(v_columns_set, 1)

        @block.vector
        def _(dve):
            dve.wait_ge(weights_loaded, 16 * NW)
            dve.wait_ge(v_columns_set, 1 + CT)
            ns.on_vector(dve, x_sb)
            inner = ns
            if affine:
                for i in range(NTT):
                    dve.tensor_scalar(xo[:, i, :], x_sb[:, i, :], ns.mv[:, i, 0:1], ns.rstd[:, i:i + 1],
                                      ALU.subtract, ALU.mult)
                dve.drain()
                ns2.on_vector(dve, xo)
                inner = ns2
            with dve.Fori(0, NCH) as c:
                dve.wait_ge(transposed, c)
                for i in range(CT):
                    tile = bass.ds(c * CT + i, 1)
                    dve.tensor_scalar((x1 if affine else xn)[:, i:i + 1, :], xo[:, tile, :],
                                      inner.mv[:, tile, 0:1], inner.rstd[:, tile], ALU.subtract, ALU.mult)\
                        .then_inc(normed, 1)
                if affine:
                    dve.drain()
                    for i in range(CT):
                        dve.tensor_tensor(x2[:, i, :], x1[:, i, :], gb[:, 0, :], ALU.mult)
                    dve.drain()
                    for i in range(CT):
                        dve.tensor_tensor(xn[:, i, :], x2[:, i, :], gb[:, 1, :], ALU.add).then_inc(normed, 1)
                dve.wait_ge(qk_stored, c * 64)
                for n in range(NQ):
                    j, m = n // KD, n % KD
                    dve.wait_ge(hi_done, c * NQ + n + 1)
                    dve.scalar_tensor_tensor(out=lo[:, j, m, :], in0=ps_qk[:, n % 2, :], scalar=bqk[:, j, m:m + 1],
                                             in1=hi[:, j, m, :], op0=ALU.add, op1=ALU.subtract).then_inc(lo_done, 1)
                dve.wait_ge(v_stored, c * 16)
                for i in range(CT):
                    dve.wait_ge(v_done, c * CT + i + 1)
                    dve.tensor_tensor(v4[:, i, :, 0:hd], ps_v[:, i % 2, 0:D].rearrange("p (h c) -> p h c", c=hd),
                                      bv[:, :].rearrange("p (h c) -> p h c", c=hd), ALU.add).then_inc(v_written, 1)

        @block.scalar
        def _(act):
            ns.on_scalar(act)
            if affine:
                ns2.on_scalar(act)
            act.wait_ge(weights_loaded, 16 * NW)
            with act.Fori(0, NCH) as c:
                act.wait_ge(transposed, c + 1)
                act.wait_ge(v_done, c * CT)
                act.activation(xt[:, :, :], ps_t[:, :, :], ACT.Copy).then_inc(xt_ready, 1)
                act.wait_ge(qk_stored, c * 64)
                for n in range(NQ):
                    j, m = n // KD, n % KD
                    act.wait_ge(qk_done, c * NQ + n + 1)
                    act.activation(hi[:, j, m, :], ps_qk[:, n % 2, :], ACT.Identity,
                                   bias=bqk[:, j, m:m + 1]).then_inc(hi_done, 1)

        @block.tensor
        def _(pe):
            pe.wait_ge(weights_loaded, 16 * NW)
            with pe.Fori(0, NCH) as c:
                pe.wait_ge(normed, (c + 1) * (2 * CT if affine else CT))
                pe.wait_ge(xt_ready, c)
                for k in range(KD):
                    for i in range(CT):
                        ins = pe.transpose(ps_t[:, k, i * P:(i + 1) * P], xn[:, i, k * P:(k + 1) * P], ident[:, :])
                ins.then_inc(transposed, 1)
                pe.wait_ge(xt_ready, c + 1)
                for n in range(NQ):
                    j, m = n // KD, n % KD
                    if n >= 2:
                        pe.wait_ge(lo_done, c * NQ + n - 1)
                    else:
                        pe.wait_ge(lo_done, c * NQ)
                    for k in range(KD):
                        ins = pe.matmul(ps_qk[:, n % 2, :], wt[j][:, k, m * P:(m + 1) * P], xt[:, k, :],
                                        start=k == 0, stop=k == KD - 1)
                    ins.then_inc(qk_done, 1)
                for i in range(CT):
                    if i >= 2:
                        pe.wait_ge(v_written, c * CT + i - 1)
                    else:
                        pe.wait_ge(v_written, c * CT)
                    for k in range(KD):
                        ins = pe.matmul(ps_v[:, i % 2, 0:D], xt[:, k, i * P:(i + 1) * P], wt[2][:, k, :],
                                        start=k == 0, stop=k == KD - 1)
                    ins.then_inc(v_done, 1)

UNITS = 16
UF = 64
SLOTS = 3
NEG_ROW = 96
S1_ORDER = (3, 2, 0, 1)


class Unit:

    def __init__(self, t, c):
        self.t, self.c = t, c
        self.n = t * SLOTS + c
        self.slot = c % SLOTS
        self.turn = t + c // SLOTS

    def plus(self, d):
        return Unit(self.t, self.c + d)

    def exists(self):
        return not isinstance(self.n, int) or 0 <= self.n < UNITS


def attention(nc, tag, ident, ident_bf, mask_q, mask_k, q_dram, k_dram, v_dram, att_dram,
              heads, pitch, causal, parts, scale):
    hu = heads * UF // D
    hd = D // heads
    nt = CT * hu
    nx = nt // 2
    rows = hu * pitch
    last_part = len(parts) - 1
    n_loads = sum(len(q) + len(k) for q, k in parts)
    with ExitStack() as ctx:
        s = Scope(nc, ctx, tag)
        qs = [[s.sbuf(f"qs{a}_{z}", [P, hu, S], F32R) for z in range(SLOTS)] for a in range(len(parts))]
        ks = [[s.sbuf(f"ks{a}_{z}", [P, hu, S], F32R) for z in range(SLOTS)] for a in range(len(parts))]
        vs = [s.sbuf(f"vs{z}", [P, CT, rows]) for z in range(SLOTS)]
        pt = s.sbuf("pt", [P, nt, S])
        mx = s.sbuf("mx", [P, nt])
        neg = s.sbuf("neg", [P, 2, nt], F32R)
        neg_t = s.sbuf("neg_t", [2 * nt, P])
        osb = s.sbuf("osb", [rows, S])
        rsum = s.sbuf("rsum", [P, CT, hu, 1])
        att = s.sbuf("att", [P, CT, UF])
        ps_1 = s.psum("ps_1", [P, 2, S])
        ps_2 = s.psum("ps_2", [P, 2, 2, S])
        ps_o = s.psum("ps_o", [rows, S])
        ps_tr = s.psum("ps_tr", [P, S])

        stacks_set = s.sem("stacks_set")
        qk_loaded = [s.sem(f"qk_loaded{z}") for z in range(SLOTS)]
        v_loaded = [s.sem(f"v_loaded{z}") for z in range(SLOTS)]
        neg_loaded = [s.sem(f"neg_loaded{z}") for z in range(SLOTS)]
        s1_done = s.sem("s1_done")
        max_done = s.sem("max_done")
        neg_ready = s.sem("neg_ready")
        neg_turned = s.sem("neg_turned")
        neg_copied = s.sem("neg_copied")
        s2_done = s.sem("s2_done")
        exp_done = s.sem("exp_done")
        pv_done = s.sem("pv_done")
        o_copied = s.sem("o_copied")
        o_turned = s.sem("o_turned")
        normalized = s.sem("normalized")
        att_stored = s.sem("att_stored")
        block = ctx.enter_context(nc.Block())

        def loop(eng, body):
            for u in (-1, 0, 1):
                body(Unit(0, u))
            with eng.Fori(0, 4) as t:
                for c in (2, 3, 4):
                    body(Unit(t, c))
            for u in (14, 15, 16, 17):
                body(Unit(0, u))

        def off(j):
            return j * P if causal else 0

        def width(i):
            return (i + 1) * P if causal else S

        def last_exp(j):
            return ((j + 1) * hu - 1) // 2 + 1

        @block.sync
        def _(sp):
            sp.wait_ge(stacks_set, 3 * SLOTS)

            def load(u):
                z = u.slot
                b, g = u.n // 4, u.n % 4
                for a, both in enumerate(parts):
                    for dram, stack, blocks in ((q_dram, qs, both[0]), (k_dram, ks, both[1])):
                        for row, half in blocks:
                            src = dram[half][bass.ds(g * UF, UF), bass.ds(b * S, S)]
                            sp.dma_start(stack[a][z][row:row + hd, :, :].bitcast(F32),
                                         src.rearrange("(h d) t -> d h t", d=hd)).then_inc(qk_loaded[z], 16)

            def load_v(u):
                z = u.slot
                b, g = u.n // 4, u.n % 4
                src = v_dram[bass.ds(b * S, S), bass.ds(g * rows, rows)]
                sp.dma_start(vs[z][:, :, :], src.rearrange("(j p) f -> p j f", p=P)).then_inc(v_loaded[z], 16)

            def body(u):
                w = u.plus(1)
                if w.exists():
                    if u.plus(-2).exists():
                        sp.wait_ge(s2_done, (u.n - 1) * nx)
                    load(w)
                    if u.plus(-2).exists():
                        sp.wait_ge(pv_done, u.n - 1)
                    load_v(w)

            loop(sp, body)

        @block.gpsimd
        def _(pool):
            for z in range(SLOTS):
                pool.memset(qs[last_part][z][64:P, :, :].bitcast(F32), 0.0).then_inc(stacks_set, 1)
                pool.memset(ks[last_part][z][64:P, :, :].bitcast(F32), 0.0).then_inc(stacks_set, 1)
            pool.wait_ge(stacks_set, 2 * SLOTS)
            for z in range(SLOTS):
                pool.memset(ks[last_part][z][NEG_ROW:NEG_ROW + 2, :, :].bitcast(F32), 1.0).then_inc(stacks_set, 1)
            pool.wait_ge(stacks_set, 3 * SLOTS)

        @block.tensor
        def _(pe):
            def scores_q(u, step):
                if not u.exists():
                    return
                i = S1_ORDER[step]
                z = u.slot
                if step == 0:
                    pe.wait_ge(qk_loaded[z], (u.turn + 1) * 16 * n_loads)
                for h in range(hu):
                    n = step * hu + h
                    if not (isinstance(u.n, int) and u.n * nt + n - 1 <= 0):
                        pe.wait_ge(max_done, u.n * nt + n - 1)
                    out = ps_1[:, n % 2, 0:width(i)]
                    for a in range(len(parts)):
                        ins = pe.matmul(out, qs[a][z][0:NEG_ROW if a == last_part else P, h, i * P:(i + 1) * P],
                                        ks[a][z][0:NEG_ROW if a == last_part else P, h, 0:width(i)],
                                        start=a == 0, stop=a == last_part and not causal)
                    if causal:
                        ins = pe.matmul(ps_1[:, n % 2, i * P:(i + 1) * P], ident_bf[:, :], mask_q[:, :],
                                        start=False, stop=True)
                    ins.then_inc(s1_done, 1)

            def scores_k(u, j):
                if not u.exists():
                    return
                z = u.slot
                if j == 0:
                    pe.wait_ge(neg_loaded[z], (u.turn + 1) * 32)
                for n in range(nx):
                    if 2 * n // hu != j:
                        continue
                    if not (isinstance(u.n, int) and u.n * nx + n - 1 <= 0):
                        pe.wait_ge(exp_done, u.n * nx + n - 1)
                    for e in (2 * n, 2 * n + 1):
                        jj, h = e // hu, e % hu
                        out = ps_2[:, n % 2, e % 2, 0:S - off(jj)]
                        for a in range(len(parts)):
                            ins = pe.matmul(out, ks[a][z][:, h, jj * P:(jj + 1) * P], qs[a][z][:, h, off(jj):S],
                                            start=a == 0, stop=a == last_part and not causal)
                        if causal:
                            ins = pe.matmul(ps_2[:, n % 2, e % 2, 0:P], ident_bf[:, :], mask_k[:, :],
                                            start=False, stop=True)
                    ins.then_inc(s2_done, 1)

            def values(u, j):
                if not u.exists():
                    return
                z = u.slot
                if j == 0:
                    pe.wait_ge(v_loaded[z], (u.turn + 1) * 16)
                    pe.wait_ge(o_copied, u.n)
                pe.wait_ge(exp_done, u.n * nx + last_exp(j))
                for h in range(hu):
                    ins = pe.matmul(ps_o[h * pitch:(h + 1) * pitch, off(j):S], vs[z][:, j, h * pitch:(h + 1) * pitch],
                                    pt[:, j * hu + h, 0:S - off(j)], start=j == 0, stop=j == CT - 1)
                if j == CT - 1:
                    ins.then_inc(pv_done, 1)

            def turn_output(u):
                if not u.exists():
                    return
                pe.wait_ge(o_copied, u.n + 1)
                pe.wait_ge(normalized, u.n)
                w = u.plus(1)
                if w.exists():
                    pe.wait_ge(neg_copied, w.n + 1)
                for i in range(CT):
                    ins = pe.transpose(ps_tr[:, i * rows:(i + 1) * rows], osb[:, i * P:(i + 1) * P],
                                       ident[0:rows, 0:rows])
                ins.then_inc(o_turned, 1)

            def turn_maxima(u):
                if not u.exists():
                    return
                pe.wait_ge(neg_ready, u.n + 1)
                if u.plus(-2).exists():
                    pe.wait_ge(normalized, u.n - 1)
                pe.transpose(ps_tr[0:2 * nt, 0:P], neg[:, :, :].bitcast(F32).rearrange("p r n -> p (r n)"),
                             ident[:, :]).then_inc(neg_turned, 1)

            def body(u):
                scores_q(u, 2)
                scores_k(u.plus(-1), 0)
                values(u.plus(-2), 3)
                scores_q(u, 3)
                scores_k(u.plus(-1), 1)
                values(u.plus(-1), 0)
                turn_output(u.plus(-2))
                scores_q(u.plus(1), 0)
                scores_k(u.plus(-1), 2)
                values(u.plus(-1), 1)
                turn_maxima(u)
                scores_q(u.plus(1), 1)
                scores_k(u.plus(-1), 3)
                values(u.plus(-1), 2)

            loop(pe, body)

        @block.scalar
        def _(act):
            def exps(u, j):
                if not u.exists():
                    return
                for n in range(nx):
                    if 2 * n // hu != j:
                        continue
                    act.wait_ge(s2_done, u.n * nx + n + 1)
                    if j == 0:
                        act.wait_ge(pv_done, u.n)
                    w = S - off(j)
                    act.activation(pt[:, 2 * n:2 * n + 2, 0:w], ps_2[:, n % 2, :, 0:w], ACT.Exp,
                                   scale=scale).then_inc(exp_done, 1)

            def copy_output(u):
                if not u.exists():
                    return
                act.wait_ge(pv_done, u.n + 1)
                act.wait_ge(o_turned, u.n)
                act.activation(osb[:, :], ps_o[:, :], ACT.Copy).then_inc(o_copied, 1)

            def copy_maxima(u):
                if not u.exists():
                    return
                act.wait_ge(neg_turned, u.n + 1)
                w = u.plus(-1)
                if w.exists():
                    act.wait_ge(neg_loaded[w.slot], (w.turn + 1) * 32)
                act.activation(neg_t[:, :], ps_tr[0:2 * nt, 0:P], ACT.Copy).then_inc(neg_copied, 1)
                act.wait_ge(neg_copied, u.n + 1)
                for r in range(2):
                    act.dma_start(qs[last_part][u.slot][NEG_ROW + r:NEG_ROW + r + 1, :, :].bitcast(F32),
                                  neg_t[r * nt:(r + 1) * nt, :]).then_inc(neg_loaded[u.slot], 16)

            def store_output(u):
                if not u.exists():
                    return
                b, g = u.n // 4, u.n % 4
                act.wait_ge(normalized, u.n + 1)
                dst = att_dram[bass.ds(b * S, S), bass.ds(g * UF, UF)]
                act.dma_start(dst.rearrange("(i p) f -> p i f", p=P), att[:, :, :]).then_inc(att_stored, 16)

            def body(u):
                copy_output(u.plus(-2))
                exps(u.plus(-1), 0)
                exps(u.plus(-1), 1)
                exps(u.plus(-1), 2)
                copy_maxima(u)
                exps(u.plus(-1), 3)
                store_output(u.plus(-2))

            loop(act, body)
            act.wait_ge(att_stored, 16 * UNITS)

        @block.vector
        def _(dve):
            def maxima(u, step):
                if not u.exists():
                    return
                i = S1_ORDER[step]
                for h in range(hu):
                    n = step * hu + h
                    dve.wait_ge(s1_done, u.n * nt + n + 1)
                    dve.tensor_reduce(mx[:, h * CT + i:h * CT + i + 1], ps_1[:, n % 2, 0:width(i)], AX_X, ALU.max)\
                        .then_inc(max_done, 1)

            def split_maxima(u):
                if not u.exists():
                    return
                dve.drain()
                dve.wait_ge(neg_turned, u.n)
                dve.tensor_scalar(neg[:, 0, :], mx[:, :], -1.0, None, ALU.mult)
                dve.drain()
                dve.scalar_tensor_tensor(out=neg[:, 1, :], in0=mx[:, :], scalar=-1.0, in1=neg[:, 0, :],
                                         op0=ALU.mult, op1=ALU.subtract).then_inc(neg_ready, 1)
                dve.drain()

            def normalize(u):
                if not u.exists():
                    return
                dve.wait_ge(o_turned, u.n + 1)
                dve.wait_ge(att_stored, u.n * 16)
                out = ps_tr[:, 0:CT * rows].rearrange("p (i h c) -> p i h c", i=CT, c=pitch)
                dve.reciprocal(rsum[:, :, :, :], out[:, :, :, hd:hd + 1])
                dve.drain()
                dve.tensor_tensor(att[:, :, :].rearrange("p i (h c) -> p i h c", c=hd), out[:, :, :, 0:hd],
                                  rsum[:, :, :, :].to_broadcast([P, CT, hu, hd]), ALU.mult).then_inc(normalized, 1)

            def body(u):
                maxima(u, 2)
                maxima(u, 3)
                split_maxima(u)
                maxima(u.plus(1), 0)
                normalize(u.plus(-2))
                maxima(u.plus(1), 1)

            loop(dve, body)


PARTS_16 = [(((0, 0), (16, 1), (32, 0), (48, 1)), ((0, 0), (16, 0), (32, 1), (48, 1)))]
PARTS_64 = [(((0, 0), (64, 1)), ((0, 0), (64, 0))), (((0, 0),), ((0, 1),))]

def project_out(nc, tag, x_sb, ident, wo, bo, att_dram):
    with ExitStack() as ctx:
        s = Scope(nc, ctx, tag)
        w = s.sbuf("w", [P, KD, D])
        b = s.sbuf("b", [P, D])
        at = [s.sbuf(f"at{z}", [P, CT, D]) for z in range(2)]
        att_t = [s.sbuf(f"att_t{z}", [P, KD, CHUNK]) for z in range(2)]
        ps_t = s.psum("ps_t", [P, 2, KD, CHUNK])
        ps_y = s.psum("ps_y", [P, 2, S])
        weights_loaded = s.sem("weights_loaded")
        loaded = [s.sem(f"loaded{z}") for z in range(2)]
        turned = s.sem("turned")
        copied = s.sem("copied")
        made = s.sem("made")
        biased = s.sem("biased")
        added = s.sem("added")
        block = ctx.enter_context(nc.Block())

        @block.sync
        def _(sp):
            sp.dma_start(b[:, :], bo.partition_broadcast(P)).then_inc(weights_loaded, 16)
            sp.dma_start(w[:, :, :], wo.rearrange("(k p) n -> p k n", p=P)).then_inc(weights_loaded, 16)
            with sp.Fori(0, NCH // 2) as t:
                for z in range(2):
                    sp.wait_ge(turned, 2 * t)
                    sp.dma_start(at[z][:, :, :], att_dram[bass.ds((2 * t + z) * CHUNK, CHUNK), :]
                                 .rearrange("(i p) f -> p i f", p=P)).then_inc(loaded[z], 16)

        @block.gpsimd
        def _(pool):
            pool.wait_ge(weights_loaded, 32)
            for i in range(NTT):
                ins = pool.tensor_tensor(x_sb[:, i, :], x_sb[:, i, :], b[:, :], ALU.add)
            ins.then_inc(biased, 1)

        @block.tensor
        def _(pe):
            pe.wait_ge(weights_loaded, 32)
            with pe.Fori(0, NCH // 2) as t:
                for z in range(2):
                    pe.wait_ge(loaded[z], 16 * t + 16)
                    pe.wait_ge(copied, 2 * t)
                    for k in range(KD):
                        for i in range(CT):
                            ins = pe.transpose(ps_t[:, z, k, i * P:(i + 1) * P], at[z][:, i, k * P:(k + 1) * P],
                                               ident[:, :])
                    ins.then_inc(turned, 1)
                for z in range(2):
                    pe.wait_ge(copied, 2 * t + z + 1)
                    for i in range(CT):
                        n = z * CT + i
                        if n >= 2:
                            pe.wait_ge(added, t * 2 * CT + n - 1)
                        else:
                            pe.wait_ge(added, t * 2 * CT)
                        for k in range(KD):
                            ins = pe.matmul(ps_y[:, n % 2, 0:D], att_t[z][:, k, i * P:(i + 1) * P], w[:, k, :],
                                            start=k == 0, stop=k == KD - 1)
                        ins.then_inc(made, 1)

        @block.scalar
        def _(act):
            with act.Fori(0, NCH // 2) as t:
                for z in range(2):
                    act.wait_ge(turned, 2 * t + z + 1)
                    act.wait_ge(made, t * 2 * CT)
                    act.activation(att_t[z][:, :, :], ps_t[:, z, :, :], ACT.Copy).then_inc(copied, 1)

        @block.vector
        def _(dve):
            dve.wait_ge(biased, 1)
            with dve.Fori(0, NCH // 2) as t:
                for n in range(2 * CT):
                    dve.wait_ge(made, t * 2 * CT + n + 1)
                    xt = x_sb[:, bass.ds(t * 2 * CT + n, 1), :]
                    dve.tensor_tensor(xt, xt, ps_y[:, n % 2, 0:D].unsqueeze(1), ALU.add).then_inc(added, 1)


def mlp(nc, tag, x_sb, ident, w_gate, w_up, w_down, sizes, func, xn_all=None, on_sync=None, on_gpsimd=None):
    nm = len(sizes)
    starts = [sum(sizes[:m]) for m in range(nm)]
    with ExitStack() as ctx:
        s = Scope(nc, ctx, tag)
        ns = NormStats(s) if xn_all is None else None
        xn = s.sbuf("xn", [P, CT, D])
        xt = s.sbuf("xt", [P, KD, CHUNK])
        gs = s.sbuf("gs", [P, 2, CHUNK])
        inner = s.sbuf("inner", [P, nm, CHUNK])
        ps_t = s.psum("ps_t", [P, KD, CHUNK])
        ps_g = s.psum("ps_g", [P, 2, CHUNK])
        ps_u = s.psum("ps_u", [P, 2, CHUNK])
        ps_y = s.psum("ps_y", [P, 2, S])
        normed = s.sem("normed")
        turned = s.sem("turned")
        xt_ready = s.sem("xt_ready")
        gate_done = s.sem("gate_done")
        up_done = s.sem("up_done")
        acted = s.sem("acted")
        gated = s.sem("gated")
        made = s.sem("made")
        added = s.sem("added")
        block = ctx.enter_context(nc.Block())

        def chunks(eng, body):
            with eng.Fori(0, NCH - 1) as c:
                body(c, True)
            body(NCH - 1, False)

        if on_sync:
            block.sync(on_sync)
        if on_gpsimd:
            block.gpsimd(on_gpsimd)

        @block.vector
        def _(dve):
            if ns:
                ns.on_vector(dve, x_sb)

            def norm(c):
                dve.wait_ge(turned, c)
                for i in range(CT):
                    tile = bass.ds(c * CT + i, 1)
                    if xn_all is not None:
                        dve.tensor_scalar(xn[:, i:i + 1, :], xn_all[:, tile, :], 1.0, None, ALU.mult)\
                            .then_inc(normed, 1)
                        continue
                    dve.tensor_scalar(xn[:, i:i + 1, :], x_sb[:, tile, :], ns.mv[:, tile, 0:1], ns.rstd[:, tile],
                                      ALU.subtract, ALU.mult).then_inc(normed, 1)

            def body(c, more):
                for m in range(nm):
                    r = sizes[m]
                    dve.wait_ge(acted, c * nm + m + 1)
                    if m == 0:
                        dve.wait_ge(made, c * CT)
                    dve.wait_ge(up_done, c * nm + m + 1)
                    dve.tensor_tensor(inner[0:r, m, :], gs[0:r, m % 2, :], ps_u[0:r, m % 2, :], ALU.mult)\
                        .then_inc(gated, 1)
                    if more and m == nm // 2:
                        norm(c + 1)
                for i in range(CT):
                    dve.wait_ge(made, c * CT + i + 1)
                    tile = x_sb[:, bass.ds(c * CT + i, 1), :]
                    dve.tensor_tensor(tile, tile, ps_y[:, i % 2, 0:D].unsqueeze(1), ALU.add).then_inc(added, 1)

            norm(0)
            chunks(dve, body)

        @block.scalar
        def _(act):
            if ns:
                ns.on_scalar(act)

            def copy_xt(c):
                act.wait_ge(turned, c + 1)
                act.wait_ge(up_done, c * nm)
                act.activation(xt[:, :, :], ps_t[:, :, :], ACT.Copy).then_inc(xt_ready, 1)

            def body(c, more):
                for m in range(nm):
                    r = sizes[m]
                    act.wait_ge(gate_done, c * nm + m + 1)
                    if m >= 2:
                        act.wait_ge(gated, c * nm + m - 1)
                    else:
                        act.wait_ge(gated, c * nm)
                    act.activation(gs[0:r, m % 2, :], ps_g[0:r, m % 2, :], func).then_inc(acted, 1)
                if more:
                    copy_xt(c + 1)

            copy_xt(0)
            chunks(act, body)

        @block.tensor
        def _(pe):
            def turn(c):
                pe.wait_ge(normed, c * CT + CT)
                pe.wait_ge(xt_ready, c)
                for k in range(KD):
                    for i in range(CT):
                        ins = pe.transpose(ps_t[:, k, i * P:(i + 1) * P], xn[:, i, k::KD], ident[:, :])
                ins.then_inc(turned, 1)

            def body(c, more):
                pe.wait_ge(xt_ready, c + 1)
                for m in range(nm):
                    r = sizes[m]
                    cols = slice(starts[m], starts[m] + r)
                    for w, ps, freed, done in ((w_gate, ps_g, acted, gate_done), (w_up, ps_u, gated, up_done)):
                        if m >= 2:
                            pe.wait_ge(freed, c * nm + m - 1)
                        else:
                            pe.wait_ge(freed, c * nm)
                        for k in range(KD):
                            ins = pe.matmul(ps[0:r, m % 2, :], w[:, k, cols], xt[:, k, :],
                                            start=k == 0, stop=k == KD - 1)
                        ins.then_inc(done, 1)
                if more:
                    turn(c + 1)
                pe.wait_ge(gated, c * nm + nm)
                for i in range(CT):
                    if i >= 2:
                        pe.wait_ge(added, c * CT + i - 1)
                    else:
                        pe.wait_ge(added, c * CT)
                    for m in range(nm):
                        r = sizes[m]
                        ins = pe.matmul(ps_y[:, i % 2, 0:D], inner[0:r, m, i * P:(i + 1) * P], w_down(m),
                                        start=m == 0, stop=m == nm - 1)
                    ins.then_inc(made, 1)

            turn(0)
            chunks(pe, body)


PIECE = 512
TABLE = 0xC8643210 - (1 << 32)


def unpack_weights(nc, tag, codes, scales, out, n_cols):
    per = n_cols // PIECE
    n_pieces = len(out) * per
    with ExitStack() as ctx:
        s = Scope(nc, ctx, tag)
        code = [s.sbuf(f"code{z}", [P, PIECE], I32) for z in range(2)]
        scale = [s.sbuf(f"scale{z}", [P, PIECE]) for z in range(2)]
        half = [s.sbuf(f"half{z}", [P, PIECE]) for z in range(2)]
        table = s.sbuf("table", [P, PIECE], I32)
        shift = s.sbuf("shift", [P, 2, PIECE], I32)
        found = s.sbuf("found", [P, 2, PIECE], I32)
        mag = [s.sbuf(f"mag{z}", [P, 2, PIECE], I32) for z in range(2)]
        magf = [s.sbuf(f"magf{z}", [P, 2, PIECE]) for z in range(2)]
        sign = s.sbuf("sign", [P, 2, PIECE], I32)
        signed = [s.sbuf(f"signed{z}", [P, 2, PIECE], I32) for z in range(2)]
        loaded = [s.sem(f"loaded{z}") for z in range(2)]
        table_set = s.sem("table_set")
        halved = s.sem("halved")
        read = s.sem("read")
        converted = s.sem("converted")
        product = s.sem("product")
        block = ctx.enter_context(nc.Block())

        @block.sync
        def _(sp):
            for n in range(n_pieces):
                z, w, cols = n % 2, n // per, slice(n % per * PIECE, (n % per + 1) * PIECE)
                if n >= 2:
                    sp.wait_ge(read, n - 1)
                sp.dma_start(code[z][:, :], codes[w][:, cols]).then_inc(loaded[z], 16)
                sp.dma_start(scale[z][:, :], scales[w][:, cols].unsqueeze(1).to_broadcast([8, 16, PIECE]))\
                    .then_inc(loaded[z], 16)

        @block.scalar
        def _(act):
            def halve(n):
                act.wait_ge(loaded[n % 2], 32 * (n // 2 + 1))
                if n >= 2:
                    act.wait_ge(read, n - 1)
                act.mul(half[n % 2][:, :], scale[n % 2][:, :], 0.5).then_inc(halved, 1)

            halve(0)
            for n in range(n_pieces):
                if n + 1 < n_pieces:
                    halve(n + 1)
                act.wait_ge(read, n + 1)
                if n >= 2:
                    act.wait_ge(product, 2 * n - 2)
                act.activation(magf[n % 2][:, :, :], mag[n % 2][:, :, :], ACT.Copy).then_inc(converted, 1)

        @block.vector
        def _(dve):
            dve.memset(table[:, :], TABLE)
            for n in range(n_pieces):
                z = n % 2
                dve.wait_ge(loaded[z], 32 * (n // 2 + 1))
                dve.tensor_scalar(shift[:, 0, :], code[z][:, :], 7, 2, ALU.bitwise_and, ALU.logical_shift_left)
                dve.tensor_scalar(shift[:, 1, :], code[z][:, :], 2, 28, ALU.logical_shift_right, ALU.bitwise_and)
                dve.tensor_scalar(sign[:, 0, :], code[z][:, :], 8, 28, ALU.bitwise_and, ALU.logical_shift_left)
                dve.tensor_scalar(sign[:, 1, :], code[z][:, :], 128, 24, ALU.bitwise_and, ALU.logical_shift_left)
                dve.drain()
                for k in range(2):
                    dve.tensor_tensor(found[:, k, :], table[:, :], shift[:, k, :], ALU.logical_shift_right)
                dve.wait_ge(halved, n + 1)
                if n >= 2:
                    dve.wait_ge(product, 2 * n - 2)
                for k in range(2):
                    dve.tensor_tensor(signed[z][:, k, :], sign[:, k, :], half[z][:, :].bitcast(I32), ALU.bitwise_xor)
                dve.drain()
                dve.tensor_scalar(mag[z][:, :, :], found[:, :, :], 15, None, ALU.bitwise_and).then_inc(read, 1)

        @block.gpsimd
        def _(pool):
            for n in range(n_pieces):
                z, w, cols = n % 2, n // per, slice(n % per * PIECE, (n % per + 1) * PIECE)
                pool.wait_ge(converted, n + 1)
                for k in range(2):
                    pool.tensor_tensor(out[w][:, k, cols], magf[z][:, k, :], signed[z][:, k, :].bitcast(F32),
                                       ALU.mult).then_inc(product, 1)
            pool.wait_ge(product, 2 * n_pieces)

NE = 64
TOP = 6
FE = 176
FEP = FE // 2
FPAD = 96
NTILE = (T * TOP - NE) // P + NE
NSLOT = NTILE * P
TOP_EPS = 1e-20


def route(nc, tag, x_sb, ident, gate_w, xn_all, weights, slots, expert_dram, load_shared):
    with ExitStack() as ctx:
        s = Scope(nc, ctx, tag)
        ns = NormStats(s)
        gw = s.sbuf("gw", [P, KD, NE])
        xt = s.sbuf("xt", [P, 2, KD, P])
        logits = s.sbuf("logits", [P, NTT, NE])
        top = s.sbuf("top", [P, NTT, 8])
        row = s.sbuf("row", [P, NTT, 1])
        row2 = s.sbuf("row2", [P, NTT, 1])
        shifted = s.sbuf("shifted", [P, NTT, NE])
        exps = s.sbuf("exps", [P, NTT, NE])
        scores = s.sbuf("scores", [P, NTT, NE])
        idx = s.sbuf("idx", [P, NTT, 8], U32)
        idxf = s.sbuf("idxf", [P, NTT, 8])
        chosen = s.sbuf("chosen", [P, TOP, NTT, NE])
        mask = [s.sbuf(f"mask{z}", [P, NTT, NE]) for z in range(2)]
        mask_bf = s.sbuf("mask_bf", [P, NTT, NE], BF16)
        before = s.sbuf("before", [P, P], BF16)
        ones = s.sbuf("ones", [P, P], BF16)
        count = s.sbuf("count", [P, NE], I32)
        tiles_i = s.sbuf("tiles_i", [P, NE], I32)
        tiles = s.sbuf("tiles", [P, NE])
        incl = [s.sbuf(f"incl{z}", [P, NE]) for z in range(2)]
        start = s.sbuf("start", [P, NE])
        slot = s.sbuf("slot", [P, NTT, NE])
        picked = s.sbuf("picked", [P, TOP, NTT, NE])
        slot_f = s.sbuf("slot_f", [P, TOP, NTT, 1])
        iota_e = s.sbuf("iota_e", [P, NE])
        iota_t = s.sbuf("iota_t", [P, 2])
        passed = s.sbuf("passed", [P, 2, NE])
        owner = s.sbuf("owner", [P, 2, 1])
        owner_i = s.sbuf("owner_i", [P, 2], I32)
        ps_t = s.psum("ps_t", [P, 2, S])
        ps_l = s.psum("ps_l", [P, 2, S])
        ps_pos = s.psum("ps_pos", [P, 2, NTT // 2, NE])
        ps_n = s.psum("ps_n", [P, S])
        gw_loaded = s.sem("gw_loaded")
        shared_loaded = s.sem("shared_loaded")
        filled = s.sem("filled")
        shaped = s.sem("shaped")
        normed = s.sem("normed")
        turned = s.sem("turned")
        xt_ready = s.sem("xt_ready")
        logits_done = s.sem("logits_done")
        logits_copied = s.sem("logits_copied")
        shifted_done = s.sem("shifted_done")
        exps_done = s.sem("exps_done")
        mask_done = s.sem("mask_done")
        placed = s.sem("placed")
        owned = s.sem("owned")
        owner_stored = s.sem("owner_stored")
        block = ctx.enter_context(nc.Block())

        @block.sync
        def _(sp):
            sp.dma_start(gw[:, :, :], gate_w.rearrange("(p k) n -> p k n", k=KD)).then_inc(gw_loaded, 16)
            n = load_shared(sp, shared_loaded)
            sp.wait_ge(owned, 1)
            sp.dma_start(expert_dram.rearrange("(p j) -> p j", p=P), owner_i[:, :]).then_inc(owner_stored, 16)
            sp.wait_ge(owner_stored, 16)
            sp.wait_ge(shared_loaded, n)

        @block.gpsimd
        def _(pool):
            pool.memset(ones[:, :], 1.0).then_inc(filled, 1)
            pool.wait_ge(filled, 1)
            pool.affine_select(out=before[:, :], in_=ones[:, :], compare_op=ALU.is_gt, fill=0.0, base=0,
                               pattern=[[1, P]], channel_multiplier=-1).then_inc(shaped, 1)
            pool.iota(iota_e[:, :], pattern=[[1, NE]], base=0, channel_multiplier=0,
                      allow_small_or_imprecise_dtypes=True).then_inc(shaped, 1)
            pool.iota(iota_t[:, :], pattern=[[1, 2]], base=0, channel_multiplier=2,
                      allow_small_or_imprecise_dtypes=True).then_inc(shaped, 1)

        @block.scalar
        def _(act):
            ns.on_scalar(act)
            for i in range(NTT):
                act.wait_ge(turned, i + 1)
                if i >= 2:
                    act.wait_ge(logits_done, i - 1)
                act.activation(xt[:, i % 2, :, :], ps_t[:, i % 2, 0:KD * P].rearrange("p (k t) -> p k t", k=KD),
                               ACT.Copy).then_inc(xt_ready, 1)
            act.wait_ge(shifted_done, 1)
            act.activation(exps[:, :, :], shifted[:, :, :], ACT.Exp).then_inc(exps_done, 1)

        @block.tensor
        def _(pe):
            pe.wait_ge(gw_loaded, 16)

            def turn(i):
                pe.wait_ge(normed, i + 1)
                if i >= 2:
                    pe.wait_ge(xt_ready, i - 1)
                for k in range(KD):
                    ins = pe.transpose(ps_t[:, i % 2, k * P:(k + 1) * P], xn_all[:, i, k::KD], ident[:, :])
                ins.then_inc(turned, 1)

            turn(0)
            for i in range(NTT):
                if i + 1 < NTT:
                    turn(i + 1)
                pe.wait_ge(xt_ready, i + 1)
                if i >= 2:
                    pe.wait_ge(logits_copied, i - 1)
                for k in range(KD):
                    ins = pe.matmul(ps_l[:, i % 2, 0:NE], xt[:, i % 2, k, :], gw[:, k, :],
                                    start=k == 0, stop=k == KD - 1)
                ins.then_inc(logits_done, 1)
            pe.wait_ge(shaped, 3)
            pe.wait_ge(mask_done, 1)
            for i in range(NTT):
                out = ps_pos[:, i // (NTT // 2), i % (NTT // 2), :]
                for j in range(i):
                    pe.matmul(out, ones[:, :], mask_bf[:, j, :], start=j == 0, stop=False)
                pe.matmul(out, before[:, :], mask_bf[:, i, :], start=i == 0, stop=True)
            for j in range(NTT):
                ins = pe.matmul(ps_n[:, 0:NE], ones[:, :], mask_bf[:, j, :], start=j == 0, stop=j == NTT - 1)
            ins.then_inc(placed, 1)

        @block.vector
        def _(dve):
            ns.on_vector(dve, x_sb)
            for i in range(NTT):
                dve.tensor_scalar(xn_all[:, i, :], x_sb[:, i, :], ns.mv[:, i, 0:1], ns.rstd[:, i:i + 1],
                                  ALU.subtract, ALU.mult).then_inc(normed, 1)
            for i in range(NTT):
                dve.wait_ge(logits_done, i + 1)
                dve.tensor_copy(logits[:, i, :], ps_l[:, i % 2, 0:NE]).then_inc(logits_copied, 1)
            dve.drain()
            full = [P, NTT, NE]
            dve.tensor_reduce(row[:, :, :], logits[:, :, :], AX_X, ALU.max)
            dve.drain()
            dve.tensor_tensor(shifted[:, :, :], logits[:, :, :], row[:, :, :].to_broadcast(full), ALU.subtract)\
                .then_inc(shifted_done, 1)
            dve.wait_ge(exps_done, 1)
            dve.tensor_reduce(row[:, :, :], exps[:, :, :], AX_X, ALU.add)
            dve.drain()
            dve.reciprocal(row2[:, :, :], row[:, :, :])
            dve.drain()
            dve.tensor_tensor(scores[:, :, :], exps[:, :, :], row2[:, :, :].to_broadcast(full), ALU.mult)
            dve.drain()
            for i in range(NTT):
                dve.max(top[:, i, :], scores[:, i, :])
            dve.drain()
            for i in range(NTT):
                dve.max_index(idx[:, i, :], top[:, i, :], scores[:, i, :])
            dve.tensor_reduce(row[:, :, :], top[:, :, 0:TOP], AX_X, ALU.add)
            dve.drain()
            dve.tensor_copy(idxf[:, :, :], idx[:, :, :])
            dve.tensor_scalar(row2[:, :, :], row[:, :, :], TOP_EPS, None, ALU.add)
            dve.drain()
            dve.reciprocal(row[:, :, :], row2[:, :, :])
            dve.wait_ge(shaped, 3)
            for k in range(TOP):
                dve.tensor_tensor(chosen[:, k, :, :], iota_e[:, :].unsqueeze(1).to_broadcast(full),
                                  idxf[:, :, k:k + 1].to_broadcast(full), ALU.is_equal)
            dve.drain()
            dve.tensor_tensor(weights[:, :, :], top[:, :, 0:TOP], row[:, :, :].to_broadcast([P, NTT, TOP]), ALU.mult)
            dve.tensor_tensor(mask[0][:, :, :], chosen[:, 0, :, :], chosen[:, 1, :, :], ALU.add)
            for k in range(2, TOP):
                dve.drain()
                out = mask[(k + 1) % 2] if k < TOP - 1 else mask_bf
                ins = dve.tensor_tensor(out[:, :, :], mask[k % 2][:, :, :], chosen[:, k, :, :], ALU.add)
            ins.then_inc(mask_done, 1)
            dve.wait_ge(placed, 1)
            dve.tensor_scalar(count[:, :], ps_n[:, 0:NE], float(P - 1), None, ALU.add)
            dve.drain()
            dve.tensor_scalar(tiles_i[:, :], count[:, :], P.bit_length() - 1, None, ALU.logical_shift_right)
            dve.drain()
            dve.tensor_copy(tiles[:, :], tiles_i[:, :])
            dve.drain()
            dve.tensor_copy(incl[0][:, :], tiles[:, :])
            z, d = 0, 1
            while d < NE:
                dve.drain()
                dve.tensor_copy(incl[1 - z][:, 0:d], incl[z][:, 0:d])
                dve.tensor_tensor(incl[1 - z][:, d:NE], incl[z][:, d:NE], incl[z][:, 0:NE - d], ALU.add)
                z, d = 1 - z, 2 * d
            dve.drain()
            last = incl[z]
            dve.tensor_tensor(incl[1 - z][:, :], last[:, :], tiles[:, :], ALU.subtract)
            dve.tensor_tensor(passed[:, :, :], last[:, :].unsqueeze(1).to_broadcast([P, 2, NE]),
                              iota_t[:, :].unsqueeze(2).to_broadcast([P, 2, NE]), ALU.is_le)
            dve.drain()
            dve.tensor_scalar(start[:, :], incl[1 - z][:, :], float(P), None, ALU.mult)
            dve.tensor_reduce(owner[:, :, :], passed[:, :, :], AX_X, ALU.add)
            dve.drain()
            dve.tensor_scalar(owner_i[:, :], owner[:, :, 0], float(NE - 1), None, ALU.min).then_inc(owned, 1)
            half = NTT // 2
            for b in range(2):
                dve.tensor_tensor(slot[:, b * half:(b + 1) * half, :], ps_pos[:, b, :, :],
                                  start[:, :].unsqueeze(1).to_broadcast([P, half, NE]), ALU.add)
            dve.drain()
            for k in range(TOP):
                dve.tensor_tensor(picked[:, k, :, :], chosen[:, k, :, :], slot[:, :, :], ALU.mult)
            dve.drain()
            dve.tensor_reduce(slot_f[:, :, :, :], picked[:, :, :, :], AX_X, ALU.add)
            dve.drain()
            dve.tensor_copy(slots[:, :, :], slot_f[:, :, :, 0])


ZERO = 2048


def zero_fill(s, dram):
    zero = s.sbuf("zero", [P, ZERO])
    zero_set, zeroed = s.sem("zero_set"), s.sem("zeroed")
    flat = dram.rearrange("(p r) d -> p (r d)", p=P)
    steps = list(range(0, flat.shape[1], ZERO))

    def on_gpsimd(pool):
        pool.memset(zero[:, :], 0.0).then_inc(zero_set, 1)

    def on_sync(sp):
        sp.wait_ge(zero_set, 1)
        for a in steps:
            n = min(ZERO, flat.shape[1] - a)
            sp.dma_start(flat[:, a:a + n], zero[:, 0:n]).then_inc(zeroed, 16)
        sp.wait_ge(zeroed, 16 * len(steps))
    return on_sync, on_gpsimd


def scatter_program(xn_all, slots, sorted_dram, scattered):
    def on_gpsimd(pool):
        for i in range(NTT):
            for k in range(TOP):
                pool.indirect_dma_start(out=sorted_dram[:, :],
                                        out_offset=bass.IndirectOffsetOnAxis(ap=slots[:, k, i:i + 1], axis=0),
                                        in_=xn_all[:, i, :], in_offset=None).then_inc(scattered, 16)
        pool.wait_ge(scattered, 16 * TOP * NTT)
    return on_gpsimd


def experts(nc, tag, ident, w1, w2, expert_dram, sorted_dram, out_dram):
    R = 6
    G = 3
    with ExitStack() as ctx:
        s = Scope(nc, ctx, tag)
        cells = [s.sbuf(f"cells{z}", [1, G], I32) for z in range(R // G)]
        x = [s.sbuf(f"x{z}", [P, D]) for z in range(R)]
        wgu = [s.sbuf(f"wgu{z}", [P, KD, 2 * FE]) for z in range(R)]
        wd = [s.sbuf(f"wd{z}", [FPAD, 2, D]) for z in range(R)]
        xt = s.sbuf("xt", [P, G, KD, P])
        gs = s.sbuf("gs", [P, FE])
        hid = s.sbuf("hid", [P, 2 * FPAD])
        ht = [s.sbuf(f"ht{z}", [FPAD, 2, P]) for z in range(2)]
        y = [s.sbuf(f"y{z}", [P, D]) for z in range(R)]
        ps_x = s.psum("ps_x", [P, S])
        ps_gu = s.psum("ps_gu", [P, G, S])
        ps_h = s.psum("ps_h", [P, S])
        ps_y = s.psum("ps_y", [P, G, S])
        pads_set = s.sem("pads_set")
        cells_loaded = [s.sem(f"cells_loaded{z}") for z in range(R // G)]
        x_loaded = [s.sem(f"x_loaded{z}") for z in range(R)]
        wgu_loaded = [s.sem(f"wgu_loaded{z}") for z in range(R)]
        wd_loaded = [s.sem(f"wd_loaded{z}") for z in range(R)]
        x_turned = s.sem("x_turned")
        xt_ready = s.sem("xt_ready")
        gu_done = s.sem("gu_done")
        acted = s.sem("acted")
        gated = s.sem("gated")
        h_turned = s.sem("h_turned")
        ht_ready = s.sem("ht_ready")
        y_done = s.sem("y_done")
        y_copied = s.sem("y_copied")
        y_stored = [s.sem(f"y_stored{z}") for z in range(R)]
        block = ctx.enter_context(nc.Block())

        class Tile:

            def __init__(self, t, c):
                self.t, self.c = t, c
                self.n = t * R + c
                self.slot, self.bank = c % R, c % G
                self.turn = t + c // R

            def plus(self, d):
                return Tile(self.t, self.c + d)

            def exists(self):
                return not isinstance(self.n, int) or 0 <= self.n < NTILE

        TURNS = NTILE // R

        def loop(eng, body):
            for u in range(-2, R):
                body(Tile(0, u))
            with eng.Fori(1, TURNS - 2) as t:
                for c in range(R):
                    body(Tile(t, c))
            for u in range((TURNS - 2) * R, NTILE + 1):
                body(Tile(0, u))

        @block.gpsimd
        def _(pool):
            for z in range(R):
                pool.memset(wd[z][64:FPAD, :, :], 0.0).then_inc(pads_set, 1)
            pool.wait_ge(pads_set, R)
            pool.memset(hid[:, FE:2 * FPAD], 0.0).then_inc(pads_set, 1)

        @block.sync
        def _(sp):
            sp.wait_ge(pads_set, R + 1)

            def load(u, first):
                z, next_group = u.slot, u.plus(1)
                last = u.n - R + 1 if isinstance(u.n, int) else sp.snap(u.n - R + 1)
                e = sp.value_load(cells[z // G][0:1, z % G:z % G + 1], min_val=0, max_val=NE - 1)
                if not first:
                    sp.wait_ge(gu_done, last)
                sp.dma_start(wgu[z][:, :, :], w1[bass.ds(e, 1)].rearrange("o (p k) f -> p (o k) f", k=KD))\
                    .then_inc(wgu_loaded[z], 16)
                if not first:
                    sp.wait_ge(y_done, last)
                if z % G == G - 1 and next_group.exists():
                    sp.wait_ge(cells_loaded[next_group.slot // G], 16 * (next_group.turn + 1))
                sp.dma_start(wd[z][0:FEP, :, :], w2[bass.ds(e, 1)].rearrange("o (p k) d -> p (o k) d", k=2))\
                    .then_inc(wd_loaded[z], 16)

            def load_cells(u):
                sp.dma_start(cells[u.slot // G][:, :], expert_dram[bass.ds(u.n, G)].unsqueeze(0))\
                    .then_inc(cells_loaded[u.slot // G], 16)

            def step(u, first, more=True):
                load(u, first)
                if u.slot % G == G - 1 and more:
                    load_cells(u.plus(R - G + 1))

            for u in range(0, R, G):
                load_cells(Tile(0, u))
            sp.wait_ge(cells_loaded[0], 16)
            for u in range(R):
                step(Tile(0, u), True)
            with sp.Fori(0, TURNS - 2) as t:
                for c in range(R, 2 * R):
                    step(Tile(t, c), False)
            for u in range((TURNS - 1) * R, NTILE):
                step(Tile(0, u), False, u + R - G + 1 < NTILE)

        @block.tensor
        def _(pe):
            def turn_x(u):
                if not u.exists():
                    return
                pe.wait_ge(xt_ready, u.n)
                pe.wait_ge(x_loaded[u.slot], 16 * (u.turn + 1))
                for k in range(KD):
                    ins = pe.transpose(ps_x[:, k * P:(k + 1) * P], x[u.slot][:, k::KD], ident[:, :])
                ins.then_inc(x_turned, 1)

            def gate_up(u):
                if not u.exists():
                    return
                pe.wait_ge(wgu_loaded[u.slot], 16 * (u.turn + 1))
                pe.wait_ge(xt_ready, u.n + 1)
                if u.plus(-G).exists():
                    pe.wait_ge(gated, u.n - G + 1)
                for k in range(KD):
                    ins = pe.matmul(ps_gu[:, u.bank, 0:2 * FE], xt[:, u.bank, k, :], wgu[u.slot][:, k, :],
                                    start=k == 0, stop=k == KD - 1)
                ins.then_inc(gu_done, 1)

            def turn_h(u):
                if not u.exists():
                    return
                pe.wait_ge(gated, u.n + 1)
                pe.wait_ge(ht_ready, u.n)
                for k in range(2):
                    ins = pe.transpose(ps_h[0:FPAD, k * P:(k + 1) * P], hid[:, k::2], ident[:, :])
                ins.then_inc(h_turned, 1)

            def down(u):
                if not u.exists():
                    return
                pe.wait_ge(wd_loaded[u.slot], 16 * (u.turn + 1))
                pe.wait_ge(ht_ready, u.n + 1)
                if u.plus(-G).exists():
                    pe.wait_ge(y_copied, u.n - G + 1)
                for k in range(2):
                    ins = pe.matmul(ps_y[:, u.bank, 0:D], ht[u.c % 2][:, k, :], wd[u.slot][:, k, :], start=k == 0, stop=k == 1)
                ins.then_inc(y_done, 1)

            pe.wait_ge(pads_set, R + 1)

            def body(u):
                gate_up(u.plus(1))
                turn_h(u)
                turn_x(u.plus(2))
                down(u.plus(-1))

            loop(pe, body)

        @block.scalar
        def _(act):
            def copy_x(u):
                if not u.exists():
                    return
                act.wait_ge(x_turned, u.n + 1)
                if u.plus(-G).exists():
                    act.wait_ge(gu_done, u.n - G + 1)
                act.activation(xt[:, u.bank, :, :], ps_x[:, 0:KD * P].rearrange("p (k t) -> p k t", k=KD), ACT.Copy)\
                    .then_inc(xt_ready, 1)

            def gate(u):
                if not u.exists():
                    return
                act.wait_ge(gu_done, u.n + 1)
                act.wait_ge(gated, u.n)
                act.activation(gs[:, :], ps_gu[:, u.bank, 0:FE], ACT.Silu).then_inc(acted, 1)

            def store(u):
                if not u.exists():
                    return
                act.wait_ge(y_copied, u.n + 1)
                act.dma_start(out_dram[bass.ds(u.n * P, P), :], y[u.slot][:, :]).then_inc(y_stored[u.slot], 16)

            def load_x(u):
                if u.exists():
                    act.dma_start(x[u.slot][:, :], sorted_dram[bass.ds(u.n * P, P), :]).then_inc(x_loaded[u.slot], 16)

            for u in range(R):
                load_x(Tile(0, u))

            def body(u):
                copy_x(u.plus(2))
                gate(u.plus(1))
                if u.plus(2).exists():
                    load_x(u.plus(2 + R))
                store(u.plus(-2))

            loop(act, body)
            for u in (NTILE - 1,):
                store(Tile(0, u))
            for z in range(R):
                act.wait_ge(y_stored[z], 16 * ((NTILE - 1 - z) // R + 1))

        @block.vector
        def _(dve):
            def mul(u):
                if not u.exists():
                    return
                dve.wait_ge(acted, u.n + 1)
                dve.wait_ge(h_turned, u.n)
                dve.tensor_tensor(hid[:, 0:FE], gs[:, :], ps_gu[:, u.bank, FE:2 * FE], ALU.mult).then_inc(gated, 1)

            def copy_h(u):
                if not u.exists():
                    return
                dve.wait_ge(h_turned, u.n + 1)
                if u.plus(-2).exists():
                    dve.wait_ge(y_done, u.n - 1)
                dve.tensor_copy(ht[u.c % 2][:, :, :], ps_h[0:FPAD, 0:2 * P].rearrange("p (k t) -> p k t", k=2))\
                    .then_inc(ht_ready, 1)

            def copy_y(u):
                if not u.exists():
                    return
                if u.plus(-R).exists():
                    dve.wait_ge(y_stored[u.slot], 16 * u.turn)
                dve.wait_ge(y_done, u.n + 1)
                dve.tensor_copy(y[u.slot][:, :], ps_y[:, u.bank, 0:D]).then_inc(y_copied, 1)

            def body(u):
                copy_h(u)
                mul(u.plus(1))
                copy_y(u.plus(-1))

            dve.wait_ge(pads_set, R + 1)
            loop(dve, body)


def gather_add(nc, tag, x_sb, weights, slots, out_dram, y_dram):
    R = 6
    with ExitStack() as ctx:
        s = Scope(nc, ctx, tag)
        got = [s.sbuf(f"got{z}", [P, D]) for z in range(R)]
        gathered = [s.sem(f"gathered{z}") for z in range(R)]
        added = s.sem("added")
        stored = s.sem("stored")
        block = ctx.enter_context(nc.Block())

        @block.gpsimd
        def _(pool):
            for i in range(NTT):
                for k in range(TOP):
                    n = i * TOP + k
                    if n >= R:
                        pool.wait_ge(added, n - R + 1)
                    pool.indirect_dma_start(out=got[n % R][:, :], out_offset=None, in_=out_dram[:, :],
                                            in_offset=bass.IndirectOffsetOnAxis(ap=slots[:, k, i:i + 1], axis=0))\
                        .then_inc(gathered[n % R], 16)

        @block.vector
        def _(dve):
            for i in range(NTT):
                for k in range(TOP):
                    n = i * TOP + k
                    dve.wait_ge(gathered[n % R], 16 * (n // R + 1))
                    if n:
                        dve.wait_ge(added, n)
                    dve.scalar_tensor_tensor(out=x_sb[:, i, :], in0=got[n % R][:, :], scalar=weights[:, i, k:k + 1],
                                             in1=x_sb[:, i, :], op0=ALU.mult, op1=ALU.add).then_inc(added, 1)

        @block.sync
        def _(sp):
            for c in range(NCH):
                sp.wait_ge(added, (c + 1) * CT * TOP)
                sp.dma_start(y_dram[c].rearrange("(i p) d -> p i d", p=P), x_sb[:, c * CT:(c + 1) * CT, :])\
                    .then_inc(stored, 16)
            sp.wait_ge(stored, 16 * NCH)


def moe(nc, ctx, x_sb, ident, gate_w, w1, w2, ws_gate_up, ws_down, sorted_dram, y_dram):
    FS = ws_down.shape[0]
    sizes = [P, P, FS - 2 * P]
    s = Scope(nc, ctx, "moe")
    xn_all = s.sbuf("xn_all", [P, NTT, D])
    weights = s.sbuf("weights", [P, NTT, TOP])
    slots = s.sbuf("slots", [P, TOP, NTT], U32)
    sgu = s.sbuf("sgu", [P, KD, 2 * FS])
    sd = s.sbuf("sd", [P, len(sizes), D])
    scattered = s.sem("scattered")
    expert_dram = nc.dram_tensor("tile_expert", [2 * P], I32, kind="Internal").ap()
    out_dram = nc.dram_tensor("y_sorted", [NSLOT, D], F32, kind="Internal").ap()

    def load_shared(sp, loaded):
        sp.dma_start(sgu[:, :, :], ws_gate_up.rearrange("(p k) f -> p k f", k=KD)).then_inc(loaded, 16)
        for m, r in enumerate(sizes):
            sp.dma_start(sd[0:r, m, :], ws_down[m * P:m * P + r, :]).then_inc(loaded, 16)
        return 16 * (1 + len(sizes))

    route(nc, "route", x_sb, ident, gate_w, xn_all, weights, slots, expert_dram, load_shared)
    mlp(nc, "shared", x_sb, ident, sgu[:, :, 0:FS], sgu[:, :, FS:2 * FS], lambda m: sd[0:sizes[m], m, :], sizes, ACT.Silu,
        xn_all=xn_all, on_gpsimd=scatter_program(xn_all, slots, sorted_dram, scattered))
    experts(nc, "experts", ident, w1, w2, expert_dram, sorted_dram, out_dram)
    gather_add(nc, "combine", x_sb, weights, slots, out_dram, y_dram)


MLP = 2048
BLOCK = 32
SCALE_1 = 0.5


def program(nc, a, y):
    with ExitStack() as ctx:
        s = Scope(nc, ctx, "all")
        x_sb = s.sbuf("x", [P, NTT, D])
        ident = s.sbuf("ident", [P, P])
        ident_bf = s.sbuf("ident_bf", [P, P], BF16)
        mask_q = s.sbuf("mask_q", [P, P], BF16)
        mask_k = s.sbuf("mask_k", [P, P], BF16)
        q_dram = nc.dram_tensor("q_parts", [2, D, T], F32, kind="Internal").ap()
        k_dram = nc.dram_tensor("k_parts", [2, D, T], F32, kind="Internal").ap()
        att_dram = nc.dram_tensor("att", [T, D], F32, kind="Internal").ap()
        first_sem = nc.free_semaphores[0]
        sorted_dram = nc.dram_tensor("x_sorted", [NSLOT, D], F32, kind="Internal").ap()
        make_constants(nc, a["L0_attn_X"], x_sb, ident, ident_bf, mask_q, mask_k)

        for layer, heads, pitch, causal, parts in ((0, 16, 32, True, PARTS_16), (1, 4, 66, False, PARTS_64)):
            w = {n: a[f"L{layer}_attn_{n}"] for n in ("Wq", "bq", "Wk", "bk", "Wv", "bv", "Wo", "bo")}
            affine = (a["L0_attn_ln_g"], a["L0_attn_ln_b"]) if layer == 0 else None
            v_dram = nc.dram_tensor(f"v{layer}", [T, heads * pitch], F32, kind="Internal").ap()
            scale = (D // heads) ** -0.5 if layer == 0 else SCALE_1
            project_qkv(nc, f"qkv{layer}", x_sb, ident, w, affine, q_dram, k_dram, v_dram, heads, pitch)
            attention(nc, f"att{layer}", ident, ident_bf, mask_q, mask_k, q_dram, k_dram, v_dram, att_dram,
                      heads, pitch, causal, parts, scale)
            project_out(nc, f"out{layer}", x_sb, ident, w["Wo"], w["bo"], att_dram)
            if layer == 0:
                with ExitStack() as mlp_ctx:
                    m = Scope(nc, mlp_ctx, "mlp_w")
                    wg, wu, wd = (m.sbuf(n, [P, 2, MLP]) for n in ("gate", "up", "down"))
                    fill = zero_fill(m, sorted_dram)
                    unpack_weights(nc, "unpack", a["codes"], a["scales"], [wg, wu, wd], MLP)
                    mlp(nc, "mlp", x_sb, ident, wg, wu, lambda i: wd[:, i % 2, i // 2 * D:(i // 2 + 1) * D],
                        [P] * (MLP // P), ACT.Gelu_apprx_tanh, on_sync=fill[0], on_gpsimd=fill[1])
                nc.all_engine_barrier(sems_to_clear=range(first_sem, nc.free_semaphores[0]))
        moe(nc, ctx, x_sb, ident, a["L1_ffn_gate_w"], a["L1_ffn_w_gate_up"], a["L1_ffn_w_down"],
            a["L1_ffn_ws_gate_up"], a["L1_ffn_ws_down"], sorted_dram, y)


def by_parity(m):
    r = m.shape[0]
    return m.reshape(r, MLP // D, P, 2).transpose(0, 1, 3, 2).reshape(r, MLP)


def kernel(**inputs):
    import concourse.bacc as bacc
    from concourse.bass_utils import run_bass_kernel_spmd

    inp = {n: np.asarray(v) for n, v in inputs.items()}
    arrays = {}
    for n in ("L0_attn_X", "L0_attn_ln_g", "L0_attn_ln_b"):
        arrays[n] = inp[n]
    for layer in (0, 1):
        for n in ("Wq", "Wk", "Wv", "Wo", "bv", "bo"):
            arrays[f"L{layer}_attn_{n}"] = inp[f"L{layer}_attn_{n}"]
        for n in ("bq", "bk"):
            arrays[f"L{layer}_attn_{n}"] = inp[f"L{layer}_attn_{n}"].reshape(KD, P).T
    g, u, d = (inp[f"L0_ffn_{n}_W_packed"] for n in ("gate", "up", "down"))
    gs, us, ds = (inp[f"L0_ffn_{n}_scales"] for n in ("gate", "up", "down"))
    nt = MLP // D
    arrays["codes"] = np.stack([by_parity(g.T), by_parity(u.T),
                                d.T.reshape(nt, P, D).transpose(1, 0, 2).reshape(P, MLP)])
    arrays["scales"] = np.stack([by_parity(gs.T), by_parity(us.T),
                                 ds.T.reshape(nt, D // BLOCK, D).transpose(1, 0, 2).reshape(D // BLOCK, MLP)])
    arrays["L1_ffn_gate_w"] = inp["L1_ffn_gate_w"].T
    arrays["L1_ffn_w_gate_up"] = inp["L1_ffn_w_gate_up"].transpose(0, 2, 1)
    arrays["L1_ffn_w_down"] = inp["L1_ffn_w_down"].transpose(0, 2, 1)
    arrays["L1_ffn_ws_gate_up"] = inp["L1_ffn_ws_gate_up"].T
    arrays["L1_ffn_ws_down"] = inp["L1_ffn_ws_down"].T
    arrays = {n: np.ascontiguousarray(v) for n, v in arrays.items()}

    nc = bacc.Bacc("TRN2", target_bir_lowering=False, num_devices=1)
    aps = {n: nc.dram_tensor(n, v.shape, mybir.dt.from_np(v.dtype), kind="ExternalInput").ap()
           for n, v in arrays.items()}
    y = nc.dram_tensor("y", inp["L0_attn_X"].shape, F32, kind="ExternalOutput").ap()
    program(nc, aps, y)
    result = run_bass_kernel_spmd(nc, [arrays], core_ids=[0])
    return result.results[0]["y"]
```

```python
from contextlib import ExitStack

import numpy as np

import concourse.bass as bass
from concourse import mybir

F32 = mybir.dt.float32
F32R = mybir.dt.float32r
BF16 = mybir.dt.bfloat16
I32 = mybir.dt.int32
U32 = mybir.dt.uint32
ALU = mybir.AluOpType
ACT = mybir.ActivationFunctionType
AX_X = mybir.AxisListType.X

P = 128
D = 256
T = 2048
S = 512
B = T // S
CT = 4
CHUNK = CT * P
NCH = T // CHUNK
KD = D // P
NTT = T // P
LN_EPS = 1e-5
NEG = -1e30


class Scope:

    def __init__(self, nc, ctx, tag):
        self.nc, self.ctx, self.tag = nc, ctx, tag

    def sbuf(self, name, shape, dt=F32):
        return self.ctx.enter_context(self.nc.sbuf_tensor(f"{self.tag}_{name}", shape, dt))

    def psum(self, name, shape, dt=F32):
        return self.ctx.enter_context(self.nc.psum_tensor(f"{self.tag}_{name}", shape, dt))

    def sem(self, name):
        return self.ctx.enter_context(self.nc.semaphore(f"{self.tag}_{name}"))


def make_constants(nc, x_dram, x_sb, ident, ident_bf, mask_q, mask_k):
    with ExitStack() as ctx:
        s = Scope(nc, ctx, "const")
        x_loaded, filled, shaped = s.sem("x_loaded"), s.sem("filled"), s.sem("shaped")
        block = ctx.enter_context(nc.Block())

        @block.sync
        def _(sp):
            for c in range(NCH):
                sp.dma_start(x_sb[:, c * CT:(c + 1) * CT, :],
                             x_dram[c].rearrange("(i p) d -> p i d", p=P)).then_inc(x_loaded, 16)
            sp.wait_ge(x_loaded, 16 * NCH)

        @block.gpsimd
        def _(pool):
            for t in (ident, ident_bf, mask_q, mask_k):
                pool.memset(t[:, :], 0.0).then_inc(filled, 1)
            pool.wait_ge(filled, 4)
            for t in (ident, ident_bf):
                pool.affine_select(out=t[:, :], in_=t[:, :], compare_op=ALU.not_equal, fill=1.0, base=0,
                                   pattern=[[-1, P]], channel_multiplier=1).then_inc(shaped, 1)
            pool.affine_select(out=mask_q[:, :], in_=mask_q[:, :], compare_op=ALU.is_ge, fill=NEG, base=0,
                               pattern=[[-1, P]], channel_multiplier=1).then_inc(shaped, 1)
            pool.affine_select(out=mask_k[:, :], in_=mask_k[:, :], compare_op=ALU.is_ge, fill=NEG, base=0,
                               pattern=[[1, P]], channel_multiplier=-1).then_inc(shaped, 1)
            pool.wait_ge(shaped, 4)


def wait(eng, sem, n):
    if not isinstance(n, int) or n > 0:
        eng.wait_ge(sem, n)


def chunks(eng, body):
    body(0, True)
    with eng.Fori(1, NCH - 1) as c:
        body(c, True)
    body(NCH - 1, False)


class NormStats:

    def __init__(self, s, n=CT, tag=""):
        self.n = n
        self.stats = s.sbuf(f"stats{tag}", [P, n, 6])
        self.mv = s.sbuf(f"mv{tag}", [P, n, 2])
        self.var = s.sbuf(f"var{tag}", [P, n])
        self.inv = s.sbuf(f"inv{tag}", [P, n])
        self.root = s.sbuf(f"root{tag}", [P, n])
        self.tmp = s.sbuf(f"tmp{tag}", [P, n])
        self.rstd = s.sbuf(f"rstd{tag}", [P, n])
        self.inv_done = s.sem(f"inv_done{tag}")
        self.root_done = s.sem(f"root_done{tag}")

    def mean(self, i):
        return self.mv[:, i, 0:1]

    def on_vector(self, dve, tile, turn=0):
        for i in range(self.n):
            dve.bn_stats(self.stats[:, i, :], tile(i))
        dve.drain()
        for i in range(self.n):
            dve.bn_aggr(self.mv[:, i, :], self.stats[:, i, :])
        dve.drain()
        dve.tensor_scalar(self.var[:, :], self.mv[:, :, 1], LN_EPS, None, ALU.add)
        dve.drain()
        dve.reciprocal(self.inv[:, :], self.var[:, :]).then_inc(self.inv_done, 1)
        dve.wait_ge(self.root_done, turn + 1)
        dve.tensor_tensor(self.tmp[:, :], self.root[:, :], self.root[:, :], ALU.mult)
        dve.drain()
        dve.tensor_tensor(self.inv[:, :], self.tmp[:, :], self.var[:, :], ALU.mult)
        dve.drain()
        dve.tensor_scalar(self.tmp[:, :], self.inv[:, :], -0.5, 1.5, ALU.mult, ALU.add)
        dve.drain()
        dve.tensor_tensor(self.rstd[:, :], self.tmp[:, :], self.root[:, :], ALU.mult)
        dve.drain()

    def on_scalar(self, act, turn=0):
        act.wait_ge(self.inv_done, turn + 1)
        act.activation(self.root[:, :], self.inv[:, :], ACT.Sqrt).then_inc(self.root_done, 1)


def token_tile(x, n):
    return x[:, bass.ds(n, 1), :].rearrange("p o d -> p (o d)")


def project_qkv(nc, tag, x_sb, ident, w, affine, q_dram, k_dram, v_dram, heads, pitch):
    hd = D // heads
    with ExitStack() as ctx:
        s = Scope(nc, ctx, tag)
        ns = NormStats(s)
        ns2 = NormStats(s, tag="2") if affine else None
        wt = [s.sbuf(f"w{n}", [P, KD, D]) for n in "qkv"]
        bqk = s.sbuf("bqk", [P, 2, KD])
        bv = s.sbuf("bv", [P, D])
        xo = s.sbuf("xo", [P, CT, D]) if affine else None
        x1 = s.sbuf("x1", [P, CT, D]) if affine else None
        gb = s.sbuf("gb", [P, 2, D]) if affine else None
        xn = s.sbuf("xn", [P, CT, D])
        xt = s.sbuf("xt", [P, KD, CHUNK])
        hi = s.sbuf("hi", [P, 2, KD, CHUNK], F32R)
        lo = s.sbuf("lo", [P, 2, KD, CHUNK], F32R)
        vs = s.sbuf("vs", [P, CT, heads * pitch])
        v4 = vs[:, :, :].rearrange("p i (h c) -> p i h c", c=pitch)
        ps_t = s.psum("ps_t", [P, KD, CHUNK])
        ps_qk = s.psum("ps_qk", [P, 2 * KD, CHUNK])
        ps_v = s.psum("ps_v", [P, 2, 2, D])

        qk_weights_loaded = s.sem("qk_weights_loaded")
        v_weights_loaded = s.sem("v_weights_loaded")
        affine_loaded = s.sem("affine_loaded")
        v_columns_set = s.sem("v_columns_set")
        normed = s.sem("normed")
        transposed = s.sem("transposed")
        xt_ready = s.sem("xt_ready")
        qk_done = s.sem("qk_done")
        hi_done = s.sem("hi_done")
        lo_done = s.sem("lo_done")
        v_done = s.sem("v_done")
        v_written = s.sem("v_written")
        qk_stored = s.sem("qk_stored")
        v_stored = s.sem("v_stored")
        block = ctx.enter_context(nc.Block())
        NQ = 2 * KD

        @block.sync
        def _(sp):
            if affine:
                for j in range(2):
                    sp.dma_start(gb[:, j, :], affine[j].partition_broadcast(P)).then_inc(affine_loaded, 16)
            for t, a in zip(wt, (w["Wq"], w["Wk"])):
                sp.dma_start(t[:, :, :], a.rearrange("(k p) n -> p k n", p=P)).then_inc(qk_weights_loaded, 16)
            sp.dma_start(bqk[:, 0, :], w["bq"]).then_inc(qk_weights_loaded, 16)
            sp.dma_start(bqk[:, 1, :], w["bk"]).then_inc(qk_weights_loaded, 16)
            sp.dma_start(wt[2][:, :, :], w["Wv"].rearrange("(k p) n -> p k n", p=P)).then_inc(v_weights_loaded, 16)
            sp.dma_start(bv[:, :], w["bv"].partition_broadcast(P)).then_inc(v_weights_loaded, 16)

            def body(c, more):
                for j, dst in enumerate((q_dram, k_dram)):
                    sp.wait_ge(lo_done, c * NQ + (j + 1) * KD)
                    for part, t in enumerate((hi, lo)):
                        sp.dma_start(dst[part].rearrange("(k p) t -> p k t", p=P)[:, :, bass.ds(c * CHUNK, CHUNK)],
                                     t[:, j, :, :].bitcast(F32)).then_inc(qk_stored, 16)
                sp.wait_ge(v_written, c * 2 + 2)
                sp.dma_start(v_dram.rearrange("(i p) f -> p i f", p=P)[:, bass.ds(c * CT, CT), :],
                             vs[:, :, :]).then_inc(v_stored, 16)

            chunks(sp, body)
            sp.wait_ge(qk_stored, 16 * 4 * NCH)
            sp.wait_ge(v_stored, 16 * NCH)

        @block.gpsimd
        def _(pool):
            pool.memset(vs[:, :, :], 0.0).then_inc(v_columns_set, 1)
            pool.wait_ge(v_columns_set, 1)
            for i in range(CT):
                pool.memset(v4[:, i, :, hd:hd + 1], 1.0).then_inc(v_columns_set, 1)

        @block.vector
        def _(dve):
            def norm(c):
                ns.on_vector(dve, lambda i: token_tile(x_sb, c * CT + i), c)
                if affine:
                    for i in range(CT):
                        dve.tensor_scalar(xo[:, i, :], token_tile(x_sb, c * CT + i), ns.mean(i), ns.rstd[:, i:i + 1],
                                          ALU.subtract, ALU.mult)
                    dve.drain()
                    ns2.on_vector(dve, lambda i: xo[:, i, :], c)
                    wait(dve, affine_loaded, 32 if isinstance(c, int) and c == 0 else 0)
                    for i in range(CT):
                        dve.scalar_tensor_tensor(out=x1[:, i, :], in0=xo[:, i, :], scalar=ns2.mean(i), in1=gb[:, 0, :],
                                                 op0=ALU.subtract, op1=ALU.mult)
                    dve.drain()
                wait(dve, transposed, c)
                for i in range(CT):
                    if affine:
                        ins = dve.scalar_tensor_tensor(out=xn[:, i, :], in0=x1[:, i, :], scalar=ns2.rstd[:, i:i + 1],
                                                       in1=gb[:, 1, :], op0=ALU.mult, op1=ALU.add)
                    else:
                        ins = dve.tensor_scalar(xn[:, i, :], token_tile(x_sb, c * CT + i), ns.mean(i),
                                                ns.rstd[:, i:i + 1], ALU.subtract, ALU.mult)
                    ins.then_inc(normed, 1)

            def body(c, more):
                if more:
                    norm(c + 1)
                wait(dve, qk_stored, c * 64)
                for n in range(NQ):
                    j, m = n // KD, n % KD
                    dve.wait_ge(hi_done, c * NQ + n + 1)
                    dve.scalar_tensor_tensor(out=lo[:, j, m, :], in0=ps_qk[:, n, :], scalar=bqk[:, j, m:m + 1],
                                             in1=hi[:, j, m, :], op0=ALU.add, op1=ALU.subtract).then_inc(lo_done, 1)
                wait(dve, v_stored, c * 16)
                for b in range(2):
                    dve.wait_ge(v_done, c * 2 + b + 1)
                    dve.tensor_tensor(v4[:, 2 * b:2 * b + 2, :, 0:hd],
                                      ps_v[:, b, :, :].rearrange("p i (h c) -> p i h c", c=hd),
                                      bv[:, :].rearrange("p (h c) -> p h c", c=hd).unsqueeze(1)
                                      .to_broadcast([P, 2, heads, hd]), ALU.add).then_inc(v_written, 1)

            norm(0)
            dve.wait_ge(qk_weights_loaded, 16 * 4)
            dve.wait_ge(v_weights_loaded, 16 * 2)
            dve.wait_ge(v_columns_set, 1 + CT)
            chunks(dve, body)

        @block.scalar
        def _(act):
            def roots(c):
                ns.on_scalar(act, c)
                if affine:
                    ns2.on_scalar(act, c)

            def copy_xt(c):
                act.wait_ge(transposed, c + 1)
                wait(act, v_done, c * 2)
                act.activation(xt[:, :, :], ps_t[:, :, :], ACT.Copy).then_inc(xt_ready, 1)

            def body(c, more):
                if more:
                    roots(c + 1)
                wait(act, qk_stored, c * 64)
                for n in range(NQ):
                    j, m = n // KD, n % KD
                    act.wait_ge(qk_done, c * NQ + n + 1)
                    act.activation(hi[:, j, m, :], ps_qk[:, n, :], ACT.Identity,
                                   bias=bqk[:, j, m:m + 1]).then_inc(hi_done, 1)
                if more:
                    copy_xt(c + 1)

            roots(0)
            act.wait_ge(qk_weights_loaded, 16 * 4)
            copy_xt(0)
            chunks(act, body)

        @block.tensor
        def _(pe):
            def turn(c):
                pe.wait_ge(normed, (c + 1) * CT)
                wait(pe, xt_ready, c)
                for k in range(KD):
                    for i in range(CT):
                        ins = pe.transpose(ps_t[:, k, i * P:(i + 1) * P], xn[:, i, k * P:(k + 1) * P], ident[:, :])
                ins.then_inc(transposed, 1)

            def body(c, more):
                pe.wait_ge(xt_ready, c + 1)
                for n in range(NQ):
                    j, m = n // KD, n % KD
                    wait(pe, lo_done, (c - 1) * NQ + n + 1)
                    for k in range(KD):
                        ins = pe.matmul(ps_qk[:, n, :], wt[j][:, k, m * P:(m + 1) * P], xt[:, k, :],
                                        start=k == 0, stop=k == KD - 1)
                    ins.then_inc(qk_done, 1)
                for b in range(2):
                    wait(pe, v_written, (c - 1) * 2 + b + 1)
                    for i in range(2):
                        for k in range(KD):
                            ins = pe.matmul(ps_v[:, b, i, :], xt[:, k, (2 * b + i) * P:(2 * b + i + 1) * P],
                                            wt[2][:, k, :], start=k == 0, stop=k == KD - 1)
                    ins.then_inc(v_done, 1)
                if more:
                    turn(c + 1)

            turn(0)
            pe.wait_ge(qk_weights_loaded, 16 * 4)
            pe.wait_ge(v_weights_loaded, 16 * 2)
            chunks(pe, body)

UNITS = 16
UF = 64
SLOTS = 4
NEG_ROW = 96
S1_ORDER = (1, 2, 3, 0)


class Unit:

    def __init__(self, t, c):
        self.t, self.c = t, c
        self.n = t * SLOTS + c
        self.slot = c % SLOTS
        self.turn = t + c // SLOTS

    def plus(self, d):
        return Unit(self.t, self.c + d)

    def exists(self):
        return not isinstance(self.n, int) or 0 <= self.n < UNITS


def attention(nc, tag, ident, ident_bf, mask_q, mask_k, q_dram, k_dram, v_dram, att_dram,
              heads, pitch, causal, parts, scale):
    hu = heads * UF // D
    hd = D // heads
    nt = CT * hu
    nx = nt // 2
    rows = hu * pitch
    last_part = len(parts) - 1
    n_loads = sum(len(q) + len(k) for q, k in parts)
    with ExitStack() as ctx:
        s = Scope(nc, ctx, tag)
        qs = [[s.sbuf(f"qs{a}_{z}", [P, hu, S], F32R) for z in range(SLOTS)] for a in range(len(parts))]
        ks = [[s.sbuf(f"ks{a}_{z}", [P, hu, S], F32R) for z in range(SLOTS)] for a in range(len(parts))]
        vs = [s.sbuf(f"vs{z}", [P, CT, rows]) for z in range(SLOTS)]
        pt = s.sbuf("pt", [P, nt, S])
        mx = s.sbuf("mx", [P, hu, CT])
        neg = s.sbuf("neg", [P, 2, nt], F32R)
        neg_t = s.sbuf("neg_t", [2 * nt, P])
        osb = s.sbuf("osb", [rows, S])
        rsum = s.sbuf("rsum", [P, CT, hu, 1])
        att = s.sbuf("att", [P, CT, UF])
        ps_1 = s.psum("ps_1", [P, 2, S])
        ps_2 = s.psum("ps_2", [P, 2, 2, S])
        ps_o = s.psum("ps_o", [rows, S])
        ps_tr = s.psum("ps_tr", [P, S])

        q_zeroed = s.sem("q_zeroed")
        k_zeroed = s.sem("k_zeroed")
        k_stacks_set = s.sem("k_stacks_set")
        qk_loaded = [s.sem(f"qk_loaded{z}") for z in range(SLOTS)]
        v_loaded = [s.sem(f"v_loaded{z}") for z in range(SLOTS)]
        neg_loaded = [s.sem(f"neg_loaded{z}") for z in range(SLOTS)]
        s1_done = s.sem("s1_done")
        max_done = s.sem("max_done")
        neg_ready = s.sem("neg_ready")
        neg_turned = s.sem("neg_turned")
        neg_copied = s.sem("neg_copied")
        s2_done = s.sem("s2_done")
        exp_done = s.sem("exp_done")
        pv_done = s.sem("pv_done")
        o_copied = s.sem("o_copied")
        o_turned = s.sem("o_turned")
        normalized = s.sem("normalized")
        att_stored = s.sem("att_stored")
        block = ctx.enter_context(nc.Block())

        def loop(eng, body):
            for u in range(-1, SLOTS):
                body(Unit(0, u))
            with eng.Fori(1, UNITS // SLOTS - 1) as t:
                for c in range(SLOTS):
                    body(Unit(t, c))
            for u in range(UNITS - SLOTS, UNITS + 2):
                body(Unit(0, u))

        def off(j):
            return j * P if causal else 0

        def width(i):
            return (i + 1) * P if causal else S

        groups = []
        for i in S1_ORDER:
            g = S // max(width(i), S // hu)
            groups.append([range(h, min(h + g, hu)) for h in range(0, hu, g)])
        ng = sum(len(g) for g in groups)

        def group(step, n):
            return sum(len(g) for g in groups[:step]) + n

        def last_exp(j):
            return ((j + 1) * hu - 1) // 2 + 1

        @block.sync
        def _(sp):
            def load(u):
                z = u.slot
                if not u.plus(-SLOTS).exists():
                    sp.wait_ge(q_zeroed, z + 1)
                    sp.wait_ge(k_stacks_set, z + 1)
                b, g = u.n // 4, u.n % 4
                for a, both in enumerate(parts):
                    for dram, stack, blocks in ((q_dram, qs, both[0]), (k_dram, ks, both[1])):
                        for row, half in blocks:
                            src = dram[half][bass.ds(g * UF, UF), bass.ds(b * S, S)]
                            sp.dma_start(stack[a][z][row:row + hd, :, :].bitcast(F32),
                                         src.rearrange("(h d) t -> d h t", d=hd)).then_inc(qk_loaded[z], 16)

            def load_v(u):
                z = u.slot
                b, g = u.n // 4, u.n % 4
                src = v_dram[bass.ds(b * S, S), bass.ds(g * rows, rows)]
                sp.dma_start(vs[z][:, :, :], src.rearrange("(j p) f -> p j f", p=P)).then_inc(v_loaded[z], 16)

            def load_maxima(u):
                if not u.exists():
                    return
                sp.wait_ge(neg_copied, u.n + 1)
                for r in range(2):
                    sp.dma_start(qs[last_part][u.slot][NEG_ROW + r:NEG_ROW + r + 1, :, :].bitcast(F32),
                                 neg_t[r * nt:(r + 1) * nt, :]).then_inc(neg_loaded[u.slot], 16)

            def store_output(u):
                if not u.exists():
                    return
                b, g = u.n // 4, u.n % 4
                sp.wait_ge(normalized, u.n + 1)
                dst = att_dram[bass.ds(b * S, S), bass.ds(g * UF, UF)]
                sp.dma_start(dst.rearrange("(i p) f -> p i f", p=P), att[:, :, :]).then_inc(att_stored, 16)

            def body(u):
                w = u.plus(2)
                if w.exists():
                    if u.plus(-2).exists():
                        sp.wait_ge(s2_done, (u.n - 1) * nx)
                    load(w)
                    if u.plus(-2).exists():
                        sp.wait_ge(pv_done, (u.n - 1) * CT)
                    load_v(w)
                load_maxima(u)
                store_output(u.plus(-2))

            load(Unit(0, 0))
            load_v(Unit(0, 0))
            loop(sp, body)
            sp.wait_ge(att_stored, 16 * UNITS)

        @block.gpsimd
        def _(pool):
            for z in range(SLOTS):
                pool.memset(qs[last_part][z][64:P, :, :].bitcast(F32), 0.0).then_inc(q_zeroed, 1)
            pool.wait_ge(q_zeroed, SLOTS)

        @block.tensor
        def _(pe):
            def scores_q(u, step, part):
                if not u.exists():
                    return
                i = S1_ORDER[step]
                z = u.slot
                if step == 0 and part == 0:
                    pe.wait_ge(qk_loaded[z], (u.turn + 1) * 16 * n_loads)
                of_step = len(groups[step])
                for n in range((part * of_step + 1) // 2, ((part + 1) * of_step + 1) // 2):
                    g = group(step, n)
                    wait(pe, max_done, u.n * ng + g - 1)
                    bank = (u.c * ng + g) % 2
                    for a_h, h in enumerate(groups[step][n]):
                        out = ps_1[:, bank, a_h * width(i):(a_h + 1) * width(i)]
                        for a in range(len(parts)):
                            rows_a = NEG_ROW if a == last_part else P
                            ins = pe.matmul(out, qs[a][z][0:rows_a, h, i * P:(i + 1) * P],
                                            ks[a][z][0:rows_a, h, 0:width(i)],
                                            start=a == 0, stop=a == last_part and not causal)
                        if causal:
                            ins = pe.matmul(out[:, i * P:(i + 1) * P], ident_bf[:, :], mask_q[:, :],
                                            start=False, stop=True)
                    ins.then_inc(s1_done, 1)

            def scores_k(u, j, part):
                if not u.exists():
                    return
                z = u.slot
                if j == 0 and part == 0:
                    pe.wait_ge(neg_loaded[z], (u.turn + 1) * 32)
                for n in [n for n in range(nx) if 2 * n // hu == j][part:part + 1]:
                    wait(pe, exp_done, u.n * nx + n - 1)
                    for e in (2 * n, 2 * n + 1):
                        jj, h = e // hu, e % hu
                        out = ps_2[:, n % 2, e % 2, 0:S - off(jj)]
                        for a in range(len(parts)):
                            ins = pe.matmul(out, ks[a][z][:, h, jj * P:(jj + 1) * P], qs[a][z][:, h, off(jj):S],
                                            start=a == 0, stop=a == last_part and not causal)
                        if causal:
                            ins = pe.matmul(ps_2[:, n % 2, e % 2, 0:P], ident_bf[:, :], mask_k[:, :],
                                            start=False, stop=True)
                    ins.then_inc(s2_done, 1)

            def values(u, j):
                if not u.exists():
                    return
                z = u.slot
                if j == 0:
                    pe.wait_ge(v_loaded[z], (u.turn + 1) * 16)
                    wait(pe, o_copied, u.n)
                pe.wait_ge(exp_done, u.n * nx + last_exp(j))
                for h in range(hu):
                    ins = pe.matmul(ps_o[h * pitch:(h + 1) * pitch, off(j):S], vs[z][:, j, h * pitch:(h + 1) * pitch],
                                    pt[:, j * hu + h, 0:S - off(j)], start=j == 0, stop=j == CT - 1)
                ins.then_inc(pv_done, 1)

            def turn_output(u):
                if not u.exists():
                    return
                pe.wait_ge(o_copied, u.n + 1)
                wait(pe, normalized, u.n)
                w = u.plus(1)
                if w.exists():
                    pe.wait_ge(neg_copied, w.n + 1)
                for i in range(CT):
                    ins = pe.transpose(ps_tr[:, i * rows:(i + 1) * rows], osb[:, i * P:(i + 1) * P],
                                       ident[0:rows, 0:rows])
                ins.then_inc(o_turned, 1)

            def turn_maxima(u):
                if not u.exists():
                    return
                pe.wait_ge(neg_ready, u.n + 1)
                if u.plus(-2).exists():
                    pe.wait_ge(normalized, u.n - 1)
                pe.transpose(ps_tr[0:2 * nt, 0:P], neg[:, :, :].bitcast(F32).rearrange("p r n -> p (r n)"),
                             ident[:, :]).then_inc(neg_turned, 1)

            def quarter(u, step, w, j, between):
                scores_q(u, step, 0)
                scores_k(w, j, 0)
                for f in between:
                    f()
                scores_q(u, step, 1)
                scores_k(w, j, 1)

            def body(u):
                v, w = u.plus(-1), u.plus(1)
                quarter(u, 3, v, 0, [lambda: values(u.plus(-2), 3)])
                quarter(w, 0, v, 1, [lambda: values(v, 0), lambda: turn_output(u.plus(-2))])
                quarter(w, 1, v, 2, [lambda: turn_maxima(u), lambda: values(v, 1)])
                quarter(w, 2, v, 3, [lambda: values(v, 2)])

            loop(pe, body)

        @block.scalar
        def _(act):
            def exps(u, j, parts=(0, 1)):
                if not u.exists():
                    return
                for n in [n for n in range(nx) if 2 * n // hu == j][parts[0]:parts[-1] + 1]:
                    act.wait_ge(s2_done, u.n * nx + n + 1)
                    wait(act, pv_done, (u.n - 1) * CT + (2 * n + 1) // hu + 1)
                    w = S - off(j)
                    act.activation(pt[:, 2 * n:2 * n + 2, 0:w], ps_2[:, n % 2, :, 0:w], ACT.Exp,
                                   scale=scale).then_inc(exp_done, 1)

            def copy_output(u):
                if not u.exists():
                    return
                act.wait_ge(pv_done, (u.n + 1) * CT)
                wait(act, o_turned, u.n)
                act.activation(osb[:, :], ps_o[:, :], ACT.Copy).then_inc(o_copied, 1)

            def copy_maxima(u):
                if not u.exists():
                    return
                act.wait_ge(neg_turned, u.n + 1)
                w = u.plus(-1)
                if w.exists():
                    act.wait_ge(neg_loaded[w.slot], (w.turn + 1) * 32)
                act.activation(neg_t[:, :], ps_tr[0:2 * nt, 0:P], ACT.Copy).then_inc(neg_copied, 1)

            def body(u):
                exps(u.plus(-1), 0, (0,))
                copy_output(u.plus(-2))
                exps(u.plus(-1), 0, (1,))
                exps(u.plus(-1), 1)
                copy_maxima(u)
                exps(u.plus(-1), 2)
                exps(u.plus(-1), 3)

            loop(act, body)

        @block.vector
        def _(dve):
            def maxima(u, step):
                if not u.exists():
                    return
                i = S1_ORDER[step]
                for n, hs in enumerate(groups[step]):
                    g = group(step, n)
                    dve.wait_ge(s1_done, u.n * ng + g + 1)
                    dve.tensor_reduce(mx[:, hs[0]:hs[-1] + 1, i], ps_1[:, (u.c * ng + g) % 2, 0:len(hs) * width(i)]
                                      .rearrange("p (h w) -> p h w", h=len(hs)), AX_X, ALU.max).then_inc(max_done, 1)

            def split_maxima(u):
                if not u.exists():
                    return
                dve.drain()
                wait(dve, neg_turned, u.n)
                dve.tensor_scalar(neg[:, 0, :], mx[:, :, :].rearrange("p h i -> p (h i)"), -1.0, None, ALU.mult)
                dve.drain()
                dve.scalar_tensor_tensor(out=neg[:, 1, :], in0=mx[:, :, :].rearrange("p h i -> p (h i)"), scalar=-1.0, in1=neg[:, 0, :],
                                         op0=ALU.mult, op1=ALU.subtract).then_inc(neg_ready, 1)
                dve.drain()

            def normalize(u):
                if not u.exists():
                    return
                dve.wait_ge(o_turned, u.n + 1)
                wait(dve, att_stored, u.n * 16)
                out = ps_tr[:, 0:CT * rows].rearrange("p (i h c) -> p i h c", i=CT, c=pitch)
                dve.reciprocal(rsum[:, :, :, :], out[:, :, :, hd:hd + 1])
                dve.drain()
                dve.tensor_tensor(att[:, :, :].rearrange("p i (h c) -> p i h c", c=hd), out[:, :, :, 0:hd],
                                  rsum[:, :, :, :].to_broadcast([P, CT, hu, hd]), ALU.mult).then_inc(normalized, 1)

            def body(u):
                maxima(u, 3)
                split_maxima(u)
                maxima(u.plus(1), 0)
                normalize(u.plus(-2))
                maxima(u.plus(1), 1)
                maxima(u.plus(1), 2)

            for z in range(SLOTS):
                dve.memset(ks[last_part][z][64:P, :, :].bitcast(F32), 0.0).then_inc(k_zeroed, 1)
                dve.wait_ge(k_zeroed, z + 1)
                dve.memset(ks[last_part][z][NEG_ROW:NEG_ROW + 2, :, :].bitcast(F32), 1.0).then_inc(k_stacks_set, 1)
            loop(dve, body)


PARTS_16 = [(((0, 0), (16, 1), (32, 0), (48, 1)), ((0, 0), (16, 0), (32, 1), (48, 1)))]
PARTS_64 = [(((0, 0), (64, 1)), ((0, 0), (64, 0))), (((0, 0),), ((0, 1),))]

def project_out(nc, tag, x_sb, ident, wo, bo, att_dram, decoder=None, n_decoded=0):
    with ExitStack() as ctx:
        s = Scope(nc, ctx, tag)
        w = s.sbuf("w", [P, KD, D])
        b = s.sbuf("b", [P, D])
        at = [s.sbuf(f"at{z}", [P, CT, D]) for z in range(2)]
        att_t = [s.sbuf(f"att_t{z}", [P, KD, CHUNK]) for z in range(2)]
        ps_t = s.psum("ps_t", [P, 2, KD, CHUNK])
        ps_y = s.psum("ps_y", [P, CT, S])
        weights_loaded = s.sem("weights_loaded")
        loaded = [s.sem(f"loaded{z}") for z in range(2)]
        turned = s.sem("turned")
        copied = s.sem("copied")
        made = s.sem("made")
        biased = s.sem("biased")
        added = s.sem("added")
        block = ctx.enter_context(nc.Block())

        @block.sync
        def _(sp):
            def load(c):
                sp.dma_start(at[c % 2][:, :, :], att_dram[c * CHUNK:(c + 1) * CHUNK, :]
                             .rearrange("(i p) f -> p i f", p=P)).then_inc(loaded[c % 2], 16)

            load(0)
            sp.dma_start(b[:, :], bo.partition_broadcast(P)).then_inc(weights_loaded, 16)
            sp.dma_start(w[:, :, :], wo.rearrange("(k p) n -> p k n", p=P)).then_inc(weights_loaded, 16)
            load(1)
            for n in range(max(NCH - 2, n_decoded)):
                if n < n_decoded:
                    decoder.load(sp, n)
                if n < NCH - 2:
                    sp.wait_ge(turned, n + 1)
                    load(n + 2)

        @block.gpsimd
        def _(pool):
            pool.wait_ge(weights_loaded, 32)
            for i in range(NTT):
                pool.tensor_tensor(x_sb[:, i, :], x_sb[:, i, :], b[:, :], ALU.add).then_inc(biased, 1)
            for n in range(n_decoded):
                decoder.multiply(pool, n)

        @block.tensor
        def _(pe):
            def turn(c):
                pe.wait_ge(loaded[c % 2], 16 * (c // 2) + 16)
                wait(pe, copied, c - 1)
                for k in range(KD):
                    for i in range(CT):
                        ins = pe.transpose(ps_t[:, c % 2, k, i * P:(i + 1) * P], at[c % 2][:, i, k * P:(k + 1) * P],
                                           ident[:, :])
                ins.then_inc(turned, 1)

            turn(0)
            pe.wait_ge(weights_loaded, 32)
            for c in range(NCH):
                if c + 1 < NCH:
                    turn(c + 1)
                pe.wait_ge(copied, c + 1)
                for i in range(CT):
                    wait(pe, added, (c - 1) * CT + i + 1)
                    for k in range(KD):
                        ins = pe.matmul(ps_y[:, i, 0:D], att_t[c % 2][:, k, i * P:(i + 1) * P], w[:, k, :],
                                        start=k == 0, stop=k == KD - 1)
                    ins.then_inc(made, 1)

        @block.scalar
        def _(act):
            def copy(c):
                act.wait_ge(turned, c + 1)
                wait(act, made, (c - 1) * CT)
                act.activation(att_t[c % 2][:, :, :], ps_t[:, c % 2, :, :], ACT.Copy).then_inc(copied, 1)

            copy(0)
            for n in range(max(NCH - 1, n_decoded)):
                if n + 1 < NCH:
                    copy(n + 1)
                if n < n_decoded:
                    decoder.convert(act, n)

        @block.vector
        def _(dve):
            if decoder:
                decoder.set_table(dve)
            for c in range(NCH):
                if c < n_decoded:
                    decoder.look_up(dve, c)
                for i in range(CT):
                    dve.wait_ge(biased, c * CT + i + 1)
                    dve.wait_ge(made, c * CT + i + 1)
                    dve.tensor_tensor(x_sb[:, c * CT + i, :], x_sb[:, c * CT + i, :], ps_y[:, i, 0:D], ALU.add)\
                        .then_inc(added, 1)
            for n in range(NCH, n_decoded):
                decoder.look_up(dve, n)


def mlp(nc, tag, x_sb, ident, w_gate, w_up, w_down, sizes, func, xn_all=None, on_sync=None, on_gpsimd=None,
        decoder=None, n_decoded=0, first=None):
    nm = len(sizes)
    starts = [sum(sizes[:m]) for m in range(nm)]
    with ExitStack() as ctx:
        s = Scope(nc, ctx, tag)
        ns = NormStats(s) if xn_all is None else None
        xn = s.sbuf("xn", [P, CT, D])
        xt = s.sbuf("xt", [P, KD, CHUNK])
        gs = s.sbuf("gs", [P, 2, CHUNK])
        inner = s.sbuf("inner", [P, nm, CHUNK])
        ps_t = s.psum("ps_t", [P, KD, CHUNK])
        ps_g = s.psum("ps_g", [P, 2, CHUNK])
        ps_u = s.psum("ps_u", [P, 2, CHUNK])
        ps_y = s.psum("ps_y", [P, 2, S])
        normed = s.sem("normed")
        turned = s.sem("turned")
        xt_ready = s.sem("xt_ready")
        gate_done = s.sem("gate_done")
        up_done = s.sem("up_done")
        acted = s.sem("acted")
        gated = s.sem("gated")
        made = s.sem("made")
        added = s.sem("added")
        block = ctx.enter_context(nc.Block())

        def decoding(c, m):
            n = n_decoded + m // 2
            return n if decoder and isinstance(c, int) and c == 0 and m % 2 == 0 and n < decoder.n else None

        def await_decoded(c, n):
            if decoder and isinstance(c, int) and c == 0:
                return n
            return 0

        if on_sync:
            block.sync(on_sync)
        if on_gpsimd:
            block.gpsimd(on_gpsimd)

        @block.vector
        def _(dve):
            def norm(c):
                if ns:
                    ns.on_vector(dve, lambda i: token_tile(x_sb, c * CT + i), c)
                wait(dve, turned, c)
                for i in range(CT):
                    tile = bass.ds(c * CT + i, 1)
                    if xn_all is not None:
                        dve.tensor_scalar(xn[:, i:i + 1, :], xn_all[:, tile, :], 1.0, None, ALU.mult)\
                            .then_inc(normed, 1)
                        continue
                    dve.tensor_scalar(xn[:, i:i + 1, :], x_sb[:, tile, :], ns.mean(i), ns.rstd[:, i:i + 1],
                                      ALU.subtract, ALU.mult).then_inc(normed, 1)

            def body(c, more):
                for m in range(nm):
                    r = sizes[m]
                    n = decoding(c, m)
                    if n is not None:
                        decoder.look_up(dve, n)
                    dve.wait_ge(acted, c * nm + m + 1)
                    if m == 0:
                        wait(dve, made, c * CT)
                    dve.wait_ge(up_done, c * nm + m + 1)
                    dve.tensor_tensor(inner[0:r, m, :], gs[0:r, m % 2, :], ps_u[0:r, m % 2, :], ALU.mult)\
                        .then_inc(gated, 1)
                    if more and m == nm - 2:
                        norm(c + 1)
                for i in range(CT):
                    dve.wait_ge(made, c * CT + i + 1)
                    tile = x_sb[:, bass.ds(c * CT + i, 1), :]
                    dve.tensor_tensor(tile, tile, ps_y[:, i % 2, 0:D].unsqueeze(1), ALU.add).then_inc(added, 1)

            norm(0)
            chunks(dve, body)

        @block.scalar
        def _(act):
            def copy_xt(c):
                act.wait_ge(turned, c + 1)
                wait(act, up_done, c * nm)
                act.activation(xt[:, :, :], ps_t[:, :, :], ACT.Copy).then_inc(xt_ready, 1)

            def body(c, more):
                for m in range(nm):
                    r = sizes[m]
                    n = decoding(c, m)
                    if n is not None:
                        decoder.convert(act, n)
                    if ns and more and m == nm - 1:
                        ns.on_scalar(act, c + 1)
                    act.wait_ge(gate_done, c * nm + m + 1)
                    wait(act, gated, c * nm + m - 1)
                    act.activation(gs[0:r, m % 2, :], ps_g[0:r, m % 2, :], func).then_inc(acted, 1)
                if more:
                    copy_xt(c + 1)

            if ns:
                ns.on_scalar(act)
            copy_xt(0)
            chunks(act, body)

        @block.tensor
        def _(pe):
            def turn(c):
                pe.wait_ge(normed, c * CT + CT)
                wait(pe, xt_ready, c)
                for k in range(KD):
                    for i in range(CT):
                        ins = pe.transpose(ps_t[:, k, i * P:(i + 1) * P], xn[:, i, k::KD], ident[:, :])
                ins.then_inc(turned, 1)

            def body(c, more):
                pe.wait_ge(xt_ready, c + 1)
                for m in range(nm):
                    r = sizes[m]
                    cols = slice(starts[m], starts[m] + r)
                    wait(pe, decoder and decoder.decoded, await_decoded(c, first(m) if first else 0))
                    for w, ps, freed, done in ((w_gate, ps_g, acted, gate_done), (w_up, ps_u, gated, up_done)):
                        wait(pe, freed, c * nm + m - 1)
                        for k in range(KD):
                            ins = pe.matmul(ps[0:r, m % 2, :], w[:, k, cols], xt[:, k, :],
                                            start=k == 0, stop=k == KD - 1)
                        ins.then_inc(done, 1)
                if more:
                    turn(c + 1)
                wait(pe, decoder and decoder.decoded, await_decoded(c, decoder.n if decoder else 0))
                pe.wait_ge(gated, c * nm + nm)
                for i in range(CT):
                    wait(pe, added, c * CT + i - 1)
                    for m in range(nm):
                        r = sizes[m]
                        ins = pe.matmul(ps_y[:, i % 2, 0:D], inner[0:r, m, i * P:(i + 1) * P], w_down(m),
                                        start=m == 0, stop=m == nm - 1)
                    ins.then_inc(made, 1)

            turn(0)
            chunks(pe, body)


PIECE = 512
TABLE = 0xC8643210 - (1 << 32)


class Decoder:

    def __init__(self, s, codes, scales, out, order):
        self.codes, self.scales, self.out, self.order = codes, scales, out, order
        self.n = len(order)
        self.code = [s.sbuf(f"code{z}", [P, PIECE], I32) for z in range(2)]
        self.scale = [s.sbuf(f"scale{z}", [P, PIECE]) for z in range(2)]
        self.half = [s.sbuf(f"half{z}", [P, PIECE]) for z in range(2)]
        self.table = s.sbuf("table", [P, 1], I32)
        self.shift = s.sbuf("shift", [P, 2, PIECE], I32)
        self.found = s.sbuf("found", [P, 2, PIECE], I32)
        self.mag = [s.sbuf(f"mag{z}", [P, 2, PIECE], I32) for z in range(2)]
        self.magf = [s.sbuf(f"magf{z}", [P, 2, PIECE]) for z in range(2)]
        self.sign = s.sbuf("sign", [P, 2, PIECE], I32)
        self.signed = [s.sbuf(f"signed{z}", [P, 2, PIECE], I32) for z in range(2)]
        self.loaded = [s.sem(f"loaded{z}") for z in range(2)]
        self.halved = s.sem("halved")
        self.read = s.sem("read")
        self.converted = s.sem("converted")
        self.decoded = s.sem("decoded")

    def place(self, n):
        w, part = self.order[n]
        return w, slice(part * PIECE, (part + 1) * PIECE)

    def load(self, sp, n):
        z, (w, cols) = n % 2, self.place(n)
        wait(sp, self.read, n - 1)
        sp.dma_start(self.code[z][:, :], self.codes[w][:, cols]).then_inc(self.loaded[z], 16)
        sp.dma_start(self.scale[z][:, :], self.scales[w][:, cols].unsqueeze(1).to_broadcast([8, 16, PIECE]))\
            .then_inc(self.loaded[z], 16)

    def set_table(self, dve):
        dve.memset(self.table[:, :], TABLE)
        dve.drain()

    def look_up(self, dve, n):
        z = n % 2
        code, half, both = self.code[z], self.half[z], [P, 2, PIECE]
        dve.wait_ge(self.loaded[z], 32 * (n // 2 + 1))
        dve.tensor_scalar(self.shift[:, 0, :], code[:, :], 7, 2, ALU.bitwise_and, ALU.logical_shift_left)
        dve.tensor_scalar(self.shift[:, 1, :], code[:, :], 2, 28, ALU.logical_shift_right, ALU.bitwise_and)
        dve.tensor_scalar(self.sign[:, 0, :], code[:, :], 8, 28, ALU.bitwise_and, ALU.logical_shift_left)
        dve.tensor_scalar(self.sign[:, 1, :], code[:, :], 128, 24, ALU.bitwise_and, ALU.logical_shift_left)
        dve.drain()
        dve.tensor_tensor(self.found[:, :, :], self.table[:, :].unsqueeze(1).to_broadcast(both), self.shift[:, :, :],
                          ALU.logical_shift_right)
        dve.wait_ge(self.halved, n + 1)
        wait(dve, self.decoded, n - 1)
        dve.tensor_tensor(self.signed[z][:, :, :], self.sign[:, :, :],
                          half[:, :].bitcast(I32).unsqueeze(1).to_broadcast(both), ALU.bitwise_xor)
        dve.drain()
        dve.tensor_scalar(self.mag[z][:, :, :], self.found[:, :, :], 15, None, ALU.bitwise_and).then_inc(self.read, 1)

    def convert(self, act, n):
        z = n % 2
        act.wait_ge(self.loaded[z], 32 * (n // 2 + 1))
        wait(act, self.read, n - 1)
        act.mul(self.half[z][:, :], self.scale[z][:, :], 0.5).then_inc(self.halved, 1)
        act.wait_ge(self.read, n + 1)
        wait(act, self.decoded, n - 1)
        act.activation(self.magf[z][:, :, :], self.mag[z][:, :, :], ACT.Copy).then_inc(self.converted, 1)

    def multiply(self, pool, n):
        z, (w, cols) = n % 2, self.place(n)
        pool.wait_ge(self.converted, n + 1)
        pool.tensor_tensor(self.out[w][:, :, cols], self.magf[z][:, :, :], self.signed[z][:, :, :].bitcast(F32),
                           ALU.mult).then_inc(self.decoded, 1)

NE = 64
TOP = 6
FE = 176
FEP = FE // 2
FPAD = 96
NTILE = (T * TOP - NE) // P + NE
NSLOT = NTILE * P
TOP_EPS = 1e-20


def route(nc, tag, x_sb, ident, gate_w, xn_all, weights, slots, expert_dram, load_shared):
    with ExitStack() as ctx:
        s = Scope(nc, ctx, tag)
        ns = NormStats(s, NTT)
        gw = s.sbuf("gw", [P, KD, NE])
        xt = s.sbuf("xt", [P, 2, KD, P])
        logits = s.sbuf("logits", [P, NTT, NE])
        top = s.sbuf("top", [P, NTT, 8])
        row = s.sbuf("row", [P, NTT, 1])
        row2 = s.sbuf("row2", [P, NTT, 1])
        shifted = s.sbuf("shifted", [P, NTT, NE])
        exps = s.sbuf("exps", [P, NTT, NE])
        scores = s.sbuf("scores", [P, NTT, NE])
        idx = s.sbuf("idx", [P, NTT, 8], U32)
        idxf = s.sbuf("idxf", [P, NTT, 8])
        chosen = s.sbuf("chosen", [P, TOP, NTT, NE])
        mask = [s.sbuf(f"mask{z}", [P, NTT, NE]) for z in range(2)]
        mask_bf = s.sbuf("mask_bf", [P, NTT, NE], BF16)
        before = s.sbuf("before", [P, P], BF16)
        ones = s.sbuf("ones", [P, P], BF16)
        count = s.sbuf("count", [P, NE], I32)
        tiles_i = s.sbuf("tiles_i", [P, NE], I32)
        tiles = s.sbuf("tiles", [P, NE])
        incl = [s.sbuf(f"incl{z}", [P, NE]) for z in range(2)]
        start = s.sbuf("start", [P, NE])
        slot = s.sbuf("slot", [P, NTT, NE])
        picked = s.sbuf("picked", [P, TOP, NTT, NE])
        slot_f = s.sbuf("slot_f", [P, TOP, NTT, 1])
        iota_e = s.sbuf("iota_e", [P, NE])
        iota_t = s.sbuf("iota_t", [P, 2])
        passed = s.sbuf("passed", [P, 2, NE])
        owner = s.sbuf("owner", [P, 2, 1])
        owner_i = s.sbuf("owner_i", [P, 2], I32)
        ps_t = s.psum("ps_t", [P, 2, S])
        ps_l = s.psum("ps_l", [P, 2, S])
        ps_pos = s.psum("ps_pos", [P, 2, NTT // 2, NE])
        ps_n = s.psum("ps_n", [P, S])
        gw_loaded = s.sem("gw_loaded")
        shared_loaded = s.sem("shared_loaded")
        filled = s.sem("filled")
        shaped = s.sem("shaped")
        normed = s.sem("normed")
        turned = s.sem("turned")
        xt_ready = s.sem("xt_ready")
        logits_done = s.sem("logits_done")
        logits_copied = s.sem("logits_copied")
        shifted_done = s.sem("shifted_done")
        exps_done = s.sem("exps_done")
        mask_done = s.sem("mask_done")
        placed = s.sem("placed")
        owned = s.sem("owned")
        owner_stored = s.sem("owner_stored")
        block = ctx.enter_context(nc.Block())

        @block.sync
        def _(sp):
            sp.dma_start(gw[:, :, :], gate_w.rearrange("(p k) n -> p k n", k=KD)).then_inc(gw_loaded, 16)
            n = load_shared(sp, shared_loaded)
            sp.wait_ge(owned, 1)
            sp.dma_start(expert_dram.rearrange("(p j) -> p j", p=P), owner_i[:, :]).then_inc(owner_stored, 16)
            sp.wait_ge(owner_stored, 16)
            sp.wait_ge(shared_loaded, n)

        @block.gpsimd
        def _(pool):
            pool.memset(ones[:, :], 1.0).then_inc(filled, 1)
            pool.wait_ge(filled, 1)
            pool.affine_select(out=before[:, :], in_=ones[:, :], compare_op=ALU.is_gt, fill=0.0, base=0,
                               pattern=[[1, P]], channel_multiplier=-1).then_inc(shaped, 1)
            pool.iota(iota_e[:, :], pattern=[[1, NE]], base=0, channel_multiplier=0,
                      allow_small_or_imprecise_dtypes=True).then_inc(shaped, 1)
            pool.iota(iota_t[:, :], pattern=[[1, 2]], base=0, channel_multiplier=2,
                      allow_small_or_imprecise_dtypes=True).then_inc(shaped, 1)

        @block.scalar
        def _(act):
            ns.on_scalar(act)
            for i in range(NTT):
                act.wait_ge(turned, i + 1)
                if i >= 2:
                    act.wait_ge(logits_done, i - 1)
                act.activation(xt[:, i % 2, :, :], ps_t[:, i % 2, 0:KD * P].rearrange("p (k t) -> p k t", k=KD),
                               ACT.Copy).then_inc(xt_ready, 1)
            act.wait_ge(shifted_done, 1)
            act.activation(exps[:, :, :], shifted[:, :, :], ACT.Exp).then_inc(exps_done, 1)

        @block.tensor
        def _(pe):
            pe.wait_ge(gw_loaded, 16)

            def turn(i):
                pe.wait_ge(normed, i + 1)
                if i >= 2:
                    pe.wait_ge(xt_ready, i - 1)
                for k in range(KD):
                    ins = pe.transpose(ps_t[:, i % 2, k * P:(k + 1) * P], xn_all[:, i, k::KD], ident[:, :])
                ins.then_inc(turned, 1)

            turn(0)
            for i in range(NTT):
                if i + 1 < NTT:
                    turn(i + 1)
                pe.wait_ge(xt_ready, i + 1)
                if i >= 2:
                    pe.wait_ge(logits_copied, i - 1)
                for k in range(KD):
                    ins = pe.matmul(ps_l[:, i % 2, 0:NE], xt[:, i % 2, k, :], gw[:, k, :],
                                    start=k == 0, stop=k == KD - 1)
                ins.then_inc(logits_done, 1)
            pe.wait_ge(shaped, 3)
            pe.wait_ge(mask_done, 1)
            for i in range(NTT):
                out = ps_pos[:, i // (NTT // 2), i % (NTT // 2), :]
                for j in range(i):
                    pe.matmul(out, ones[:, :], mask_bf[:, j, :], start=j == 0, stop=False)
                pe.matmul(out, before[:, :], mask_bf[:, i, :], start=i == 0, stop=True)
            for j in range(NTT):
                ins = pe.matmul(ps_n[:, 0:NE], ones[:, :], mask_bf[:, j, :], start=j == 0, stop=j == NTT - 1)
            ins.then_inc(placed, 1)

        @block.vector
        def _(dve):
            ns.on_vector(dve, lambda i: x_sb[:, i, :])
            for i in range(NTT):
                dve.tensor_scalar(xn_all[:, i, :], x_sb[:, i, :], ns.mv[:, i, 0:1], ns.rstd[:, i:i + 1],
                                  ALU.subtract, ALU.mult).then_inc(normed, 1)
            for i in range(NTT):
                dve.wait_ge(logits_done, i + 1)
                dve.tensor_copy(logits[:, i, :], ps_l[:, i % 2, 0:NE]).then_inc(logits_copied, 1)
            dve.drain()
            full = [P, NTT, NE]
            dve.tensor_reduce(row[:, :, :], logits[:, :, :], AX_X, ALU.max)
            dve.drain()
            dve.tensor_tensor(shifted[:, :, :], logits[:, :, :], row[:, :, :].to_broadcast(full), ALU.subtract)\
                .then_inc(shifted_done, 1)
            dve.wait_ge(exps_done, 1)
            dve.tensor_reduce(row[:, :, :], exps[:, :, :], AX_X, ALU.add)
            dve.drain()
            dve.reciprocal(row2[:, :, :], row[:, :, :])
            dve.drain()
            dve.tensor_tensor(scores[:, :, :], exps[:, :, :], row2[:, :, :].to_broadcast(full), ALU.mult)
            dve.drain()
            for i in range(NTT):
                dve.max(top[:, i, :], scores[:, i, :])
            dve.drain()
            for i in range(NTT):
                dve.max_index(idx[:, i, :], top[:, i, :], scores[:, i, :])
            dve.tensor_reduce(row[:, :, :], top[:, :, 0:TOP], AX_X, ALU.add)
            dve.drain()
            dve.tensor_copy(idxf[:, :, :], idx[:, :, :])
            dve.tensor_scalar(row2[:, :, :], row[:, :, :], TOP_EPS, None, ALU.add)
            dve.drain()
            dve.reciprocal(row[:, :, :], row2[:, :, :])
            dve.wait_ge(shaped, 3)
            for k in range(TOP):
                dve.tensor_tensor(chosen[:, k, :, :], iota_e[:, :].unsqueeze(1).to_broadcast(full),
                                  idxf[:, :, k:k + 1].to_broadcast(full), ALU.is_equal)
            dve.drain()
            dve.tensor_tensor(weights[:, :, :], top[:, :, 0:TOP], row[:, :, :].to_broadcast([P, NTT, TOP]), ALU.mult)
            dve.tensor_tensor(mask[0][:, :, :], chosen[:, 0, :, :], chosen[:, 1, :, :], ALU.add)
            for k in range(2, TOP):
                dve.drain()
                out = mask[(k + 1) % 2] if k < TOP - 1 else mask_bf
                ins = dve.tensor_tensor(out[:, :, :], mask[k % 2][:, :, :], chosen[:, k, :, :], ALU.add)
            ins.then_inc(mask_done, 1)
            dve.wait_ge(placed, 1)
            dve.tensor_scalar(count[:, :], ps_n[:, 0:NE], float(P - 1), None, ALU.add)
            dve.drain()
            dve.tensor_scalar(tiles_i[:, :], count[:, :], P.bit_length() - 1, None, ALU.logical_shift_right)
            dve.drain()
            dve.tensor_copy(tiles[:, :], tiles_i[:, :])
            dve.drain()
            dve.tensor_copy(incl[0][:, :], tiles[:, :])
            z, d = 0, 1
            while d < NE:
                dve.drain()
                dve.tensor_copy(incl[1 - z][:, 0:d], incl[z][:, 0:d])
                dve.tensor_tensor(incl[1 - z][:, d:NE], incl[z][:, d:NE], incl[z][:, 0:NE - d], ALU.add)
                z, d = 1 - z, 2 * d
            dve.drain()
            last = incl[z]
            dve.tensor_tensor(incl[1 - z][:, :], last[:, :], tiles[:, :], ALU.subtract)
            dve.tensor_tensor(passed[:, :, :], last[:, :].unsqueeze(1).to_broadcast([P, 2, NE]),
                              iota_t[:, :].unsqueeze(2).to_broadcast([P, 2, NE]), ALU.is_le)
            dve.drain()
            dve.tensor_scalar(start[:, :], incl[1 - z][:, :], float(P), None, ALU.mult)
            dve.tensor_reduce(owner[:, :, :], passed[:, :, :], AX_X, ALU.add)
            dve.drain()
            dve.tensor_scalar(owner_i[:, :], owner[:, :, 0], float(NE - 1), None, ALU.min).then_inc(owned, 1)
            half = NTT // 2
            for b in range(2):
                dve.tensor_tensor(slot[:, b * half:(b + 1) * half, :], ps_pos[:, b, :, :],
                                  start[:, :].unsqueeze(1).to_broadcast([P, half, NE]), ALU.add)
            dve.drain()
            for k in range(TOP):
                dve.tensor_tensor(picked[:, k, :, :], chosen[:, k, :, :], slot[:, :, :], ALU.mult)
            dve.drain()
            dve.tensor_reduce(slot_f[:, :, :, :], picked[:, :, :, :], AX_X, ALU.add)
            dve.drain()
            dve.tensor_copy(slots[:, :, :], slot_f[:, :, :, 0])


ZERO = 2048


class ZeroFill:

    def __init__(self, s, dram):
        self.zero = s.sbuf("zero", [P, ZERO])
        self.zero_set, self.zeroed = s.sem("zero_set"), s.sem("zeroed")
        self.flat = dram.rearrange("(p r) d -> p (r d)", p=P)

    def set(self, pool):
        pool.memset(self.zero[:, :], 0.0).then_inc(self.zero_set, 1)

    def store(self, sp):
        sp.wait_ge(self.zero_set, 1)
        size = self.flat.shape[1]
        starts = range(0, size, ZERO)
        for a in starts:
            n = min(ZERO, size - a)
            sp.dma_start(self.flat[:, a:a + n], self.zero[:, 0:n]).then_inc(self.zeroed, 16)
        sp.wait_ge(self.zeroed, 16 * len(starts))


def scatter_program(xn_all, slots, sorted_dram, scattered):
    def on_gpsimd(pool):
        for i in range(NTT):
            for k in range(TOP):
                pool.indirect_dma_start(out=sorted_dram[:, :],
                                        out_offset=bass.IndirectOffsetOnAxis(ap=slots[:, k, i:i + 1], axis=0),
                                        in_=xn_all[:, i, :], in_offset=None).then_inc(scattered, 16)
        pool.wait_ge(scattered, 16 * TOP * NTT)
    return on_gpsimd


def experts(nc, tag, ident, w1, w2, expert_dram, sorted_dram, out_dram):
    R = 6
    G = 3
    with ExitStack() as ctx:
        s = Scope(nc, ctx, tag)
        cells = [s.sbuf(f"cells{z}", [1, G], I32) for z in range(R // G)]
        x = [s.sbuf(f"x{z}", [P, D]) for z in range(R)]
        wgu = [s.sbuf(f"wgu{z}", [P, KD, 2 * FE]) for z in range(R)]
        wd = [s.sbuf(f"wd{z}", [FPAD, 2, D]) for z in range(R)]
        xt = s.sbuf("xt", [P, G, KD, P])
        gs = s.sbuf("gs", [P, FE])
        hid = s.sbuf("hid", [P, 2 * FPAD])
        ht = [s.sbuf(f"ht{z}", [FPAD, 2, P]) for z in range(2)]
        y = [s.sbuf(f"y{z}", [P, D]) for z in range(R)]
        ps_x = s.psum("ps_x", [P, S])
        ps_gu = s.psum("ps_gu", [P, G, S])
        ps_h = s.psum("ps_h", [P, S])
        ps_y = s.psum("ps_y", [P, G, S])
        pads_set = s.sem("pads_set")
        cells_loaded = [s.sem(f"cells_loaded{z}") for z in range(R // G)]
        x_loaded = [s.sem(f"x_loaded{z}") for z in range(R)]
        wgu_loaded = [s.sem(f"wgu_loaded{z}") for z in range(R)]
        wd_loaded = [s.sem(f"wd_loaded{z}") for z in range(R)]
        x_turned = s.sem("x_turned")
        xt_ready = s.sem("xt_ready")
        gu_done = s.sem("gu_done")
        acted = s.sem("acted")
        gated = s.sem("gated")
        h_turned = s.sem("h_turned")
        ht_ready = s.sem("ht_ready")
        y_done = s.sem("y_done")
        y_copied = s.sem("y_copied")
        y_stored = [s.sem(f"y_stored{z}") for z in range(R)]
        block = ctx.enter_context(nc.Block())

        class Tile:

            def __init__(self, t, c):
                self.t, self.c = t, c
                self.n = t * R + c
                self.slot, self.bank = c % R, c % G
                self.turn = t + c // R

            def plus(self, d):
                return Tile(self.t, self.c + d)

            def exists(self):
                return not isinstance(self.n, int) or 0 <= self.n < NTILE

        TURNS = NTILE // R

        def loop(eng, body):
            for u in range(-2, R):
                body(Tile(0, u))
            with eng.Fori(1, TURNS - 2) as t:
                for c in range(R):
                    body(Tile(t, c))
            for u in range((TURNS - 2) * R, NTILE + 1):
                body(Tile(0, u))

        @block.gpsimd
        def _(pool):
            for z in range(R):
                pool.memset(wd[z][64:FPAD, :, :], 0.0).then_inc(pads_set, 1)
            pool.wait_ge(pads_set, R)
            pool.memset(hid[:, FE:2 * FPAD], 0.0).then_inc(pads_set, 1)

        @block.sync
        def _(sp):
            sp.wait_ge(pads_set, R + 1)

            def load(u, first):
                z, next_group = u.slot, u.plus(1)
                last = u.n - R + 1 if isinstance(u.n, int) else sp.snap(u.n - R + 1)
                e = sp.value_load(cells[z // G][0:1, z % G:z % G + 1], min_val=0, max_val=NE - 1)
                if not first:
                    sp.wait_ge(gu_done, last)
                sp.dma_start(wgu[z][:, :, :], w1[bass.ds(e, 1)].rearrange("o (p k) f -> p (o k) f", k=KD))\
                    .then_inc(wgu_loaded[z], 16)
                if not first:
                    sp.wait_ge(y_done, last)
                if z % G == G - 1 and next_group.exists():
                    sp.wait_ge(cells_loaded[next_group.slot // G], 16 * (next_group.turn + 1))
                sp.dma_start(wd[z][0:FEP, :, :], w2[bass.ds(e, 1)].rearrange("o (p k) d -> p (o k) d", k=2))\
                    .then_inc(wd_loaded[z], 16)

            def load_cells(u):
                sp.dma_start(cells[u.slot // G][:, :], expert_dram[bass.ds(u.n, G)].unsqueeze(0))\
                    .then_inc(cells_loaded[u.slot // G], 16)

            def step(u, first, more=True):
                load(u, first)
                if u.slot % G == G - 1 and more:
                    load_cells(u.plus(R - G + 1))

            for u in range(0, R, G):
                load_cells(Tile(0, u))
            sp.wait_ge(cells_loaded[0], 16)
            for u in range(R):
                step(Tile(0, u), True)
            with sp.Fori(1, TURNS - 1) as t:
                for c in range(R):
                    step(Tile(t, c), False)
            for u in range((TURNS - 1) * R, NTILE):
                step(Tile(0, u), False, u + R - G + 1 < NTILE)

        @block.tensor
        def _(pe):
            def turn_x(u):
                if not u.exists():
                    return
                pe.wait_ge(xt_ready, u.n)
                pe.wait_ge(x_loaded[u.slot], 16 * (u.turn + 1))
                for k in range(KD):
                    ins = pe.transpose(ps_x[:, k * P:(k + 1) * P], x[u.slot][:, k::KD], ident[:, :])
                ins.then_inc(x_turned, 1)

            def gate_up(u):
                if not u.exists():
                    return
                pe.wait_ge(wgu_loaded[u.slot], 16 * (u.turn + 1))
                pe.wait_ge(xt_ready, u.n + 1)
                if u.plus(-G).exists():
                    pe.wait_ge(gated, u.n - G + 1)
                for k in range(KD):
                    ins = pe.matmul(ps_gu[:, u.bank, 0:2 * FE], xt[:, u.bank, k, :], wgu[u.slot][:, k, :],
                                    start=k == 0, stop=k == KD - 1)
                ins.then_inc(gu_done, 1)

            def turn_h(u):
                if not u.exists():
                    return
                pe.wait_ge(gated, u.n + 1)
                pe.wait_ge(ht_ready, u.n)
                for k in range(2):
                    ins = pe.transpose(ps_h[0:FPAD, k * P:(k + 1) * P], hid[:, k::2], ident[:, :])
                ins.then_inc(h_turned, 1)

            def down(u):
                if not u.exists():
                    return
                pe.wait_ge(wd_loaded[u.slot], 16 * (u.turn + 1))
                pe.wait_ge(ht_ready, u.n + 1)
                if u.plus(-G).exists():
                    pe.wait_ge(y_copied, u.n - G + 1)
                for k in range(2):
                    ins = pe.matmul(ps_y[:, u.bank, 0:D], ht[u.c % 2][:, k, :], wd[u.slot][:, k, :], start=k == 0, stop=k == 1)
                ins.then_inc(y_done, 1)

            pe.wait_ge(pads_set, R + 1)

            def body(u):
                gate_up(u.plus(1))
                turn_h(u)
                turn_x(u.plus(2))
                down(u.plus(-1))

            loop(pe, body)

        @block.scalar
        def _(act):
            def copy_x(u):
                if not u.exists():
                    return
                act.wait_ge(x_turned, u.n + 1)
                if u.plus(-G).exists():
                    act.wait_ge(gu_done, u.n - G + 1)
                act.activation(xt[:, u.bank, :, :], ps_x[:, 0:KD * P].rearrange("p (k t) -> p k t", k=KD), ACT.Copy)\
                    .then_inc(xt_ready, 1)

            def gate(u):
                if not u.exists():
                    return
                act.wait_ge(gu_done, u.n + 1)
                act.wait_ge(gated, u.n)
                act.activation(gs[:, :], ps_gu[:, u.bank, 0:FE], ACT.Silu).then_inc(acted, 1)

            def store(u):
                if not u.exists():
                    return
                act.wait_ge(y_copied, u.n + 1)
                act.dma_start(out_dram[bass.ds(u.n * P, P), :], y[u.slot][:, :]).then_inc(y_stored[u.slot], 16)

            def load_x(u):
                if u.exists():
                    act.dma_start(x[u.slot][:, :], sorted_dram[bass.ds(u.n * P, P), :]).then_inc(x_loaded[u.slot], 16)

            for u in range(R):
                load_x(Tile(0, u))

            def body(u):
                copy_x(u.plus(2))
                gate(u.plus(1))
                if u.plus(2).exists():
                    load_x(u.plus(2 + R))
                store(u.plus(-2))

            loop(act, body)
            for u in (NTILE - 1,):
                store(Tile(0, u))
            for z in range(R):
                act.wait_ge(y_stored[z], 16 * ((NTILE - 1 - z) // R + 1))

        @block.vector
        def _(dve):
            def mul(u):
                if not u.exists():
                    return
                dve.wait_ge(acted, u.n + 1)
                dve.wait_ge(h_turned, u.n)
                dve.tensor_tensor(hid[:, 0:FE], gs[:, :], ps_gu[:, u.bank, FE:2 * FE], ALU.mult).then_inc(gated, 1)

            def copy_h(u):
                if not u.exists():
                    return
                dve.wait_ge(h_turned, u.n + 1)
                if u.plus(-2).exists():
                    dve.wait_ge(y_done, u.n - 1)
                dve.tensor_copy(ht[u.c % 2][:, :, :], ps_h[0:FPAD, 0:2 * P].rearrange("p (k t) -> p k t", k=2))\
                    .then_inc(ht_ready, 1)

            def copy_y(u):
                if not u.exists():
                    return
                if u.plus(-R).exists():
                    dve.wait_ge(y_stored[u.slot], 16 * u.turn)
                dve.wait_ge(y_done, u.n + 1)
                dve.tensor_copy(y[u.slot][:, :], ps_y[:, u.bank, 0:D]).then_inc(y_copied, 1)

            def body(u):
                copy_h(u)
                mul(u.plus(1))
                copy_y(u.plus(-1))

            dve.wait_ge(pads_set, R + 1)
            loop(dve, body)


def gather_add(nc, tag, x_sb, weights, slots, out_dram, y_dram):
    R = 6
    with ExitStack() as ctx:
        s = Scope(nc, ctx, tag)
        got = [s.sbuf(f"got{z}", [P, D]) for z in range(R)]
        gathered = [s.sem(f"gathered{z}") for z in range(R)]
        added = s.sem("added")
        stored = s.sem("stored")
        block = ctx.enter_context(nc.Block())

        @block.gpsimd
        def _(pool):
            for i in range(NTT):
                for k in range(TOP):
                    n = i * TOP + k
                    if n >= R:
                        pool.wait_ge(added, n - R + 1)
                    pool.indirect_dma_start(out=got[n % R][:, :], out_offset=None, in_=out_dram[:, :],
                                            in_offset=bass.IndirectOffsetOnAxis(ap=slots[:, k, i:i + 1], axis=0))\
                        .then_inc(gathered[n % R], 16)

        @block.vector
        def _(dve):
            for i in range(NTT):
                for k in range(TOP):
                    n = i * TOP + k
                    dve.wait_ge(gathered[n % R], 16 * (n // R + 1))
                    if n:
                        dve.wait_ge(added, n)
                    dve.scalar_tensor_tensor(out=x_sb[:, i, :], in0=got[n % R][:, :], scalar=weights[:, i, k:k + 1],
                                             in1=x_sb[:, i, :], op0=ALU.mult, op1=ALU.add).then_inc(added, 1)

        @block.sync
        def _(sp):
            for c in range(NCH):
                sp.wait_ge(added, (c + 1) * CT * TOP)
                sp.dma_start(y_dram[c].rearrange("(i p) d -> p i d", p=P), x_sb[:, c * CT:(c + 1) * CT, :])\
                    .then_inc(stored, 16)
            sp.wait_ge(stored, 16 * NCH)


def moe(nc, ctx, x_sb, ident, gate_w, w1, w2, ws_gate_up, ws_down, sorted_dram, y_dram):
    FS = ws_down.shape[0]
    sizes = [P, P, FS - 2 * P]
    s = Scope(nc, ctx, "moe")
    xn_all = s.sbuf("xn_all", [P, NTT, D])
    weights = s.sbuf("weights", [P, NTT, TOP])
    slots = s.sbuf("slots", [P, TOP, NTT], U32)
    sgu = s.sbuf("sgu", [P, KD, 2 * FS])
    sd = s.sbuf("sd", [P, len(sizes), D])
    scattered = s.sem("scattered")
    expert_dram = nc.dram_tensor("tile_expert", [2 * P], I32, kind="Internal").ap()
    out_dram = nc.dram_tensor("y_sorted", [NSLOT, D], F32, kind="Internal").ap()

    def load_shared(sp, loaded):
        sp.dma_start(sgu[:, :, :], ws_gate_up.rearrange("(p k) f -> p k f", k=KD)).then_inc(loaded, 16)
        for m, r in enumerate(sizes):
            sp.dma_start(sd[0:r, m, :], ws_down[m * P:m * P + r, :]).then_inc(loaded, 16)
        return 16 * (1 + len(sizes))

    route(nc, "route", x_sb, ident, gate_w, xn_all, weights, slots, expert_dram, load_shared)
    mlp(nc, "shared", x_sb, ident, sgu[:, :, 0:FS], sgu[:, :, FS:2 * FS], lambda m: sd[0:sizes[m], m, :], sizes, ACT.Silu,
        xn_all=xn_all, on_gpsimd=scatter_program(xn_all, slots, sorted_dram, scattered))
    experts(nc, "experts", ident, w1, w2, expert_dram, sorted_dram, out_dram)
    gather_add(nc, "combine", x_sb, weights, slots, out_dram, y_dram)


MLP = 2048
BLOCK = 32
SCALE_1 = 0.5


def decoded_mlp(nc, x_sb, ident, wo, bo, att_dram, codes, scales, sorted_dram):
    with ExitStack() as ctx:
        s = Scope(nc, ctx, "mlp_w")
        w_gate, w_up, w_down = (s.sbuf(n, [P, KD, MLP]) for n in ("gate", "up", "down"))
        order = [(w, n) for n in range(MLP // PIECE) for w in (0, 1)] + [(2, n) for n in range(MLP // PIECE)]
        decoder = Decoder(s, codes, scales, [w_gate, w_up, w_down], order)
        zeros = ZeroFill(s, sorted_dram)
        beside_projection = 5
        project_out(nc, "out0", x_sb, ident, wo, bo, att_dram, decoder, beside_projection)

        def on_sync(sp):
            for n in range(beside_projection, decoder.n):
                decoder.load(sp, n)
            zeros.store(sp)

        def on_gpsimd(pool):
            zeros.set(pool)
            for n in range(beside_projection, decoder.n):
                decoder.multiply(pool, n)

        mlp(nc, "mlp", x_sb, ident, w_gate, w_up, lambda m: w_down[:, m % 2, m // 2 * D:(m // 2 + 1) * D],
            [P] * (MLP // P), ACT.Gelu_apprx_tanh, on_sync=on_sync, on_gpsimd=on_gpsimd,
            decoder=decoder, n_decoded=beside_projection, first=lambda m: 2 * (m * P // PIECE + 1))


def program(nc, a, y):
    with ExitStack() as ctx:
        s = Scope(nc, ctx, "all")
        x_sb = s.sbuf("x", [P, NTT, D])
        ident = s.sbuf("ident", [P, P])
        ident_bf = s.sbuf("ident_bf", [P, P], BF16)
        mask_q = s.sbuf("mask_q", [P, P], BF16)
        mask_k = s.sbuf("mask_k", [P, P], BF16)
        q_dram = nc.dram_tensor("q_parts", [2, D, T], F32, kind="Internal").ap()
        k_dram = nc.dram_tensor("k_parts", [2, D, T], F32, kind="Internal").ap()
        att_dram = nc.dram_tensor("att", [T, D], F32, kind="Internal").ap()
        first_sem = nc.free_semaphores[0]
        sorted_dram = nc.dram_tensor("x_sorted", [NSLOT, D], F32, kind="Internal").ap()
        make_constants(nc, a["L0_attn_X"], x_sb, ident, ident_bf, mask_q, mask_k)

        for layer, heads, pitch, causal, parts in ((0, 16, 32, True, PARTS_16), (1, 4, 66, False, PARTS_64)):
            w = {n: a[f"L{layer}_attn_{n}"] for n in ("Wq", "bq", "Wk", "bk", "Wv", "bv", "Wo", "bo")}
            affine = (a["L0_attn_ln_g"], a["L0_attn_ln_b"]) if layer == 0 else None
            v_dram = nc.dram_tensor(f"v{layer}", [T, heads * pitch], F32, kind="Internal").ap()
            scale = (D // heads) ** -0.5 if layer == 0 else SCALE_1
            project_qkv(nc, f"qkv{layer}", x_sb, ident, w, affine, q_dram, k_dram, v_dram, heads, pitch)
            attention(nc, f"att{layer}", ident, ident_bf, mask_q, mask_k, q_dram, k_dram, v_dram, att_dram,
                      heads, pitch, causal, parts, scale)
            if layer == 1:
                project_out(nc, "out1", x_sb, ident, w["Wo"], w["bo"], att_dram)
            else:
                decoded_mlp(nc, x_sb, ident, w["Wo"], w["bo"], att_dram, a["codes"], a["scales"], sorted_dram)
                nc.all_engine_barrier(sems_to_clear=range(first_sem, nc.free_semaphores[0]))
        moe(nc, ctx, x_sb, ident, a["L1_ffn_gate_w"], a["L1_ffn_w_gate_up"], a["L1_ffn_w_down"],
            a["L1_ffn_ws_gate_up"], a["L1_ffn_ws_down"], sorted_dram, y)


def by_parity(m):
    r = m.shape[0]
    return m.reshape(r, MLP // D, P, 2).transpose(0, 1, 3, 2).reshape(r, MLP)


def kernel(**inputs):
    import concourse.bacc as bacc
    from concourse.bass_utils import run_bass_kernel_spmd

    inp = {n: np.asarray(v) for n, v in inputs.items()}
    arrays = {}
    for n in ("L0_attn_X", "L0_attn_ln_g", "L0_attn_ln_b"):
        arrays[n] = inp[n]
    for layer in (0, 1):
        for n in ("Wq", "Wk", "Wv", "Wo", "bv", "bo"):
            arrays[f"L{layer}_attn_{n}"] = inp[f"L{layer}_attn_{n}"]
        for n in ("bq", "bk"):
            arrays[f"L{layer}_attn_{n}"] = inp[f"L{layer}_attn_{n}"].reshape(KD, P).T
    g, u, d = (inp[f"L0_ffn_{n}_W_packed"] for n in ("gate", "up", "down"))
    gs, us, ds = (inp[f"L0_ffn_{n}_scales"] for n in ("gate", "up", "down"))
    nt = MLP // D
    arrays["codes"] = np.stack([by_parity(g.T), by_parity(u.T),
                                d.T.reshape(nt, P, D).transpose(1, 0, 2).reshape(P, MLP)])
    arrays["scales"] = np.stack([by_parity(gs.T), by_parity(us.T),
                                 ds.T.reshape(nt, D // BLOCK, D).transpose(1, 0, 2).reshape(D // BLOCK, MLP)])
    arrays["L1_ffn_gate_w"] = inp["L1_ffn_gate_w"].T
    arrays["L1_ffn_w_gate_up"] = inp["L1_ffn_w_gate_up"].transpose(0, 2, 1)
    arrays["L1_ffn_w_down"] = inp["L1_ffn_w_down"].transpose(0, 2, 1)
    arrays["L1_ffn_ws_gate_up"] = inp["L1_ffn_ws_gate_up"].T
    arrays["L1_ffn_ws_down"] = inp["L1_ffn_ws_down"].T
    arrays = {n: np.ascontiguousarray(v) for n, v in arrays.items()}

    nc = bacc.Bacc("TRN2", target_bir_lowering=False, num_devices=1)
    aps = {n: nc.dram_tensor(n, v.shape, mybir.dt.from_np(v.dtype), kind="ExternalInput").ap()
           for n, v in arrays.items()}
    y = nc.dram_tensor("y", inp["L0_attn_X"].shape, F32, kind="ExternalOutput").ap()
    program(nc, aps, y)
    result = run_bass_kernel_spmd(nc, [arrays], core_ids=[0])
    return result.results[0]["y"]
```

```python
from contextlib import ExitStack

import numpy as np

import concourse.bass as bass
from concourse import mybir

F32 = mybir.dt.float32
F32R = mybir.dt.float32r
BF16 = mybir.dt.bfloat16
I32 = mybir.dt.int32
U32 = mybir.dt.uint32
ALU = mybir.AluOpType
ACT = mybir.ActivationFunctionType
AX_X = mybir.AxisListType.X

P = 128
D = 256
T = 2048
S = 512
B = T // S
CT = 4
CHUNK = CT * P
NCH = T // CHUNK
KD = D // P
NTT = T // P
LN_EPS = 1e-5
NEG = -1e30


class Scope:

    def __init__(self, nc, ctx, tag):
        self.nc, self.ctx, self.tag = nc, ctx, tag

    def sbuf(self, name, shape, dt=F32):
        return self.ctx.enter_context(self.nc.sbuf_tensor(f"{self.tag}_{name}", shape, dt))

    def psum(self, name, shape, dt=F32):
        return self.ctx.enter_context(self.nc.psum_tensor(f"{self.tag}_{name}", shape, dt))

    def sem(self, name):
        return self.ctx.enter_context(self.nc.semaphore(f"{self.tag}_{name}"))


def make_constants(nc, x_dram, x_sb, ident, ident_bf, mask_q):
    with ExitStack() as ctx:
        s = Scope(nc, ctx, "const")
        x_loaded, filled, shaped = s.sem("x_loaded"), s.sem("filled"), s.sem("shaped")
        block = ctx.enter_context(nc.Block())

        @block.sync
        def _(sp):
            for c in range(NCH):
                sp.dma_start(x_sb[:, c * CT:(c + 1) * CT, :],
                             x_dram[c].rearrange("(i p) d -> p i d", p=P)).then_inc(x_loaded, 16)
            sp.wait_ge(x_loaded, 16 * NCH)

        @block.gpsimd
        def _(pool):
            for t in (ident, ident_bf, mask_q):
                pool.memset(t[:, :], 0.0).then_inc(filled, 1)
            pool.wait_ge(filled, 3)
            for t in (ident, ident_bf):
                pool.affine_select(out=t[:, :], in_=t[:, :], compare_op=ALU.not_equal, fill=1.0, base=0,
                                   pattern=[[-1, P]], channel_multiplier=1).then_inc(shaped, 1)
            pool.affine_select(out=mask_q[:, :], in_=mask_q[:, :], compare_op=ALU.is_ge, fill=NEG, base=0,
                               pattern=[[-1, P]], channel_multiplier=1).then_inc(shaped, 1)
            pool.wait_ge(shaped, 3)


def wait(eng, sem, n):
    if not isinstance(n, int) or n > 0:
        eng.wait_ge(sem, n)


def chunks(eng, body):
    body(0, True)
    with eng.Fori(1, NCH - 1) as c:
        body(c, True)
    body(NCH - 1, False)


class NormStats:

    def __init__(self, s, n=CT, tag=""):
        self.n = n
        self.stats = s.sbuf(f"stats{tag}", [P, n, 6])
        self.mv = s.sbuf(f"mv{tag}", [P, n, 2])
        self.var = s.sbuf(f"var{tag}", [P, n])
        self.inv = s.sbuf(f"inv{tag}", [P, n])
        self.root = s.sbuf(f"root{tag}", [P, n])
        self.tmp = s.sbuf(f"tmp{tag}", [P, n])
        self.rstd = s.sbuf(f"rstd{tag}", [P, n])
        self.inv_done = s.sem(f"inv_done{tag}")
        self.root_done = s.sem(f"root_done{tag}")

    def mean(self, i):
        return self.mv[:, i, 0:1]

    def on_vector(self, dve, tile, turn=0):
        for i in range(self.n):
            dve.bn_stats(self.stats[:, i, :], tile(i))
        dve.drain()
        for i in range(self.n):
            dve.bn_aggr(self.mv[:, i, :], self.stats[:, i, :])
        dve.drain()
        dve.tensor_scalar(self.var[:, :], self.mv[:, :, 1], LN_EPS, None, ALU.add)
        dve.drain()
        dve.reciprocal(self.inv[:, :], self.var[:, :]).then_inc(self.inv_done, 1)
        dve.wait_ge(self.root_done, turn + 1)
        dve.tensor_tensor(self.tmp[:, :], self.root[:, :], self.root[:, :], ALU.mult)
        dve.drain()
        dve.tensor_tensor(self.inv[:, :], self.tmp[:, :], self.var[:, :], ALU.mult)
        dve.drain()
        dve.tensor_scalar(self.tmp[:, :], self.inv[:, :], -0.5, 1.5, ALU.mult, ALU.add)
        dve.drain()
        dve.tensor_tensor(self.rstd[:, :], self.tmp[:, :], self.root[:, :], ALU.mult)
        dve.drain()

    def on_scalar(self, act, turn=0):
        act.wait_ge(self.inv_done, turn + 1)
        act.activation(self.root[:, :], self.inv[:, :], ACT.Sqrt).then_inc(self.root_done, 1)


def token_tile(x, n):
    return x[:, bass.ds(n, 1), :].rearrange("p o d -> p (o d)")


def project_qkv(nc, tag, x_sb, ident, w, affine, q_dram, k_dram, v_dram, heads, pitch):
    hd = D // heads
    with ExitStack() as ctx:
        s = Scope(nc, ctx, tag)
        ns = NormStats(s)
        ns2 = NormStats(s, tag="2") if affine else None
        wt = [s.sbuf(f"w{n}", [P, KD, D]) for n in "qkv"]
        bqk = s.sbuf("bqk", [P, 2, KD])
        bv = s.sbuf("bv", [P, D])
        xo = s.sbuf("xo", [P, CT, D]) if affine else None
        x1 = s.sbuf("x1", [P, CT, D]) if affine else None
        gb = s.sbuf("gb", [P, 2, D]) if affine else None
        xn = s.sbuf("xn", [P, CT, D])
        xt = s.sbuf("xt", [P, KD, CHUNK])
        hi = s.sbuf("hi", [P, 2, KD, CHUNK], F32R)
        lo = s.sbuf("lo", [P, 2, KD, CHUNK], F32R)
        vs = s.sbuf("vs", [P, CT, heads * pitch])
        v4 = vs[:, :, :].rearrange("p i (h c) -> p i h c", c=pitch)
        ps_t = s.psum("ps_t", [P, KD, CHUNK])
        ps_qk = s.psum("ps_qk", [P, 2 * KD, CHUNK])
        ps_v = s.psum("ps_v", [P, 2, 2, D])

        qk_weights_loaded = s.sem("qk_weights_loaded")
        v_weights_loaded = s.sem("v_weights_loaded")
        affine_loaded = s.sem("affine_loaded")
        v_columns_set = s.sem("v_columns_set")
        normed = s.sem("normed")
        transposed = s.sem("transposed")
        xt_ready = s.sem("xt_ready")
        qk_done = s.sem("qk_done")
        hi_done = s.sem("hi_done")
        lo_done = s.sem("lo_done")
        v_done = s.sem("v_done")
        v_written = s.sem("v_written")
        qk_stored = s.sem("qk_stored")
        v_stored = s.sem("v_stored")
        block = ctx.enter_context(nc.Block())
        NQ = 2 * KD

        @block.sync
        def _(sp):
            if affine:
                for j in range(2):
                    sp.dma_start(gb[:, j, :], affine[j].partition_broadcast(P)).then_inc(affine_loaded, 16)
            for t, a in zip(wt, (w["Wq"], w["Wk"])):
                sp.dma_start(t[:, :, :], a.rearrange("(k p) n -> p k n", p=P)).then_inc(qk_weights_loaded, 16)
            sp.dma_start(bqk[:, 0, :], w["bq"]).then_inc(qk_weights_loaded, 16)
            sp.dma_start(bqk[:, 1, :], w["bk"]).then_inc(qk_weights_loaded, 16)
            sp.dma_start(wt[2][:, :, :], w["Wv"].rearrange("(k p) n -> p k n", p=P)).then_inc(v_weights_loaded, 16)
            sp.dma_start(bv[:, :], w["bv"].partition_broadcast(P)).then_inc(v_weights_loaded, 16)

            def body(c, more):
                for j, dst in enumerate((q_dram, k_dram)):
                    sp.wait_ge(lo_done, c * NQ + (j + 1) * KD)
                    for part, t in enumerate((hi, lo)):
                        sp.dma_start(dst[part].rearrange("(k p) t -> p k t", p=P)[:, :, bass.ds(c * CHUNK, CHUNK)],
                                     t[:, j, :, :].bitcast(F32)).then_inc(qk_stored, 16)
                sp.wait_ge(v_written, c * 2 + 2)
                sp.dma_start(v_dram.rearrange("(i p) f -> p i f", p=P)[:, bass.ds(c * CT, CT), :],
                             vs[:, :, :]).then_inc(v_stored, 16)

            chunks(sp, body)
            sp.wait_ge(qk_stored, 16 * 4 * NCH)
            sp.wait_ge(v_stored, 16 * NCH)

        @block.gpsimd
        def _(pool):
            pool.memset(vs[:, :, :], 0.0).then_inc(v_columns_set, 1)
            pool.wait_ge(v_columns_set, 1)
            for i in range(CT):
                pool.memset(v4[:, i, :, hd:hd + 1], 1.0).then_inc(v_columns_set, 1)

        @block.vector
        def _(dve):
            def norm(c):
                ns.on_vector(dve, lambda i: token_tile(x_sb, c * CT + i), c)
                if affine:
                    for i in range(CT):
                        dve.tensor_scalar(xo[:, i, :], token_tile(x_sb, c * CT + i), ns.mean(i), ns.rstd[:, i:i + 1],
                                          ALU.subtract, ALU.mult)
                    dve.drain()
                    ns2.on_vector(dve, lambda i: xo[:, i, :], c)
                    wait(dve, affine_loaded, 32 if isinstance(c, int) and c == 0 else 0)
                    for i in range(CT):
                        dve.scalar_tensor_tensor(out=x1[:, i, :], in0=xo[:, i, :], scalar=ns2.mean(i), in1=gb[:, 0, :],
                                                 op0=ALU.subtract, op1=ALU.mult)
                    dve.drain()
                wait(dve, transposed, c)
                for i in range(CT):
                    if affine:
                        ins = dve.scalar_tensor_tensor(out=xn[:, i, :], in0=x1[:, i, :], scalar=ns2.rstd[:, i:i + 1],
                                                       in1=gb[:, 1, :], op0=ALU.mult, op1=ALU.add)
                    else:
                        ins = dve.tensor_scalar(xn[:, i, :], token_tile(x_sb, c * CT + i), ns.mean(i),
                                                ns.rstd[:, i:i + 1], ALU.subtract, ALU.mult)
                    ins.then_inc(normed, 1)

            def body(c, more):
                if more:
                    norm(c + 1)
                wait(dve, qk_stored, c * 64)
                for n in range(NQ):
                    j, m = n // KD, n % KD
                    dve.wait_ge(hi_done, c * NQ + n + 1)
                    dve.scalar_tensor_tensor(out=lo[:, j, m, :], in0=ps_qk[:, n, :], scalar=bqk[:, j, m:m + 1],
                                             in1=hi[:, j, m, :], op0=ALU.add, op1=ALU.subtract).then_inc(lo_done, 1)
                wait(dve, v_stored, c * 16)
                for b in range(2):
                    dve.wait_ge(v_done, c * 2 + b + 1)
                    dve.tensor_tensor(v4[:, 2 * b:2 * b + 2, :, 0:hd],
                                      ps_v[:, b, :, :].rearrange("p i (h c) -> p i h c", c=hd),
                                      bv[:, :].rearrange("p (h c) -> p h c", c=hd).unsqueeze(1)
                                      .to_broadcast([P, 2, heads, hd]), ALU.add).then_inc(v_written, 1)

            norm(0)
            dve.wait_ge(qk_weights_loaded, 16 * 4)
            dve.wait_ge(v_weights_loaded, 16 * 2)
            dve.wait_ge(v_columns_set, 1 + CT)
            chunks(dve, body)

        @block.scalar
        def _(act):
            def roots(c):
                ns.on_scalar(act, c)
                if affine:
                    ns2.on_scalar(act, c)

            def copy_xt(c):
                act.wait_ge(transposed, c + 1)
                wait(act, v_done, c * 2)
                act.activation(xt[:, :, :], ps_t[:, :, :], ACT.Copy).then_inc(xt_ready, 1)

            def body(c, more):
                if more:
                    roots(c + 1)
                wait(act, qk_stored, c * 64)
                for n in range(NQ):
                    j, m = n // KD, n % KD
                    act.wait_ge(qk_done, c * NQ + n + 1)
                    act.activation(hi[:, j, m, :], ps_qk[:, n, :], ACT.Identity,
                                   bias=bqk[:, j, m:m + 1]).then_inc(hi_done, 1)
                if more:
                    copy_xt(c + 1)

            roots(0)
            act.wait_ge(qk_weights_loaded, 16 * 4)
            copy_xt(0)
            chunks(act, body)

        @block.tensor
        def _(pe):
            def turn(c):
                pe.wait_ge(normed, (c + 1) * CT)
                wait(pe, xt_ready, c)
                for k in range(KD):
                    for i in range(CT):
                        ins = pe.transpose(ps_t[:, k, i * P:(i + 1) * P], xn[:, i, k * P:(k + 1) * P], ident[:, :])
                ins.then_inc(transposed, 1)

            def body(c, more):
                pe.wait_ge(xt_ready, c + 1)
                for n in range(NQ):
                    j, m = n // KD, n % KD
                    wait(pe, lo_done, (c - 1) * NQ + n + 1)
                    for k in range(KD):
                        ins = pe.matmul(ps_qk[:, n, :], wt[j][:, k, m * P:(m + 1) * P], xt[:, k, :],
                                        start=k == 0, stop=k == KD - 1)
                    ins.then_inc(qk_done, 1)
                for b in range(2):
                    wait(pe, v_written, (c - 1) * 2 + b + 1)
                    for i in range(2):
                        for k in range(KD):
                            ins = pe.matmul(ps_v[:, b, i, :], xt[:, k, (2 * b + i) * P:(2 * b + i + 1) * P],
                                            wt[2][:, k, :], start=k == 0, stop=k == KD - 1)
                    ins.then_inc(v_done, 1)
                if more:
                    turn(c + 1)

            turn(0)
            pe.wait_ge(qk_weights_loaded, 16 * 4)
            pe.wait_ge(v_weights_loaded, 16 * 2)
            chunks(pe, body)

UNITS = 16
UF = 64
SLOTS = 4
NEG_ROW = 96
S1_ORDER = (2, 1, 0, 3)


class Unit:

    def __init__(self, t, c):
        self.t, self.c = t, c
        self.n = t * SLOTS + c
        self.slot = c % SLOTS
        self.turn = t + c // SLOTS

    def plus(self, d):
        return Unit(self.t, self.c + d)

    def exists(self):
        return not isinstance(self.n, int) or 0 <= self.n < UNITS


def attention(nc, tag, ident, ident_bf, mask_q, q_dram, k_dram, v_dram, att_dram,
              heads, pitch, causal, parts, scale):
    hu = heads * UF // D
    hd = D // heads
    nt = CT * hu
    nx = nt // 2
    rows = hu * pitch
    last_part = len(parts) - 1
    n_loads = sum(len(q) + len(k) for q, k in parts)
    with ExitStack() as ctx:
        s = Scope(nc, ctx, tag)
        qs = [[s.sbuf(f"qs{a}_{z}", [P, hu, S], F32R) for z in range(SLOTS)] for a in range(len(parts))]
        ks = [[s.sbuf(f"ks{a}_{z}", [P, hu, S], F32R) for z in range(SLOTS)] for a in range(len(parts))]
        vs = [s.sbuf(f"vs{z}", [P, CT, rows]) for z in range(SLOTS)]
        pt = s.sbuf("pt", [P, nt, S])
        mx = s.sbuf("mx", [P, hu, CT])
        neg = s.sbuf("neg", [P, 2, nt], F32R)
        neg_t = s.sbuf("neg_t", [2 * nt, P])
        osb = s.sbuf("osb", [rows, S])
        rsum = s.sbuf("rsum", [P, CT, hu, 1])
        att = s.sbuf("att", [P, CT, UF])
        ps_1 = s.psum("ps_1", [P, 2, S])
        ps_2 = s.psum("ps_2", [P, 2, 2, S])
        ps_o = s.psum("ps_o", [rows, S])
        ps_tr = s.psum("ps_tr", [P, S])

        zero_rows_set = [s.sem(f"zero_rows_set{z}") for z in range(SLOTS)]
        stack_set = [[s.sem(f"{n}_stack_set{z}") for n in "qk"] for z in range(SLOTS)]
        qk_loaded = [s.sem(f"qk_loaded{z}") for z in range(SLOTS)]
        v_loaded = [s.sem(f"v_loaded{z}") for z in range(SLOTS)]
        neg_loaded = [s.sem(f"neg_loaded{z}") for z in range(SLOTS)]
        s1_done = s.sem("s1_done")
        max_done = s.sem("max_done")
        neg_ready = s.sem("neg_ready")
        neg_turned = s.sem("neg_turned")
        neg_copied = s.sem("neg_copied")
        s2_done = s.sem("s2_done")
        exp_done = s.sem("exp_done")
        exp_seen = s.sem("exp_seen")
        masked = s.sem("masked")
        pv_done = s.sem("pv_done")
        o_copied = s.sem("o_copied")
        o_turned = s.sem("o_turned")
        normalized = s.sem("normalized")
        att_stored = s.sem("att_stored")
        block = ctx.enter_context(nc.Block())

        def loop(eng, body):
            for u in range(-1, SLOTS):
                body(Unit(0, u))
            with eng.Fori(1, UNITS // SLOTS - 1) as t:
                for c in range(SLOTS):
                    body(Unit(t, c))
            for u in range(UNITS - SLOTS, UNITS + 2):
                body(Unit(0, u))

        def off(j):
            return j * P if causal else 0

        def width(i):
            return (i + 1) * P if causal else S

        groups = []
        for i in S1_ORDER:
            g = S // max(width(i), S // hu)
            groups.append([range(h, min(h + g, hu)) for h in range(0, hu, g)])
        ng = sum(len(g) for g in groups)

        def group(step, n):
            return sum(len(g) for g in groups[:step]) + n

        def last_exp(j):
            return ((j + 1) * hu - 1) // 2 + 1

        @block.sync
        def _(sp):
            def load(u):
                z = u.slot
                b, g = u.n // 4, u.n % 4
                for a, both in enumerate(parts):
                    for dram, stack, blocks in ((q_dram, qs, both[0]), (k_dram, ks, both[1])):
                        for row, half in blocks:
                            src = dram[half][bass.ds(g * UF, UF), bass.ds(b * S, S)]
                            sp.dma_start(stack[a][z][row:row + hd, :, :].bitcast(F32),
                                         src.rearrange("(h d) t -> d h t", d=hd)).then_inc(qk_loaded[z], 16)

            def load_v(u):
                z = u.slot
                b, g = u.n // 4, u.n % 4
                src = v_dram[bass.ds(b * S, S), bass.ds(g * rows, rows)]
                sp.dma_start(vs[z][:, :, :], src.rearrange("(j p) f -> p j f", p=P)).then_inc(v_loaded[z], 16)

            def load_maxima(u):
                if not u.exists():
                    return
                sp.wait_ge(neg_copied, u.n + 1)
                for r in range(2):
                    sp.dma_start(qs[last_part][u.slot][NEG_ROW + r:NEG_ROW + r + 1, :, :].bitcast(F32),
                                 neg_t[r * nt:(r + 1) * nt, :]).then_inc(neg_loaded[u.slot], 16)

            def store_output(u):
                if not u.exists():
                    return
                b, g = u.n // 4, u.n % 4
                sp.wait_ge(normalized, u.n + 1)
                dst = att_dram[bass.ds(b * S, S), bass.ds(g * UF, UF)]
                sp.dma_start(dst.rearrange("(i p) f -> p i f", p=P), att[:, :, :]).then_inc(att_stored, 16)

            def body(u):
                w = u.plus(2)
                if w.exists():
                    if u.plus(-2).exists():
                        sp.wait_ge(s2_done, (u.n - 1) * nx)
                    load(w)
                    if u.plus(-2).exists():
                        sp.wait_ge(pv_done, (u.n - 1) * CT)
                    load_v(w)
                load_maxima(u)
                store_output(u.plus(-2))

            load(Unit(0, 0))
            load_v(Unit(0, 0))
            loop(sp, body)
            sp.wait_ge(att_stored, 16 * UNITS)

        def set_rows(eng, stacks, is_k, z):
            stack, zeroed = stacks[last_part][z], zero_rows_set[z]
            ins = eng.memset(stack[64:P, :, :].bitcast(F32), 0.0)
            if is_k:
                ins.then_inc(zeroed, 1)
                eng.wait_ge(zeroed, 1)
                ins = eng.memset(stack[NEG_ROW:NEG_ROW + 2, :, :].bitcast(F32), 1.0)
            ins.then_inc(stack_set[z][is_k], 1)
            if is_k:
                eng.wait_ge(stack_set[z][is_k], 1)

        @block.gpsimd
        def _(pool):
            set_rows(pool, qs, 0, 0)
            for z in range(1, SLOTS):
                set_rows(pool, qs, 0, z)
                set_rows(pool, ks, 1, z)

            def mask(u):
                if not u.exists():
                    return
                for n in range(nx):
                    pool.wait_ge(exp_done, u.n * nx + n + 1)
                    pool.sem_inc(exp_seen, 1)
                    diagonal = pt[:, 2 * n:2 * n + 2, 0:P]
                    pool.affine_select(out=diagonal, in_=diagonal, compare_op=ALU.is_ge, fill=0.0, base=0,
                                       pattern=[[0, 2], [1, P]], channel_multiplier=-1).then_inc(masked, 1)

            if causal:
                loop(pool, lambda u: mask(u.plus(-1)))

        @block.tensor
        def _(pe):
            def scores_q(u, step, part):
                if not u.exists():
                    return
                i = S1_ORDER[step]
                z = u.slot
                if step == 0 and part == 0 and not u.plus(-SLOTS).exists():
                    for sem in stack_set[z]:
                        pe.wait_ge(sem, 1)
                if step == 0 and part == 0:
                    pe.wait_ge(qk_loaded[z], (u.turn + 1) * 16 * n_loads)
                of_step = len(groups[step])
                for n in range((part * of_step + 1) // 2, ((part + 1) * of_step + 1) // 2):
                    g = group(step, n)
                    wait(pe, max_done, u.n * ng + g - 1)
                    bank = (u.c * ng + g) % 2
                    for a_h, h in enumerate(groups[step][n]):
                        out = ps_1[:, bank, a_h * width(i):(a_h + 1) * width(i)]
                        for a in range(len(parts)):
                            rows_a = NEG_ROW if a == last_part else P
                            ins = pe.matmul(out, qs[a][z][0:rows_a, h, i * P:(i + 1) * P],
                                            ks[a][z][0:rows_a, h, 0:width(i)],
                                            start=a == 0, stop=a == last_part and not causal)
                        if causal:
                            ins = pe.matmul(out[:, i * P:(i + 1) * P], ident_bf[:, :], mask_q[:, :],
                                            start=False, stop=True)
                    ins.then_inc(s1_done, 1)

            def scores_k(u, j, part):
                if not u.exists():
                    return
                z = u.slot
                if j == 0 and part == 0:
                    pe.wait_ge(neg_loaded[z], (u.turn + 1) * 32)
                for n in [n for n in range(nx) if 2 * n // hu == j][part:part + 1]:
                    wait(pe, exp_done, u.n * nx + n - 1)
                    for e in (2 * n, 2 * n + 1):
                        jj, h = e // hu, e % hu
                        out = ps_2[:, n % 2, e % 2, 0:S - off(jj)]
                        for a in range(len(parts)):
                            ins = pe.matmul(out, ks[a][z][:, h, jj * P:(jj + 1) * P], qs[a][z][:, h, off(jj):S],
                                            start=a == 0, stop=a == last_part)
                    ins.then_inc(s2_done, 1)

            def values(u, j):
                if not u.exists():
                    return
                z = u.slot
                if j == 0:
                    pe.wait_ge(v_loaded[z], (u.turn + 1) * 16)
                    wait(pe, o_copied, u.n)
                pe.wait_ge(masked if causal else exp_done, u.n * nx + last_exp(j))
                for h in range(hu):
                    ins = pe.matmul(ps_o[h * pitch:(h + 1) * pitch, off(j):S], vs[z][:, j, h * pitch:(h + 1) * pitch],
                                    pt[:, j * hu + h, 0:S - off(j)], start=j == 0, stop=j == CT - 1)
                ins.then_inc(pv_done, 1)

            def turn_output(u):
                if not u.exists():
                    return
                pe.wait_ge(o_copied, u.n + 1)
                wait(pe, normalized, u.n)
                w = u.plus(2)
                if w.exists():
                    pe.wait_ge(neg_copied, w.n + 1)
                for i in range(CT):
                    ins = pe.transpose(ps_tr[:, i * rows:(i + 1) * rows], osb[:, i * P:(i + 1) * P],
                                       ident[0:rows, 0:rows])
                ins.then_inc(o_turned, 1)

            def turn_maxima(u):
                if not u.exists():
                    return
                pe.wait_ge(neg_ready, u.n + 1)
                wait(pe, normalized, u.n - 2)
                pe.transpose(ps_tr[0:2 * nt, 0:P], neg[:, :, :].bitcast(F32).rearrange("p r n -> p (r n)"),
                             ident[:, :]).then_inc(neg_turned, 1)

            def scores(u, step, w, j, part):
                scores_q(u, step, part)
                scores_k(w, j, part)

            def body(u):
                t, v, w = u.plus(-2), u.plus(-1), u.plus(1)
                scores(u, 3, v, 0, 0)
                values(t, 2)
                scores(u, 3, v, 0, 1)
                scores(w, 0, v, 1, 0)
                values(t, 3)
                scores(w, 0, v, 1, 1)
                scores(w, 1, v, 2, 0)
                turn_maxima(u)
                values(v, 0)
                scores(w, 1, v, 2, 1)
                scores(w, 2, v, 3, 0)
                turn_output(t)
                values(v, 1)
                scores(w, 2, v, 3, 1)

            loop(pe, body)

        @block.scalar
        def _(act):
            def exps(u, j, parts=(0, 1)):
                if not u.exists():
                    return
                for n in [n for n in range(nx) if 2 * n // hu == j][parts[0]:parts[-1] + 1]:
                    act.wait_ge(s2_done, u.n * nx + n + 1)
                    wait(act, pv_done, (u.n - 1) * CT + (2 * n + 1) // hu + 1)
                    w = S - off(j)
                    act.activation(pt[:, 2 * n:2 * n + 2, 0:w], ps_2[:, n % 2, :, 0:w], ACT.Exp,
                                   scale=scale).then_inc(exp_done, 1)

            def copy_output(u):
                if not u.exists():
                    return
                act.wait_ge(pv_done, (u.n + 1) * CT)
                wait(act, o_turned, u.n)
                act.activation(osb[:, :], ps_o[:, :], ACT.Copy).then_inc(o_copied, 1)

            def copy_maxima(u):
                if not u.exists():
                    return
                act.wait_ge(neg_turned, u.n + 1)
                w = u.plus(-1)
                if w.exists():
                    act.wait_ge(neg_loaded[w.slot], (w.turn + 1) * 32)
                act.activation(neg_t[:, :], ps_tr[0:2 * nt, 0:P], ACT.Copy).then_inc(neg_copied, 1)

            def body(u):
                v = u.plus(-1)
                exps(v, 0)
                exps(v, 1, (0,))
                copy_output(u.plus(-2))
                exps(v, 1, (1,))
                copy_maxima(u)
                exps(v, 2)
                exps(v, 3)

            loop(act, body)

        @block.vector
        def _(dve):
            def maxima(u, step):
                if not u.exists():
                    return
                i = S1_ORDER[step]
                for n, hs in enumerate(groups[step]):
                    g = group(step, n)
                    dve.wait_ge(s1_done, u.n * ng + g + 1)
                    dve.tensor_reduce(mx[:, hs[0]:hs[-1] + 1, i], ps_1[:, (u.c * ng + g) % 2, 0:len(hs) * width(i)]
                                      .rearrange("p (h w) -> p h w", h=len(hs)), AX_X, ALU.max).then_inc(max_done, 1)

            def split_maxima(u):
                if not u.exists():
                    return
                dve.drain()
                wait(dve, neg_turned, u.n)
                dve.tensor_scalar(neg[:, 0, :], mx[:, :, :].rearrange("p h i -> p (h i)"), -1.0, None, ALU.mult)
                dve.drain()
                dve.scalar_tensor_tensor(out=neg[:, 1, :], in0=mx[:, :, :].rearrange("p h i -> p (h i)"),
                                         scalar=-1.0, in1=neg[:, 0, :], op0=ALU.mult, op1=ALU.subtract)\
                    .then_inc(neg_ready, 1)
                dve.drain()

            def normalize(u):
                if not u.exists():
                    return
                dve.wait_ge(o_turned, u.n + 1)
                wait(dve, att_stored, u.n * 16)
                out = ps_tr[:, 0:CT * rows].rearrange("p (i h c) -> p i h c", i=CT, c=pitch)
                dve.reciprocal(rsum[:, :, :, :], out[:, :, :, hd:hd + 1])
                dve.drain()
                dve.tensor_tensor(att[:, :, :].rearrange("p i (h c) -> p i h c", c=hd), out[:, :, :, 0:hd],
                                  rsum[:, :, :, :].to_broadcast([P, CT, hu, hd]), ALU.mult).then_inc(normalized, 1)

            def body(u):
                maxima(u, 3)
                split_maxima(u)
                for step in range(3):
                    maxima(u.plus(1), step)
                normalize(u.plus(-2))

            set_rows(dve, ks, 1, 0)
            loop(dve, body)


PARTS_16 = [(((0, 0), (16, 1), (32, 0), (48, 1)), ((0, 0), (16, 0), (32, 1), (48, 1)))]
PARTS_64 = [(((0, 0), (64, 1)), ((0, 0), (64, 0))), (((0, 0),), ((0, 1),))]

def project_out(nc, tag, x_sb, ident, wo, bo, att_dram, decoder=None, n_decoded=0, xn_all=None):
    with ExitStack() as ctx:
        s = Scope(nc, ctx, tag)
        ns = NormStats(s) if xn_all is not None else None
        w = s.sbuf("w", [P, KD, D])
        b = s.sbuf("b", [P, D])
        at = [s.sbuf(f"at{z}", [P, CT, D]) for z in range(2)]
        att_t = [s.sbuf(f"att_t{z}", [P, KD, CHUNK]) for z in range(2)]
        ps_t = s.psum("ps_t", [P, 2, KD, CHUNK])
        ps_y = s.psum("ps_y", [P, CT, S])
        weights_loaded = s.sem("weights_loaded")
        loaded = [s.sem(f"loaded{z}") for z in range(2)]
        turned = s.sem("turned")
        copied = s.sem("copied")
        made = s.sem("made")
        biased = s.sem("biased")
        added = s.sem("added")
        block = ctx.enter_context(nc.Block())

        @block.sync
        def _(sp):
            def load(c):
                sp.dma_start(at[c % 2][:, :, :], att_dram[c * CHUNK:(c + 1) * CHUNK, :]
                             .rearrange("(i p) f -> p i f", p=P)).then_inc(loaded[c % 2], 16)

            load(0)
            sp.dma_start(b[:, :], bo.partition_broadcast(P)).then_inc(weights_loaded, 16)
            sp.dma_start(w[:, :, :], wo.rearrange("(k p) n -> p k n", p=P)).then_inc(weights_loaded, 16)
            load(1)
            for n in range(max(NCH - 2, n_decoded)):
                if n < n_decoded:
                    decoder.load(sp, n)
                if n < NCH - 2:
                    sp.wait_ge(turned, n + 1)
                    load(n + 2)

        @block.gpsimd
        def _(pool):
            pool.wait_ge(weights_loaded, 32)
            for i in range(NTT):
                pool.tensor_tensor(x_sb[:, i, :], x_sb[:, i, :], b[:, :], ALU.add).then_inc(biased, 1)
            for n in range(n_decoded):
                decoder.multiply(pool, n)

        @block.tensor
        def _(pe):
            def turn(c):
                pe.wait_ge(loaded[c % 2], 16 * (c // 2) + 16)
                wait(pe, copied, c - 1)
                for k in range(KD):
                    for i in range(CT):
                        ins = pe.transpose(ps_t[:, c % 2, k, i * P:(i + 1) * P], at[c % 2][:, i, k * P:(k + 1) * P],
                                           ident[:, :])
                ins.then_inc(turned, 1)

            turn(0)
            pe.wait_ge(weights_loaded, 32)
            for c in range(NCH):
                if c + 1 < NCH:
                    turn(c + 1)
                pe.wait_ge(copied, c + 1)
                for i in range(CT):
                    wait(pe, added, (c - 1) * CT + i + 1)
                    for k in range(KD):
                        ins = pe.matmul(ps_y[:, i, 0:D], att_t[c % 2][:, k, i * P:(i + 1) * P], w[:, k, :],
                                        start=k == 0, stop=k == KD - 1)
                    ins.then_inc(made, 1)

        @block.scalar
        def _(act):
            def copy(c):
                act.wait_ge(turned, c + 1)
                wait(act, made, (c - 1) * CT)
                act.activation(att_t[c % 2][:, :, :], ps_t[:, c % 2, :, :], ACT.Copy).then_inc(copied, 1)

            copy(0)
            for n in range(max(NCH, n_decoded)):
                if n + 1 < NCH:
                    copy(n + 1)
                if n < n_decoded:
                    decoder.halve(act, n)
                    decoder.convert(act, n)
                if ns and n < NCH:
                    ns.on_scalar(act, n)

        @block.vector
        def _(dve):
            if decoder:
                decoder.set_table(dve)
            for c in range(NCH):
                if c < n_decoded:
                    decoder.look_up(dve, c)
                for i in range(CT):
                    dve.wait_ge(biased, c * CT + i + 1)
                    dve.wait_ge(made, c * CT + i + 1)
                    dve.tensor_tensor(x_sb[:, c * CT + i, :], x_sb[:, c * CT + i, :], ps_y[:, i, 0:D], ALU.add)\
                        .then_inc(added, 1)
                if ns:
                    dve.drain()
                    ns.on_vector(dve, lambda i: x_sb[:, c * CT + i, :], c)
                    for i in range(CT):
                        t = c * CT + i
                        dve.tensor_scalar(xn_all[:, t, :], x_sb[:, t, :], ns.mean(i), ns.rstd[:, i:i + 1],
                                          ALU.subtract, ALU.mult)
            for n in range(NCH, n_decoded):
                decoder.look_up(dve, n)


def mlp(nc, tag, x_sb, ident, w_gate, w_up, w_down, sizes, func, xn_all=None, on_sync=None, on_gpsimd=None,
        on_vector=None, decoder=None, n_decoded=0, first=None, split=False):
    nm = len(sizes)
    starts = [sum(sizes[:m]) for m in range(nm)]
    with ExitStack() as ctx:
        s = Scope(nc, ctx, tag)
        ns = NormStats(s) if xn_all is None else None
        xn = s.sbuf("xn", [P, CT, D])
        xt = s.sbuf("xt", [P, KD, CHUNK], F32R if split else F32)
        xt_low = s.sbuf("xt_low", [P, KD, CHUNK], F32R) if split else None
        gs = s.sbuf("gs", [P, 2, CHUNK])
        inner = s.sbuf("inner", [P, nm, CHUNK])
        ps_t = s.psum("ps_t", [P, KD, CHUNK])
        ps_g = s.psum("ps_g", [P, 2, CHUNK])
        ps_u = s.psum("ps_u", [P, 2, CHUNK])
        ps_y = s.psum("ps_y", [P, 2, S])
        normed = s.sem("normed")
        turned = s.sem("turned")
        xt_ready = s.sem("xt_ready")
        low_ready = s.sem("low_ready") if split else xt_ready
        gate_done = s.sem("gate_done")
        up_done = s.sem("up_done")
        acted = s.sem("acted")
        gated = s.sem("gated")
        made = s.sem("made")
        added = s.sem("added")
        block = ctx.enter_context(nc.Block())

        def decoding(c, m):
            if not (decoder and isinstance(c, int) and c == 0):
                return None
            left = decoder.n - n_decoded
            return n_decoded + m * left // nm if m * left // nm > (m - 1) * left // nm else None

        def await_decoded(c, n):
            if decoder and isinstance(c, int) and c == 0:
                return n
            return 0

        if on_sync:
            block.sync(on_sync)
        if on_gpsimd:
            block.gpsimd(on_gpsimd)

        @block.vector
        def _(dve):
            def stats(c):
                if ns:
                    ns.on_vector(dve, lambda i: token_tile(x_sb, c * CT + i), c)

            def norm(c):
                wait(dve, turned, c)
                for i in range(CT):
                    tile = bass.ds(c * CT + i, 1)
                    if xn_all is not None:
                        dve.tensor_scalar(xn[:, i:i + 1, :], xn_all[:, tile, :], 1.0, None, ALU.mult)\
                            .then_inc(normed, 1)
                        continue
                    dve.tensor_scalar(xn[:, i:i + 1, :], x_sb[:, tile, :], ns.mean(i), ns.rstd[:, i:i + 1],
                                      ALU.subtract, ALU.mult).then_inc(normed, 1)

            def low_part(c):
                if split:
                    dve.wait_ge(xt_ready, c + 1)
                    dve.tensor_tensor(xt_low[:, :, :], ps_t[:, :, :], xt[:, :, :].bitcast(F32), ALU.subtract)\
                        .then_inc(low_ready, 1)

            def body(c, more):
                for m in range(nm):
                    r = sizes[m]
                    n = decoding(c, m)
                    if n is not None:
                        decoder.look_up(dve, n)
                    dve.wait_ge(acted, c * nm + m + 1)
                    if m == 0:
                        wait(dve, made, c * CT)
                    dve.wait_ge(up_done, c * nm + m + 1)
                    dve.tensor_tensor(inner[0:r, m, :], gs[0:r, m % 2, :], ps_u[0:r, m % 2, :], ALU.mult)\
                        .then_inc(gated, 1)
                    if more and m == nm - 5:
                        stats(c + 1)
                    if more and m == nm - 2:
                        norm(c + 1)
                    if more and m == 0 and on_vector:
                        on_vector(dve, c + 1)
                if more:
                    low_part(c + 1)
                for i in range(CT):
                    dve.wait_ge(made, c * CT + i + 1)
                    tile = x_sb[:, bass.ds(c * CT + i, 1), :]
                    dve.tensor_tensor(tile, tile, ps_y[:, i % 2, 0:D].unsqueeze(1), ALU.add).then_inc(added, 1)

            stats(0)
            norm(0)
            low_part(0)
            if on_vector:
                on_vector(dve, 0)
            chunks(dve, body)

        @block.scalar
        def _(act):
            def copy_xt(c):
                act.wait_ge(turned, c + 1)
                wait(act, up_done, c * nm)
                act.activation(xt[:, :, :], ps_t[:, :, :], ACT.Copy).then_inc(xt_ready, 1)

            def body(c, more):
                for m in range(nm):
                    r = sizes[m]
                    if ns and more and m == nm - 4:
                        ns.on_scalar(act, c + 1)
                    n = decoding(c, m)
                    if n is not None:
                        decoder.halve(act, n)
                    act.wait_ge(gate_done, c * nm + m + 1)
                    wait(act, gated, c * nm + m - 1)
                    act.activation(gs[0:r, m % 2, :], ps_g[0:r, m % 2, :], func).then_inc(acted, 1)
                    if n is not None:
                        decoder.convert(act, n)
                if more:
                    copy_xt(c + 1)

            if ns:
                ns.on_scalar(act)
            copy_xt(0)
            chunks(act, body)

        @block.tensor
        def _(pe):
            def turn(c):
                pe.wait_ge(normed, c * CT + CT)
                wait(pe, low_ready, c)
                for k in range(KD):
                    for i in range(CT):
                        ins = pe.transpose(ps_t[:, k, i * P:(i + 1) * P], xn[:, i, k::KD], ident[:, :])
                ins.then_inc(turned, 1)

            def body(c, more):
                pe.wait_ge(low_ready, c + 1)
                for m in range(nm):
                    r = sizes[m]
                    cols = slice(starts[m], starts[m] + r)
                    wait(pe, decoder and decoder.low_done, await_decoded(c, first(m) if first else 0))
                    for w, ps, freed, done in ((w_gate, ps_g, acted, gate_done), (w_up, ps_u, gated, up_done)):
                        wait(pe, freed, c * nm + m - 1)
                        products = [(w[0], xt), (w[0], xt_low), (w[1], xt)] if split else [(w, xt)]
                        products = [(a[:, k, cols], b[:, k, :]) for k in range(KD) for a, b in products]
                        for n, (a, b) in enumerate(products):
                            ins = pe.matmul(ps[0:r, m % 2, :], a, b, start=n == 0, stop=n == len(products) - 1)
                        ins.then_inc(done, 1)
                if more:
                    turn(c + 1)
                wait(pe, decoder and decoder.multiplied, await_decoded(c, decoder.n if decoder else 0))
                pe.wait_ge(gated, c * nm + nm)
                for i in range(CT):
                    wait(pe, added, c * CT + i - 1)
                    for m in range(nm):
                        r = sizes[m]
                        ins = pe.matmul(ps_y[:, i % 2, 0:D], inner[0:r, m, i * P:(i + 1) * P], w_down(m),
                                        start=m == 0, stop=m == nm - 1)
                    ins.then_inc(made, 1)

            turn(0)
            chunks(pe, body)


PIECE = 512
TABLE = 0xC8643210 - (1 << 32)


class Decoder:

    def __init__(self, s, codes, scales, out, order):
        self.codes, self.scales, self.out, self.order = codes, scales, out, order
        self.n = len(order)
        self.code = [s.sbuf(f"code{z}", [P, PIECE], I32) for z in range(2)]
        self.scale = [s.sbuf(f"scale{z}", [P, PIECE]) for z in range(2)]
        self.half = [s.sbuf(f"half{z}", [P, PIECE]) for z in range(2)]
        self.table = s.sbuf("table", [P, 1], I32)
        self.shift = s.sbuf("shift", [P, 2, PIECE], I32)
        self.product = s.sbuf("product", [P, 2, PIECE])
        self.mag = s.sbuf("mag", [P, 2, PIECE], I32)
        self.magf = s.sbuf("magf", [P, 2, PIECE])
        self.sign = s.sbuf("sign", [P, 2, PIECE], I32)
        self.signed = [s.sbuf(f"signed{z}", [P, 2, PIECE], I32) for z in range(2)]
        self.loaded = [s.sem(f"loaded{z}") for z in range(2)]
        self.halved = s.sem("halved")
        self.read = s.sem("read")
        self.converted = s.sem("converted")
        self.multiplied = s.sem("multiplied")
        self.high_done = s.sem("high_done")
        self.low_done = s.sem("low_done")

    def place(self, n):
        w, part = self.order[n]
        return w, slice(part * PIECE, (part + 1) * PIECE)

    def is_pair(self, n):
        return isinstance(self.out[self.order[n][0]], tuple)

    def pairs_before(self, n):
        return sum(self.is_pair(i) for i in range(n))

    def load(self, sp, n):
        z, (w, cols) = n % 2, self.place(n)
        wait(sp, self.read, n - 1)
        sp.dma_start(self.code[z][:, :], self.codes[w][:, cols]).then_inc(self.loaded[z], 16)
        sp.dma_start(self.scale[z][:, :], self.scales[w][:, cols].unsqueeze(1).to_broadcast([8, 16, PIECE]))\
            .then_inc(self.loaded[z], 16)

    def set_table(self, dve):
        dve.memset(self.table[:, :], TABLE)
        dve.drain()

    def look_up(self, dve, n):
        z = n % 2
        code, half, both = self.code[z], self.half[z], [P, 2, PIECE]
        wait(dve, self.read, n)
        dve.wait_ge(self.loaded[z], 32 * (n // 2 + 1))
        dve.tensor_scalar(self.shift[:, 0, :], code[:, :], 7, 2, ALU.bitwise_and, ALU.logical_shift_left)
        dve.tensor_scalar(self.shift[:, 1, :], code[:, :], 2, 28, ALU.logical_shift_right, ALU.bitwise_and)
        dve.tensor_scalar(self.sign[:, 0, :], code[:, :], 8, 28, ALU.bitwise_and, ALU.logical_shift_left)
        dve.tensor_scalar(self.sign[:, 1, :], code[:, :], 128, 24, ALU.bitwise_and, ALU.logical_shift_left)
        dve.drain()
        dve.tensor_tensor(self.shift[:, :, :], self.table[:, :].unsqueeze(1).to_broadcast(both), self.shift[:, :, :],
                          ALU.logical_shift_right)
        dve.wait_ge(self.halved, n + 1)
        wait(dve, self.multiplied, n - 1)
        dve.tensor_tensor(self.signed[z][:, :, :], self.sign[:, :, :],
                          half[:, :].bitcast(I32).unsqueeze(1).to_broadcast(both), ALU.bitwise_xor)
        dve.drain()
        wait(dve, self.converted, n)
        dve.tensor_scalar(self.mag[:, :, :], self.shift[:, :, :], 15, None, ALU.bitwise_and).then_inc(self.read, 1)

    def halve(self, act, n):
        z = n % 2
        act.wait_ge(self.loaded[z], 32 * (n // 2 + 1))
        wait(act, self.read, n - 1)
        act.mul(self.half[z][:, :], self.scale[z][:, :], 0.5).then_inc(self.halved, 1)

    def convert(self, act, n):
        if n and self.is_pair(n - 1):
            w, cols = self.place(n - 1)
            act.wait_ge(self.multiplied, n)
            act.activation(self.out[w][0][:, :, cols], self.product[:, :, :], ACT.Copy).then_inc(self.high_done, 1)
        act.wait_ge(self.read, n + 1)
        wait(act, self.multiplied, n)
        act.activation(self.magf[:, :, :], self.mag[:, :, :], ACT.Copy).then_inc(self.converted, 1)

    def multiply(self, pool, n):
        z, (w, cols) = n % 2, self.place(n)
        if n and self.is_pair(n - 1):
            w1, cols1 = self.place(n - 1)
            done = self.pairs_before(n)
            pool.wait_ge(self.high_done, done)
            pool.tensor_tensor(self.out[w1][1][:, :, cols1], self.product[:, :, :],
                               self.out[w1][0][:, :, cols1].bitcast(F32), ALU.subtract).then_inc(self.low_done, 1)
            pool.wait_ge(self.low_done, done)
        pool.wait_ge(self.converted, n + 1)
        out = self.product[:, :, :] if self.is_pair(n) else self.out[w][:, :, cols]
        pool.tensor_tensor(out, self.magf[:, :, :], self.signed[z][:, :, :].bitcast(F32),
                           ALU.mult).then_inc(self.multiplied, 1)

NE = 64
TOP = 6
FE = 176
FEP = FE // 2
FPAD = 96
NTILE = (T * TOP - NE) // P + NE
NSLOT = NTILE * P
TOP_EPS = 1e-20


def route(nc, tag, ident, gate_w, xn_all, weights, chosen, slot, expert_dram, load_shared):
    with ExitStack() as ctx:
        s = Scope(nc, ctx, tag)
        gw = s.sbuf("gw", [P, KD, NE])
        xt = s.sbuf("xt", [P, 2, KD, P])
        logits = s.sbuf("logits", [P, NTT, NE])
        top = s.sbuf("top", [P, NTT, 8])
        row = s.sbuf("row", [P, NTT, 1])
        row2 = s.sbuf("row2", [P, NTT, 1])
        shifted = s.sbuf("shifted", [P, NTT, NE])
        exps = s.sbuf("exps", [P, NTT, NE])
        scores = s.sbuf("scores", [P, NTT, NE])
        idx = s.sbuf("idx", [P, NTT, 8], U32)
        idxf = s.sbuf("idxf", [P, NTT, 8], BF16)
        mask = [s.sbuf(f"mask{z}", [P, NTT, NE], BF16) for z in range(2)]
        mask_bf = s.sbuf("mask_bf", [P, NTT, NE], BF16)
        before = s.sbuf("before", [P, P], BF16)
        ones = s.sbuf("ones", [P, P], BF16)
        count = s.sbuf("count", [P, NE], I32)
        tiles_i = s.sbuf("tiles_i", [P, NE], I32)
        tiles = s.sbuf("tiles", [P, NE])
        incl = [s.sbuf(f"incl{z}", [P, NE]) for z in range(2)]
        start = s.sbuf("start", [P, NE])
        iota_e = s.sbuf("iota_e", [P, NE], BF16)
        iota_t = s.sbuf("iota_t", [P, 2])
        passed = s.sbuf("passed", [P, 2, NE])
        owner = s.sbuf("owner", [P, 2, 1])
        owner_i = s.sbuf("owner_i", [P, 2], I32)
        ps_t = s.psum("ps_t", [P, 2, S])
        ps_l = s.psum("ps_l", [P, 2, S])
        ps_pos = s.psum("ps_pos", [P, 2, NTT // 2, NE])
        ps_n = s.psum("ps_n", [P, S])
        gw_loaded = s.sem("gw_loaded")
        shared_loaded = s.sem("shared_loaded")
        filled = s.sem("filled")
        shaped = s.sem("shaped")
        turned = s.sem("turned")
        xt_ready = s.sem("xt_ready")
        logits_done = s.sem("logits_done")
        logits_copied = s.sem("logits_copied")
        shifted_done = s.sem("shifted_done")
        exps_done = s.sem("exps_done")
        mask_done = s.sem("mask_done")
        placed = s.sem("placed")
        owned = s.sem("owned")
        owner_stored = s.sem("owner_stored")
        block = ctx.enter_context(nc.Block())

        @block.sync
        def _(sp):
            sp.dma_start(gw[:, :, :], gate_w.rearrange("(p k) n -> p k n", k=KD)).then_inc(gw_loaded, 16)
            n = load_shared(sp, shared_loaded)
            sp.wait_ge(owned, 1)
            sp.dma_start(expert_dram.rearrange("(p j) -> p j", p=P), owner_i[:, :]).then_inc(owner_stored, 16)
            sp.wait_ge(owner_stored, 16)
            sp.wait_ge(shared_loaded, n)

        @block.gpsimd
        def _(pool):
            pool.memset(ones[:, :], 1.0).then_inc(filled, 1)
            pool.wait_ge(filled, 1)
            pool.affine_select(out=before[:, :], in_=ones[:, :], compare_op=ALU.is_gt, fill=0.0, base=0,
                               pattern=[[1, P]], channel_multiplier=-1).then_inc(shaped, 1)
            pool.iota(iota_e[:, :], pattern=[[1, NE]], base=0, channel_multiplier=0,
                      allow_small_or_imprecise_dtypes=True).then_inc(shaped, 1)
            pool.iota(iota_t[:, :], pattern=[[1, 2]], base=0, channel_multiplier=2,
                      allow_small_or_imprecise_dtypes=True).then_inc(shaped, 1)

        @block.scalar
        def _(act):
            for i in range(NTT):
                act.wait_ge(turned, i + 1)
                if i >= 2:
                    act.wait_ge(logits_done, i - 1)
                act.activation(xt[:, i % 2, :, :], ps_t[:, i % 2, 0:KD * P].rearrange("p (k t) -> p k t", k=KD),
                               ACT.Copy).then_inc(xt_ready, 1)
            act.wait_ge(shifted_done, 1)
            act.activation(exps[:, :, :], shifted[:, :, :], ACT.Exp).then_inc(exps_done, 1)

        @block.tensor
        def _(pe):
            pe.wait_ge(gw_loaded, 16)

            def turn(i):
                if i >= 2:
                    pe.wait_ge(xt_ready, i - 1)
                for k in range(KD):
                    ins = pe.transpose(ps_t[:, i % 2, k * P:(k + 1) * P], xn_all[:, i, k::KD], ident[:, :])
                ins.then_inc(turned, 1)

            turn(0)
            for i in range(NTT):
                if i + 1 < NTT:
                    turn(i + 1)
                pe.wait_ge(xt_ready, i + 1)
                if i >= 2:
                    pe.wait_ge(logits_copied, i - 1)
                for k in range(KD):
                    ins = pe.matmul(ps_l[:, i % 2, 0:NE], xt[:, i % 2, k, :], gw[:, k, :],
                                    start=k == 0, stop=k == KD - 1)
                ins.then_inc(logits_done, 1)
            pe.wait_ge(shaped, 3)
            pe.wait_ge(mask_done, 1)
            for i in range(NTT):
                out = ps_pos[:, i // (NTT // 2), i % (NTT // 2), :]
                for j in range(i):
                    pe.matmul(out, ones[:, :], mask_bf[:, j, :], start=j == 0, stop=False)
                pe.matmul(out, before[:, :], mask_bf[:, i, :], start=i == 0, stop=True)
            for j in range(NTT):
                ins = pe.matmul(ps_n[:, 0:NE], ones[:, :], mask_bf[:, j, :], start=j == 0, stop=j == NTT - 1)
            ins.then_inc(placed, 1)

        @block.vector
        def _(dve):
            for i in range(NTT):
                dve.wait_ge(logits_done, i + 1)
                dve.tensor_copy(logits[:, i, :], ps_l[:, i % 2, 0:NE]).then_inc(logits_copied, 1)
            dve.drain()
            full = [P, NTT, NE]
            dve.tensor_reduce(row[:, :, :], logits[:, :, :], AX_X, ALU.max)
            dve.drain()
            dve.tensor_tensor(shifted[:, :, :], logits[:, :, :], row[:, :, :].to_broadcast(full), ALU.subtract)\
                .then_inc(shifted_done, 1)
            dve.wait_ge(exps_done, 1)
            dve.tensor_reduce(row[:, :, :], exps[:, :, :], AX_X, ALU.add)
            dve.drain()
            dve.reciprocal(row2[:, :, :], row[:, :, :])
            dve.drain()
            dve.tensor_tensor(scores[:, :, :], exps[:, :, :], row2[:, :, :].to_broadcast(full), ALU.mult)
            dve.drain()
            for i in range(NTT):
                dve.max(top[:, i, :], scores[:, i, :])
            dve.drain()
            for i in range(NTT):
                dve.max_index(idx[:, i, :], top[:, i, :], scores[:, i, :])
            dve.tensor_reduce(row[:, :, :], top[:, :, 0:TOP], AX_X, ALU.add)
            dve.drain()
            dve.tensor_copy(idxf[:, :, :], idx[:, :, :])
            dve.tensor_scalar(row2[:, :, :], row[:, :, :], TOP_EPS, None, ALU.add)
            dve.drain()
            dve.reciprocal(row[:, :, :], row2[:, :, :])
            dve.wait_ge(shaped, 3)
            for k in range(TOP):
                dve.tensor_tensor(chosen[:, k, :, :], iota_e[:, :].unsqueeze(1).to_broadcast(full),
                                  idxf[:, :, k:k + 1].to_broadcast(full), ALU.is_equal)
            dve.drain()
            dve.tensor_tensor(weights[:, :, :], top[:, :, 0:TOP], row[:, :, :].to_broadcast([P, NTT, TOP]), ALU.mult)
            dve.tensor_tensor(mask[0][:, :, :], chosen[:, 0, :, :], chosen[:, 1, :, :], ALU.add)
            for k in range(2, TOP):
                dve.drain()
                out = mask[(k + 1) % 2] if k < TOP - 1 else mask_bf
                ins = dve.tensor_tensor(out[:, :, :], mask[k % 2][:, :, :], chosen[:, k, :, :], ALU.add)
            ins.then_inc(mask_done, 1)
            dve.wait_ge(placed, 1)
            dve.tensor_scalar(count[:, :], ps_n[:, 0:NE], float(P - 1), None, ALU.add)
            dve.drain()
            dve.tensor_scalar(tiles_i[:, :], count[:, :], P.bit_length() - 1, None, ALU.logical_shift_right)
            dve.drain()
            dve.tensor_copy(tiles[:, :], tiles_i[:, :])
            dve.drain()
            dve.tensor_copy(incl[0][:, :], tiles[:, :])
            z, d = 0, 1
            while d < NE:
                dve.drain()
                dve.tensor_copy(incl[1 - z][:, 0:d], incl[z][:, 0:d])
                dve.tensor_tensor(incl[1 - z][:, d:NE], incl[z][:, d:NE], incl[z][:, 0:NE - d], ALU.add)
                z, d = 1 - z, 2 * d
            dve.drain()
            last = incl[z]
            dve.tensor_tensor(incl[1 - z][:, :], last[:, :], tiles[:, :], ALU.subtract)
            dve.tensor_tensor(passed[:, :, :], last[:, :].unsqueeze(1).to_broadcast([P, 2, NE]),
                              iota_t[:, :].unsqueeze(2).to_broadcast([P, 2, NE]), ALU.is_le)
            dve.drain()
            dve.tensor_scalar(start[:, :], incl[1 - z][:, :], float(P), None, ALU.mult)
            dve.tensor_reduce(owner[:, :, :], passed[:, :, :], AX_X, ALU.add)
            dve.drain()
            dve.tensor_scalar(owner_i[:, :], owner[:, :, 0], float(NE - 1), None, ALU.min).then_inc(owned, 1)
            half = NTT // 2
            for b in range(2):
                dve.tensor_tensor(slot[:, b * half:(b + 1) * half, :], ps_pos[:, b, :, :],
                                  start[:, :].unsqueeze(1).to_broadcast([P, half, NE]), ALU.add)


class Scatter:

    def __init__(self, s, xn_all, chosen, slot, slots, sorted_dram):
        self.xn_all, self.chosen, self.slot, self.slots, self.dram = xn_all, chosen, slot, slots, sorted_dram
        self.picked = s.sbuf("picked", [P, TOP, CT, NE])
        self.slot_f = s.sbuf("slot_f", [P, TOP, CT, 1])
        self.slots_ready = s.sem("slots_ready")
        self.scattered = s.sem("scattered")

    def pick(self, dve, c):
        tiles = bass.ds(c * CT, CT)
        dve.tensor_tensor(self.picked[:, :, :, :], self.chosen[:, :, tiles, :],
                          self.slot[:, tiles, :].unsqueeze(1).to_broadcast([P, TOP, CT, NE]), ALU.mult)
        dve.drain()
        dve.tensor_reduce(self.slot_f[:, :, :, :], self.picked[:, :, :, :], AX_X, ALU.add)
        dve.drain()
        dve.tensor_copy(self.slots[:, :, tiles], self.slot_f[:, :, :, 0]).then_inc(self.slots_ready, 1)

    def send(self, pool):
        for i in range(NTT):
            if i % CT == 0:
                pool.wait_ge(self.slots_ready, i // CT + 1)
            for k in range(TOP):
                pool.indirect_dma_start(out=self.dram[:, :],
                                        out_offset=bass.IndirectOffsetOnAxis(ap=self.slots[:, k, i:i + 1], axis=0),
                                        in_=self.xn_all[:, i, :], in_offset=None).then_inc(self.scattered, 16)
        pool.wait_ge(self.scattered, 16 * TOP * NTT)


ZERO = 1024


class ZeroFill:

    def __init__(self, s, dram):
        self.zero = s.sbuf("zero", [P, ZERO])
        self.zero_set, self.zeroed = s.sem("zero_set"), s.sem("zeroed")
        self.flat = dram.rearrange("(p r) d -> p (r d)", p=P)

    def set(self, pool):
        pool.memset(self.zero[:, :], 0.0).then_inc(self.zero_set, 1)

    def store(self, sp):
        sp.wait_ge(self.zero_set, 1)
        size = self.flat.shape[1]
        starts = range(0, size, ZERO)
        for a in starts:
            n = min(ZERO, size - a)
            sp.dma_start(self.flat[:, a:a + n], self.zero[:, 0:n]).then_inc(self.zeroed, 16)
        sp.wait_ge(self.zeroed, 16 * len(starts))


def experts(nc, tag, ident, w1, w2, expert_dram, sorted_dram, out_dram):
    R = 6
    G = 3
    with ExitStack() as ctx:
        s = Scope(nc, ctx, tag)
        cells = [s.sbuf(f"cells{z}", [1, G], I32) for z in range(R // G)]
        x = [s.sbuf(f"x{z}", [P, D]) for z in range(R)]
        wgu = [s.sbuf(f"wgu{z}", [P, KD, 2 * FE]) for z in range(R)]
        wd = [s.sbuf(f"wd{z}", [FPAD, 2, D]) for z in range(R)]
        xt = s.sbuf("xt", [P, G, KD, P])
        gs = s.sbuf("gs", [P, FE])
        hid = s.sbuf("hid", [P, 2 * FPAD])
        ht = [s.sbuf(f"ht{z}", [FPAD, 2, P]) for z in range(2)]
        y = [s.sbuf(f"y{z}", [P, D]) for z in range(R)]
        ps_x = s.psum("ps_x", [P, S])
        ps_gu = s.psum("ps_gu", [P, G, S])
        ps_h = s.psum("ps_h", [P, S])
        ps_y = s.psum("ps_y", [P, G, S])
        pads_set = s.sem("pads_set")
        cells_loaded = [s.sem(f"cells_loaded{z}") for z in range(R // G)]
        x_loaded = [s.sem(f"x_loaded{z}") for z in range(R)]
        wgu_loaded = [s.sem(f"wgu_loaded{z}") for z in range(R)]
        wd_loaded = [s.sem(f"wd_loaded{z}") for z in range(R)]
        x_turned = s.sem("x_turned")
        xt_ready = s.sem("xt_ready")
        gu_done = s.sem("gu_done")
        acted = s.sem("acted")
        gated = s.sem("gated")
        h_turned = s.sem("h_turned")
        ht_ready = s.sem("ht_ready")
        y_done = s.sem("y_done")
        y_copied = s.sem("y_copied")
        y_stored = [s.sem(f"y_stored{z}") for z in range(R)]
        block = ctx.enter_context(nc.Block())

        class Tile:

            def __init__(self, t, c):
                self.t, self.c = t, c
                self.n = t * R + c
                self.slot, self.bank = c % R, c % G
                self.turn = t + c // R

            def plus(self, d):
                return Tile(self.t, self.c + d)

            def exists(self):
                return not isinstance(self.n, int) or 0 <= self.n < NTILE

        TURNS = NTILE // R

        def loop(eng, body):
            for u in range(-2, R):
                body(Tile(0, u))
            with eng.Fori(1, TURNS - 2) as t:
                for c in range(R):
                    body(Tile(t, c))
            for u in range((TURNS - 2) * R, NTILE + 1):
                body(Tile(0, u))

        @block.sync
        def _(sp):
            def load(u, first):
                z, next_group = u.slot, u.plus(1)
                last = u.n - R + 1 if isinstance(u.n, int) else sp.snap(u.n - R + 1)
                e = sp.value_load(cells[z // G][0:1, z % G:z % G + 1], min_val=0, max_val=NE - 1)
                if not first:
                    sp.wait_ge(gu_done, last)
                sp.dma_start(wgu[z][:, :, :], w1[bass.ds(e, 1)].rearrange("o (p k) f -> p (o k) f", k=KD))\
                    .then_inc(wgu_loaded[z], 16)
                sp.wait_ge(pads_set, z + 1) if first else sp.wait_ge(y_done, last)
                if z % G == G - 1 and next_group.exists():
                    sp.wait_ge(cells_loaded[next_group.slot // G], 16 * (next_group.turn + 1))
                sp.dma_start(wd[z][0:FEP, :, :], w2[bass.ds(e, 1)].rearrange("o (p k) d -> p (o k) d", k=2))\
                    .then_inc(wd_loaded[z], 16)

            def load_cells(u):
                sp.dma_start(cells[u.slot // G][:, :], expert_dram[bass.ds(u.n, G)].unsqueeze(0))\
                    .then_inc(cells_loaded[u.slot // G], 16)

            def step(u, first, more=True):
                load(u, first)
                if u.slot % G == G - 1 and more:
                    load_cells(u.plus(R - G + 1))

            for u in range(0, R, G):
                load_cells(Tile(0, u))
            sp.wait_ge(cells_loaded[0], 16)
            for u in range(R):
                step(Tile(0, u), True)
            with sp.Fori(1, TURNS - 1) as t:
                for c in range(R):
                    step(Tile(t, c), False)
            for u in range((TURNS - 1) * R, NTILE):
                step(Tile(0, u), False, u + R - G + 1 < NTILE)

        @block.tensor
        def _(pe):
            def turn_x(u):
                if not u.exists():
                    return
                wait(pe, xt_ready, u.n)
                pe.wait_ge(x_loaded[u.slot], 16 * (u.turn + 1))
                for k in range(KD):
                    ins = pe.transpose(ps_x[:, k * P:(k + 1) * P], x[u.slot][:, k::KD], ident[:, :])
                ins.then_inc(x_turned, 1)

            def gate_up(u):
                if not u.exists():
                    return
                pe.wait_ge(wgu_loaded[u.slot], 16 * (u.turn + 1))
                pe.wait_ge(xt_ready, u.n + 1)
                if u.plus(-G).exists():
                    pe.wait_ge(gated, u.n - G + 1)
                for k in range(KD):
                    ins = pe.matmul(ps_gu[:, u.bank, 0:2 * FE], xt[:, u.bank, k, :], wgu[u.slot][:, k, :],
                                    start=k == 0, stop=k == KD - 1)
                ins.then_inc(gu_done, 1)

            def turn_h(u):
                if not u.exists():
                    return
                pe.wait_ge(gated, u.n + 1)
                wait(pe, ht_ready, u.n)
                for k in range(2):
                    ins = pe.transpose(ps_h[0:FPAD, k * P:(k + 1) * P], hid[:, k::2], ident[:, :])
                ins.then_inc(h_turned, 1)

            def down(u):
                if not u.exists():
                    return
                pe.wait_ge(wd_loaded[u.slot], 16 * (u.turn + 1))
                pe.wait_ge(ht_ready, u.n + 1)
                if u.plus(-G).exists():
                    pe.wait_ge(y_copied, u.n - G + 1)
                for k in range(2):
                    ins = pe.matmul(ps_y[:, u.bank, 0:D], ht[u.c % 2][:, k, :], wd[u.slot][:, k, :],
                                    start=k == 0, stop=k == 1)
                ins.then_inc(y_done, 1)

            pe.wait_ge(pads_set, R + 1)

            def body(u):
                gate_up(u.plus(1))
                turn_h(u)
                turn_x(u.plus(2))
                down(u.plus(-1))

            loop(pe, body)

        @block.scalar
        def _(act):
            def copy_x(u):
                if not u.exists():
                    return
                act.wait_ge(x_turned, u.n + 1)
                if u.plus(-G).exists():
                    act.wait_ge(gu_done, u.n - G + 1)
                act.activation(xt[:, u.bank, :, :], ps_x[:, 0:KD * P].rearrange("p (k t) -> p k t", k=KD), ACT.Copy)\
                    .then_inc(xt_ready, 1)

            def gate(u):
                if not u.exists():
                    return
                act.wait_ge(gu_done, u.n + 1)
                wait(act, gated, u.n)
                act.activation(gs[:, :], ps_gu[:, u.bank, 0:FE], ACT.Silu).then_inc(acted, 1)

            def store(u):
                if not u.exists():
                    return
                act.wait_ge(y_copied, u.n + 1)
                act.dma_start(out_dram[bass.ds(u.n * P, P), :], y[u.slot][:, :]).then_inc(y_stored[u.slot], 16)

            def load_x(u):
                if u.exists():
                    act.dma_start(x[u.slot][:, :], sorted_dram[bass.ds(u.n * P, P), :]).then_inc(x_loaded[u.slot], 16)

            for u in range(R):
                load_x(Tile(0, u))

            def body(u):
                copy_x(u.plus(2))
                gate(u.plus(1))
                if u.plus(2).exists():
                    load_x(u.plus(2 + R))
                store(u.plus(-2))

            loop(act, body)
            store(Tile(0, NTILE - 1))
            for z in range(R):
                act.wait_ge(y_stored[z], 16 * ((NTILE - 1 - z) // R + 1))

        @block.vector
        def _(dve):
            def mul(u):
                if not u.exists():
                    return
                dve.wait_ge(acted, u.n + 1)
                wait(dve, h_turned, u.n)
                dve.tensor_tensor(hid[:, 0:FE], gs[:, :], ps_gu[:, u.bank, FE:2 * FE], ALU.mult).then_inc(gated, 1)

            def copy_h(u):
                if not u.exists():
                    return
                dve.wait_ge(h_turned, u.n + 1)
                if u.plus(-2).exists():
                    dve.wait_ge(y_done, u.n - 1)
                dve.tensor_copy(ht[u.c % 2][:, :, :], ps_h[0:FPAD, 0:2 * P].rearrange("p (k t) -> p k t", k=2))\
                    .then_inc(ht_ready, 1)

            def copy_y(u):
                if not u.exists():
                    return
                if u.plus(-R).exists():
                    dve.wait_ge(y_stored[u.slot], 16 * u.turn)
                dve.wait_ge(y_done, u.n + 1)
                dve.tensor_copy(y[u.slot][:, :], ps_y[:, u.bank, 0:D]).then_inc(y_copied, 1)

            def body(u):
                copy_h(u)
                mul(u.plus(1))
                copy_y(u.plus(-1))

            for z in range(R):
                dve.memset(wd[z][64:FPAD, :, :], 0.0).then_inc(pads_set, 1)
            dve.memset(hid[:, FE:2 * FPAD], 0.0).then_inc(pads_set, 1)
            dve.wait_ge(pads_set, R + 1)
            loop(dve, body)


def gather_add(nc, tag, x_sb, weights, slots, out_dram, y_dram):
    R = 6
    with ExitStack() as ctx:
        s = Scope(nc, ctx, tag)
        got = [s.sbuf(f"got{z}", [P, D]) for z in range(R)]
        gathered = [s.sem(f"gathered{z}") for z in range(R)]
        added = s.sem("added")
        stored = s.sem("stored")
        block = ctx.enter_context(nc.Block())

        @block.gpsimd
        def _(pool):
            for i in range(NTT):
                for k in range(TOP):
                    n = i * TOP + k
                    if n >= R:
                        pool.wait_ge(added, n - R + 1)
                    pool.indirect_dma_start(out=got[n % R][:, :], out_offset=None, in_=out_dram[:, :],
                                            in_offset=bass.IndirectOffsetOnAxis(ap=slots[:, k, i:i + 1], axis=0))\
                        .then_inc(gathered[n % R], 16)

        @block.vector
        def _(dve):
            for i in range(NTT):
                for k in range(TOP):
                    n = i * TOP + k
                    dve.wait_ge(gathered[n % R], 16 * (n // R + 1))
                    if n:
                        dve.wait_ge(added, n)
                    dve.scalar_tensor_tensor(out=x_sb[:, i, :], in0=got[n % R][:, :], scalar=weights[:, i, k:k + 1],
                                             in1=x_sb[:, i, :], op0=ALU.mult, op1=ALU.add).then_inc(added, 1)

        @block.sync
        def _(sp):
            for c in range(NCH):
                sp.wait_ge(added, (c + 1) * CT * TOP)
                sp.dma_start(y_dram[c].rearrange("(i p) d -> p i d", p=P), x_sb[:, c * CT:(c + 1) * CT, :])\
                    .then_inc(stored, 16)
            sp.wait_ge(stored, 16 * NCH)


def moe(nc, ctx, x_sb, xn_all, ident, gate_w, w1, w2, ws_gate_up, ws_down, sorted_dram, y_dram):
    FS = ws_down.shape[0]
    sizes = [P, P, FS - 2 * P]
    s = Scope(nc, ctx, "moe")
    weights = s.sbuf("weights", [P, NTT, TOP])
    slots = s.sbuf("slots", [P, TOP, NTT], U32)
    sgu = s.sbuf("sgu", [P, KD, 2 * FS])
    sd = s.sbuf("sd", [P, len(sizes), D])
    chosen = s.sbuf("chosen", [P, TOP, NTT, NE], BF16)
    slot = s.sbuf("slot", [P, NTT, NE])
    scatter = Scatter(s, xn_all, chosen, slot, slots, sorted_dram)
    expert_dram = nc.dram_tensor("tile_expert", [2 * P], I32, kind="Internal").ap()
    out_dram = nc.dram_tensor("y_sorted", [NSLOT, D], F32, kind="Internal").ap()

    def load_shared(sp, loaded):
        sp.dma_start(sgu[:, :, :], ws_gate_up.rearrange("(p k) f -> p k f", k=KD)).then_inc(loaded, 16)
        for m, r in enumerate(sizes):
            sp.dma_start(sd[0:r, m, :], ws_down[m * P:m * P + r, :]).then_inc(loaded, 16)
        return 16 * (1 + len(sizes))

    route(nc, "route", ident, gate_w, xn_all, weights, chosen, slot, expert_dram, load_shared)
    mlp(nc, "shared", x_sb, ident, sgu[:, :, 0:FS], sgu[:, :, FS:2 * FS], lambda m: sd[0:sizes[m], m, :],
        sizes, ACT.Silu,
        xn_all=xn_all, on_gpsimd=scatter.send, on_vector=scatter.pick)
    experts(nc, "experts", ident, w1, w2, expert_dram, sorted_dram, out_dram)
    gather_add(nc, "combine", x_sb, weights, slots, out_dram, y_dram)


MLP = 2048
BLOCK = 32
SCALE_1 = 0.5


def decoded_mlp(nc, x_sb, ident, wo, bo, att_dram, codes, scales, sorted_dram):
    with ExitStack() as ctx:
        s = Scope(nc, ctx, "mlp_w")
        w_gate, w_up = (tuple(s.sbuf(n + part, [P, KD, MLP], F32R) for part in ("_high", "_low"))
                        for n in ("gate", "up"))
        w_down = s.sbuf("down", [P, KD, MLP])
        order = [(w, n) for n in range(MLP // PIECE) for w in (0, 1)] + [(2, n) for n in range(MLP // PIECE)]
        decoder = Decoder(s, codes, scales, [w_gate, w_up, w_down], order)
        zeros = ZeroFill(s, sorted_dram)
        beside_projection = 4
        project_out(nc, "out0", x_sb, ident, wo, bo, att_dram, decoder, beside_projection)

        def on_sync(sp):
            for n in range(beside_projection, decoder.n):
                decoder.load(sp, n)
            zeros.store(sp)

        def on_gpsimd(pool):
            zeros.set(pool)
            for n in range(beside_projection, decoder.n):
                decoder.multiply(pool, n)

        mlp(nc, "mlp", x_sb, ident, w_gate, w_up, lambda m: w_down[:, m % 2, m // 2 * D:(m // 2 + 1) * D],
            [P] * (MLP // P), ACT.Gelu_apprx_tanh, on_sync=on_sync, on_gpsimd=on_gpsimd,
            decoder=decoder, n_decoded=beside_projection, first=lambda m: 2 * (m * P // PIECE + 1), split=True)


def program(nc, a, y):
    with ExitStack() as ctx:
        s = Scope(nc, ctx, "all")
        x_sb = s.sbuf("x", [P, NTT, D])
        ident = s.sbuf("ident", [P, P])
        ident_bf = s.sbuf("ident_bf", [P, P], BF16)
        mask_q = s.sbuf("mask_q", [P, P], BF16)
        q_dram = nc.dram_tensor("q_parts", [2, D, T], F32, kind="Internal").ap()
        k_dram = nc.dram_tensor("k_parts", [2, D, T], F32, kind="Internal").ap()
        att_dram = nc.dram_tensor("att", [T, D], F32, kind="Internal").ap()
        first_sem = nc.free_semaphores[0]
        sorted_dram = nc.dram_tensor("x_sorted", [NSLOT, D], F32, kind="Internal").ap()
        make_constants(nc, a["L0_attn_X"], x_sb, ident, ident_bf, mask_q)

        for layer, heads, pitch, causal, parts in ((0, 16, 32, True, PARTS_16), (1, 4, 66, False, PARTS_64)):
            w = {n: a[f"L{layer}_attn_{n}"] for n in ("Wq", "bq", "Wk", "bk", "Wv", "bv", "Wo", "bo")}
            affine = (a["L0_attn_ln_g"], a["L0_attn_ln_b"]) if layer == 0 else None
            v_dram = nc.dram_tensor(f"v{layer}", [T, heads * pitch], F32, kind="Internal").ap()
            scale = (D // heads) ** -0.5 if layer == 0 else SCALE_1
            project_qkv(nc, f"qkv{layer}", x_sb, ident, w, affine, q_dram, k_dram, v_dram, heads, pitch)
            attention(nc, f"att{layer}", ident, ident_bf, mask_q, q_dram, k_dram, v_dram, att_dram,
                      heads, pitch, causal, parts, scale)
            if layer == 1:
                xn_all = s.sbuf("xn_all", [P, NTT, D])
                project_out(nc, "out1", x_sb, ident, w["Wo"], w["bo"], att_dram, xn_all=xn_all)
            else:
                decoded_mlp(nc, x_sb, ident, w["Wo"], w["bo"], att_dram, a["codes"], a["scales"], sorted_dram)
                nc.all_engine_barrier(sems_to_clear=range(first_sem, nc.free_semaphores[0]))
        moe(nc, ctx, x_sb, xn_all, ident, a["L1_ffn_gate_w"], a["L1_ffn_w_gate_up"], a["L1_ffn_w_down"],
            a["L1_ffn_ws_gate_up"], a["L1_ffn_ws_down"], sorted_dram, y)


def by_parity(m):
    r = m.shape[0]
    return m.reshape(r, MLP // D, P, 2).transpose(0, 1, 3, 2).reshape(r, MLP)


def kernel(**inputs):
    import concourse.bacc as bacc
    from concourse.bass_utils import run_bass_kernel_spmd

    inp = {n: np.asarray(v) for n, v in inputs.items()}
    arrays = {}
    for n in ("L0_attn_X", "L0_attn_ln_g", "L0_attn_ln_b"):
        arrays[n] = inp[n]
    for layer in (0, 1):
        for n in ("Wq", "Wk", "Wv", "Wo", "bv", "bo"):
            arrays[f"L{layer}_attn_{n}"] = inp[f"L{layer}_attn_{n}"]
        for n in ("bq", "bk"):
            arrays[f"L{layer}_attn_{n}"] = inp[f"L{layer}_attn_{n}"].reshape(KD, P).T
    g, u, d = (inp[f"L0_ffn_{n}_W_packed"] for n in ("gate", "up", "down"))
    gs, us, ds = (inp[f"L0_ffn_{n}_scales"] for n in ("gate", "up", "down"))
    nt = MLP // D
    arrays["codes"] = np.stack([by_parity(g.T), by_parity(u.T),
                                d.T.reshape(nt, P, D).transpose(1, 0, 2).reshape(P, MLP)])
    arrays["scales"] = np.stack([by_parity(gs.T), by_parity(us.T),
                                 ds.T.reshape(nt, D // BLOCK, D).transpose(1, 0, 2).reshape(D // BLOCK, MLP)])
    arrays["L1_ffn_gate_w"] = inp["L1_ffn_gate_w"].T
    arrays["L1_ffn_w_gate_up"] = inp["L1_ffn_w_gate_up"].transpose(0, 2, 1)
    arrays["L1_ffn_w_down"] = inp["L1_ffn_w_down"].transpose(0, 2, 1)
    arrays["L1_ffn_ws_gate_up"] = inp["L1_ffn_ws_gate_up"].T
    arrays["L1_ffn_ws_down"] = inp["L1_ffn_ws_down"].T
    arrays = {n: np.ascontiguousarray(v) for n, v in arrays.items()}

    nc = bacc.Bacc("TRN2", target_bir_lowering=False, num_devices=1)
    aps = {n: nc.dram_tensor(n, v.shape, mybir.dt.from_np(v.dtype), kind="ExternalInput").ap()
           for n, v in arrays.items()}
    y = nc.dram_tensor("y", inp["L0_attn_X"].shape, F32, kind="ExternalOutput").ap()
    program(nc, aps, y)
    result = run_bass_kernel_spmd(nc, [arrays], core_ids=[0])
    return result.results[0]["y"]
```
